# Optimizing a Trainium2 kernel written in Bass

```python
import numpy as np
import jax
import jax.numpy as jnp

def _softmax(x, axis=-1):
    return jax.nn.softmax(x, axis=axis)

def _gelu(x):
    return jax.nn.gelu(x, approximate=True)

def _silu(x):
    return jax.nn.silu(x)

def _sigmoid(x):
    return jax.nn.sigmoid(x)

def _layernorm(x, axis=-1, eps=1e-05):
    m = jnp.mean(x, axis=axis, keepdims=True)
    v = jnp.var(x, axis=axis, keepdims=True)
    return (x - m) / jnp.sqrt(v + eps)

def _scatter_add(tgt, idx, src, axis=0):
    return tgt.at[idx].add(src)

def _segment_sum(src, seg, n):
    return jax.ops.segment_sum(src, seg, n)
kernel_name = 'mk_perceiver_d1_seqx_r4_46911b'

def setup_inputs(seed: int=0):
    np.random.seed(seed)
    _w = jnp.asarray

    def _rec_inputs():
        import jax
        import jax.numpy as jnp
        _rk = jax.random.key(seed)
        x = -1.394e-06 + 0.9999 * jax.random.normal(jax.random.fold_in(_rk, 1), (1, 256, 256), jnp.float32)
        _lenS = 256 - jax.random.randint(jax.random.fold_in(_rk, 7), (1,), 0, max(1, 256 // 4) + 1, jnp.int32)
        _lenS2 = 4096 - jax.random.randint(jax.random.fold_in(_rk, 8), (1,), 0, max(1, 4096 // 4) + 1, jnp.int32)
        _ctx_1024P = jax.random.normal(jax.random.fold_in(_rk, 11), (1, 16, 256), jnp.float32)
        _ctx_1024c = jax.random.dirichlet(jax.random.fold_in(_rk, 511), 0.3 * jnp.ones((16,), jnp.float32), (1, 4096))
        _ctx_1024t = jnp.einsum('bsk,bkd->bsd', _ctx_1024c, _ctx_1024P)
        _ctx_1024t = _ctx_1024t * jax.lax.rsqrt(jnp.mean(jnp.square(_ctx_1024t)) + 1e-12) * 0.953939
        ctx_1024 = -0.000292821 + 1.00034 * (_ctx_1024t + 0.3 * jax.random.normal(jax.random.fold_in(_rk, 611), (1, 4096, 256), jnp.float32))
        return (x, ctx_1024)
    x, ctx_1024 = _rec_inputs()

    def _L0_xattn_setup():
        import jax, jax.numpy as jnp
        import numpy as np
        NUM_HEADS = 16
        D_MODEL = 256
        LN_EPS = 1e-05
        key = jax.random.key(seed)
        ks = jax.random.split(key, 10)
        B, S, D = (2, 512, D_MODEL)
        s = 1.0 / np.sqrt(D)
        return {'encoded': jax.random.normal(ks[0], (B, S, D), jnp.float32), 'decoded': jax.random.normal(ks[1], (B, S, D), jnp.float32), 'Wq': jax.random.normal(ks[2], (D, D), jnp.float32) * s, 'bq': jax.random.normal(ks[3], (D,), jnp.float32) * s, 'Wk': jax.random.normal(ks[4], (D, D), jnp.float32) * s, 'bk': jax.random.normal(ks[5], (D,), jnp.float32) * s, 'Wv': jax.random.normal(ks[6], (D, D), jnp.float32) * s, 'bv': jax.random.normal(ks[7], (D,), jnp.float32) * s, 'gamma': jnp.ones((D,), jnp.float32), 'beta': jnp.zeros((D,), jnp.float32)}
    _L0_xattn_all = _L0_xattn_setup()
    _L0_xattn_in = {k: v for k, v in _L0_xattn_all.items() if k in ('Wq', 'bq', 'Wk', 'bk', 'Wv', 'bv', 'gamma', 'beta')}
    del _L0_xattn_all

    def _L0_attn_setup():
        import jax, jax.numpy as jnp
        import numpy as np
        DIM = 256
        HEADS = 16
        DIM_HEAD = DIM // HEADS
        LATENT = DIM // 4
        SCALE = DIM_HEAD ** (-0.5)
        key = jax.random.key(seed)
        ks = jax.random.split(key, 8)
        B, S = (2, 512)
        init = lambda k, shape, fan_in: jax.random.normal(k, shape, jnp.float32) * fan_in ** (-0.5)
        return {'x': jax.random.normal(ks[0], (B, S, DIM), jnp.float32), 'Wq': init(ks[1], (DIM, DIM), DIM), 'bq': jnp.zeros((DIM,), jnp.float32), 'Wl': init(ks[2], (DIM, LATENT), DIM), 'bl': jnp.zeros((LATENT,), jnp.float32), 'Wk': init(ks[3], (LATENT, DIM), LATENT), 'bk': jnp.zeros((DIM,), jnp.float32), 'Wv': init(ks[4], (LATENT, DIM), LATENT), 'bv': jnp.zeros((DIM,), jnp.float32), 'Wo': init(ks[5], (DIM, DIM), DIM), 'bo': jnp.zeros((DIM,), jnp.float32)}
    _L0_attn_all = _L0_attn_setup()
    _L0_attn_in = {k: v for k, v in _L0_attn_all.items() if k in ('Wq', 'bq', 'Wl', 'bl', 'Wk', 'bk', 'Wv', 'bv', 'Wo', 'bo')}
    del _L0_attn_all

    def _L0_ffn_setup():
        import jax, jax.numpy as jnp
        import numpy as np
        from jax.scipy.linalg import expm
        B, S, D, E, K, NROT = (2, 512, 256, 8, 2, 3)
        EPS = 1e-05

        def _gelu(x):
            return jax.nn.gelu(x, approximate=False)

        def _forward(x, ln_gamma, ln_beta, abel_w, abel_b, moe_gate_w, moe_gate_b, ew1, eb1, ew2, eb2, gens, gc_w, gc_b):
            residual = x
            mu = jnp.mean(x, axis=-1, keepdims=True)
            var = jnp.mean((x - mu) ** 2, axis=-1, keepdims=True)
            xn = (x - mu) * jax.lax.rsqrt(var + EPS) * ln_gamma + ln_beta
            abel_out = _gelu(xn @ abel_w + abel_b)
            logits = xn @ moe_gate_w + moe_gate_b
            topw, topi = jax.lax.top_k(logits, K)
            topw = jax.nn.softmax(topw, axis=-1)
            w_dense = jnp.sum(jax.nn.one_hot(topi, E, dtype=xn.dtype) * topw[..., None], axis=-2)
            h = _gelu(jnp.einsum('bsd,edh->ebsh', xn, ew1) + eb1[:, None, None, :])
            eo = jnp.einsum('ebsh,ehd->ebsd', h, ew2) + eb2[:, None, None, :]
            moe_out = jnp.einsum('ebsd,bse->bsd', eo, w_dense)
            for i in range(NROT):
                moe_out = moe_out @ expm(gens[i])
            combined = jnp.concatenate([abel_out, moe_out], axis=-1)
            gate = jax.nn.sigmoid(combined @ gc_w + gc_b)
            mixed = abel_out * (1.0 - gate) + moe_out * gate
            return residual + mixed
        key = jax.random.key(seed)
        ks = jax.random.split(key, 16)
        sc = 0.02
        x = jax.random.normal(ks[0], (B, S, D), jnp.float32)
        ln_gamma = 1.0 + sc * jax.random.normal(ks[1], (D,), jnp.float32)
        ln_beta = sc * jax.random.normal(ks[2], (D,), jnp.float32)
        abel_w = sc * jax.random.normal(ks[3], (D, D), jnp.float32)
        abel_b = sc * jax.random.normal(ks[4], (D,), jnp.float32)
        moe_gate_w = sc * jax.random.normal(ks[5], (D, E), jnp.float32)
        moe_gate_b = sc * jax.random.normal(ks[6], (E,), jnp.float32)
        ew1 = sc * jax.random.normal(ks[7], (E, D, 2 * D), jnp.float32)
        eb1 = sc * jax.random.normal(ks[8], (E, 2 * D), jnp.float32)
        ew2 = sc * jax.random.normal(ks[9], (E, 2 * D, D), jnp.float32)
        eb2 = sc * jax.random.normal(ks[10], (E, D), jnp.float32)
        g = sc * jax.random.normal(ks[11], (NROT, D, D), jnp.float32)
        gens = 0.5 * (g - jnp.swapaxes(g, -1, -2))
        gc_w = sc * jax.random.normal(ks[12], (2 * D, 1), jnp.float32)
        gc_b = sc * jax.random.normal(ks[13], (1,), jnp.float32)
        return dict(x=x, ln_gamma=ln_gamma, ln_beta=ln_beta, abel_w=abel_w, abel_b=abel_b, moe_gate_w=moe_gate_w, moe_gate_b=moe_gate_b, ew1=ew1, eb1=eb1, ew2=ew2, eb2=eb2, gens=gens, gc_w=gc_w, gc_b=gc_b)
    _L0_ffn_all = _L0_ffn_setup()
    _L0_ffn_in = {k: v for k, v in _L0_ffn_all.items() if k in ('ln_gamma', 'ln_beta', 'abel_w', 'abel_b', 'moe_gate_w', 'moe_gate_b', 'ew1', 'eb1', 'ew2', 'eb2', 'gens', 'gc_w', 'gc_b')}
    del _L0_ffn_all
    return {'x': x, 'ctx_1024': ctx_1024, 'L0_xattn_Wq': _L0_xattn_in['Wq'], 'L0_xattn_bq': _L0_xattn_in['bq'], 'L0_xattn_Wk': _L0_xattn_in['Wk'], 'L0_xattn_bk': _L0_xattn_in['bk'], 'L0_xattn_Wv': _L0_xattn_in['Wv'], 'L0_xattn_bv': _L0_xattn_in['bv'], 'L0_xattn_gamma': _L0_xattn_in['gamma'], 'L0_xattn_beta': _L0_xattn_in['beta'], 'L0_attn_Wq': _L0_attn_in['Wq'], 'L0_attn_bq': _L0_attn_in['bq'], 'L0_attn_Wl': _L0_attn_in['Wl'], 'L0_attn_bl': _L0_attn_in['bl'], 'L0_attn_Wk': _L0_attn_in['Wk'], 'L0_attn_bk': _L0_attn_in['bk'], 'L0_attn_Wv': _L0_attn_in['Wv'], 'L0_attn_bv': _L0_attn_in['bv'], 'L0_attn_Wo': _L0_attn_in['Wo'], 'L0_attn_bo': _L0_attn_in['bo'], 'L0_ffn_ln_gamma': _L0_ffn_in['ln_gamma'], 'L0_ffn_ln_beta': _L0_ffn_in['ln_beta'], 'L0_ffn_abel_w': _L0_ffn_in['abel_w'], 'L0_ffn_abel_b': _L0_ffn_in['abel_b'], 'L0_ffn_moe_gate_w': _L0_ffn_in['moe_gate_w'], 'L0_ffn_moe_gate_b': _L0_ffn_in['moe_gate_b'], 'L0_ffn_ew1': _L0_ffn_in['ew1'], 'L0_ffn_eb1': _L0_ffn_in['eb1'], 'L0_ffn_ew2': _L0_ffn_in['ew2'], 'L0_ffn_eb2': _L0_ffn_in['eb2'], 'L0_ffn_gens': _L0_ffn_in['gens'], 'L0_ffn_gc_w': _L0_ffn_in['gc_w'], 'L0_ffn_gc_b': _L0_ffn_in['gc_b']}

def reference(x, ctx_1024, L0_xattn_Wq, L0_xattn_bq, L0_xattn_Wk, L0_xattn_bk, L0_xattn_Wv, L0_xattn_bv, L0_xattn_gamma, L0_xattn_beta, L0_attn_Wq, L0_attn_bq, L0_attn_Wl, L0_attn_bl, L0_attn_Wk, L0_attn_bk, L0_attn_Wv, L0_attn_bv, L0_attn_Wo, L0_attn_bo, L0_ffn_ln_gamma, L0_ffn_ln_beta, L0_ffn_abel_w, L0_ffn_abel_b, L0_ffn_moe_gate_w, L0_ffn_moe_gate_b, L0_ffn_ew1, L0_ffn_eb1, L0_ffn_ew2, L0_ffn_eb2, L0_ffn_gens, L0_ffn_gc_w, L0_ffn_gc_b):
    import jax
    import jax.numpy as jnp

    def _L0_xattn_ref(encoded, decoded, Wq, bq, Wk, bk, Wv, bv, gamma, beta):
        import jax, jax.numpy as jnp
        import numpy as np
        NUM_HEADS = 16
        D_MODEL = 256
        LN_EPS = 1e-05
        B, Sq, D = decoded.shape
        H = NUM_HEADS
        dh = D // H
        q = decoded @ Wq.T + bq
        k = encoded @ Wk.T + bk
        v = encoded @ Wv.T + bv
        q = q.reshape(B, Sq, H, dh).transpose(0, 2, 1, 3)
        k = k.reshape(B, -1, H, dh).transpose(0, 2, 1, 3)
        v = v.reshape(B, -1, H, dh).transpose(0, 2, 1, 3)
        qk = jnp.einsum('bhqd,bhkd->bhqk', q, k)
        qk = jnp.where(jnp.isnan(qk), -jnp.inf, qk)
        attn = jax.nn.softmax(qk, axis=-1)
        attn = jnp.where(jnp.isnan(attn), 0.0, attn)
        v = jnp.where(jnp.isnan(v), 0.0, v)
        z = jnp.einsum('bhqk,bhkd->bhqd', attn, v)
        z = z.reshape(B, Sq, D)
        x = z + decoded
        mu = jnp.mean(x, axis=-1, keepdims=True)
        var = jnp.var(x, axis=-1, keepdims=True)
        return (x - mu) * jax.lax.rsqrt(var + LN_EPS) * gamma + beta

    def _L0_attn_ref(x, Wq, bq, Wl, bl, Wk, bk, Wv, bv, Wo, bo):
        import jax, jax.numpy as jnp
        import numpy as np
        DIM = 256
        HEADS = 16
        DIM_HEAD = DIM // HEADS
        LATENT = DIM // 4
        SCALE = DIM_HEAD ** (-0.5)
        B, S, D = x.shape
        H, Dh = (HEADS, DIM_HEAD)
        q = (x @ Wq + bq).reshape(B, S, H, Dh)
        latent = x @ Wl + bl
        k = (latent @ Wk + bk).reshape(B, S, H, Dh)
        v = (latent @ Wv + bv).reshape(B, S, H, Dh)
        scores = jnp.einsum('bihd,bjhd->bhij', q, k) * SCALE
        attn = jax.nn.softmax(scores, axis=-1)
        out = jnp.einsum('bhij,bjhd->bihd', attn, v).reshape(B, S, D)
        out = out @ Wo + bo
        return out

    def _L0_ffn_ref(x, ln_gamma, ln_beta, abel_w, abel_b, moe_gate_w, moe_gate_b, ew1, eb1, ew2, eb2, gens, gc_w, gc_b):
        import jax, jax.numpy as jnp
        import numpy as np
        from jax.scipy.linalg import expm
        B, S, D, E, K, NROT = (2, 512, 256, 8, 2, 3)
        EPS = 1e-05

        def _gelu(x):
            return jax.nn.gelu(x, approximate=False)

        def _forward(x, ln_gamma, ln_beta, abel_w, abel_b, moe_gate_w, moe_gate_b, ew1, eb1, ew2, eb2, gens, gc_w, gc_b):
            residual = x
            mu = jnp.mean(x, axis=-1, keepdims=True)
            var = jnp.mean((x - mu) ** 2, axis=-1, keepdims=True)
            xn = (x - mu) * jax.lax.rsqrt(var + EPS) * ln_gamma + ln_beta
            abel_out = _gelu(xn @ abel_w + abel_b)
            logits = xn @ moe_gate_w + moe_gate_b
            topw, topi = jax.lax.top_k(logits, K)
            topw = jax.nn.softmax(topw, axis=-1)
            w_dense = jnp.sum(jax.nn.one_hot(topi, E, dtype=xn.dtype) * topw[..., None], axis=-2)
            h = _gelu(jnp.einsum('bsd,edh->ebsh', xn, ew1) + eb1[:, None, None, :])
            eo = jnp.einsum('ebsh,ehd->ebsd', h, ew2) + eb2[:, None, None, :]
            moe_out = jnp.einsum('ebsd,bse->bsd', eo, w_dense)
            for i in range(NROT):
                moe_out = moe_out @ expm(gens[i])
            combined = jnp.concatenate([abel_out, moe_out], axis=-1)
            gate = jax.nn.sigmoid(combined @ gc_w + gc_b)
            mixed = abel_out * (1.0 - gate) + moe_out * gate
            return residual + mixed
        return _forward(x, ln_gamma, ln_beta, abel_w, abel_b, moe_gate_w, moe_gate_b, ew1, eb1, ew2, eb2, gens, gc_w, gc_b)
    x = x + _L0_xattn_ref(ctx_1024, _layernorm(x, axis=-1), L0_xattn_Wq, L0_xattn_bq, L0_xattn_Wk, L0_xattn_bk, L0_xattn_Wv, L0_xattn_bv, L0_xattn_gamma, L0_xattn_beta)
    x = x + _L0_attn_ref(_layernorm(x, axis=-1), L0_attn_Wq, L0_attn_bq, L0_attn_Wl, L0_attn_bl, L0_attn_Wk, L0_attn_bk, L0_attn_Wv, L0_attn_bv, L0_attn_Wo, L0_attn_bo)
    x = x + _L0_ffn_ref(_layernorm(x, axis=-1), L0_ffn_ln_gamma, L0_ffn_ln_beta, L0_ffn_abel_w, L0_ffn_abel_b, L0_ffn_moe_gate_w, L0_ffn_moe_gate_b, L0_ffn_ew1, L0_ffn_eb1, L0_ffn_ew2, L0_ffn_eb2, L0_ffn_gens, L0_ffn_gc_w, L0_ffn_gc_b)
    return x

_drawn_inputs = setup_inputs


def setup_inputs(seed=0):
    import zlib

    import numpy as np

    out = dict(_drawn_inputs(seed))
    spreads = {'L0_xattn_gamma': (1.0, 0.2),
     'L0_xattn_beta': (0.0, 0.1),
     'L0_attn_bq': (0.0, 0.8),
     'L0_attn_bl': (0.0, 0.1),
     'L0_attn_bk': (0.0, 2.0),
     'L0_attn_bv': (0.0, 0.1),
     'L0_attn_bo': (0.0, 0.1)}
    factors = {'L0_xattn_bk': 64.0,
     'L0_ffn_ln_gamma': 8.0,
     'L0_ffn_ln_beta': 8.0,
     'L0_ffn_abel_b': 46.622,
     'L0_ffn_moe_gate_w': 6.297,
     'L0_ffn_moe_gate_b': 8.0,
     'L0_ffn_ew1': 5.961,
     'L0_ffn_eb1': 8.0,
     'L0_ffn_ew2': 5.784,
     'L0_ffn_eb2': 60.719,
     'L0_ffn_gens': 8.0,
     'L0_ffn_gc_w': 8.0}
    for name, (base, spread) in spreads.items():
        noise = np.random.default_rng([zlib.crc32(name.encode()), seed]).standard_normal(out[name].shape)
        drawn = base * np.exp(spread * noise) if base else spread * noise
        out[name] = jnp.asarray(drawn.astype(out[name].dtype))
    for name, factor in factors.items():
        out[name] = (out[name] * factor).astype(out[name].dtype)
    return out
```

```python
import concourse.bass as bass
from concourse import mybir
from contextlib import ExitStack

FP32 = mybir.dt.float32
BF16 = mybir.dt.bfloat16
ALU = mybir.AluOpType
ACT = mybir.ActivationFunctionType
AX = mybir.AxisListType

P = 128
D = 256
NT = 256
NCTX = 4096
H = 16
DH = D // H
DT = D // P
TT = NT // P
EPS = 1e-5

KPART = (0, 1, 2, 0, 1, 0)
QPART = (0, 0, 0, 1, 1, 2)
NB = len(KPART)
ROWS = NB * DH
MROWS = 3

CHUNK = 512
SUPER = 2 * CHUNK
NSUPER = NCTX // SUPER
GROUP = 4
NG = H // GROUP
KT = NCTX // P
UN = 8
NIT = KT // UN
LAT = D // 4
E = 8
HID = 2 * D
HT = HID // P
QTILE = 5 * KT // 8
SLOTS = 4
NROT = 3
ROT = NROT * DT * D
SQUARINGS = 6
T1, T2, T3 = 4.980119205559973e-3, 1.992047682223989e-2, 7.665265321119147e-2
T4, T5, T6 = 8.765009801785554e-1, 1.225521150112075e-1, 2.974307204847627
VW = 32


def bcast(ap, n=P):
    return bass.AP(ap.tensor, ap.offset, [[0, n]] + [list(x) for x in ap.ap])


def spread(ap, n):
    return bass.AP(ap.tensor, ap.offset, [list(x) for x in ap.ap] + [[0, n]])


class Chain:

    def __init__(self, eng, sem):
        self.eng, self.sem, self.n = eng, sem, 0

    def step(self, ins):
        self.n += 1
        ins.then_inc(self.sem, 1)
        self.eng.wait_ge(self.sem, self.n)


def build(nc, x, ctx_in, xWq, xbq, xWk, xbk, xWv, xbv, xgamma, xbeta,
          aWq, abq, aWl, abl, aWk, abk, aWv, abv, aWo, abo,
          lng, lnb, abw, abb, gw, gb, ew1, eb1, ew2, eb2, gens, gcw, gcb, out, stop=None):
    ctx = ExitStack()
    proj = ExitStack()
    with ctx:
        ctx.enter_context(nc.allow_non_contiguous_dma("biases laid along partitions"))

        def sem(name):
            return ctx.enter_context(nc.semaphore(name))

        def sems(name, n):
            return [sem(f"{name}{i}") for i in range(n)]

        def sb(name, shape, dt=FP32, where=ctx):
            return where.enter_context(nc.sbuf_tensor(name, shape, dt))

        x_sb = sb("x_sb", [P, TT, D])
        dec = sb("dec", [P, TT, D])
        identf = sb("identf", [P, P])
        identb = sb("identb", [P, P], BF16)
        stats = sb("stats", [P, TT, 6])
        mv = sb("mv", [P, TT, 2])
        vare = sb("vare", [P, TT])
        mhalf = sb("mhalf", [P, TT])
        rstd = sb("rstd", [P, TT])
        bq_c = sb("bq_c", [P, DT])
        bk_c = sb("bk_c", [P, DT])
        hmask = sb("hmask", [P, P // DH])
        tri = sb("tri", [P, E, E])
        abq_c = sb("abq_c", [P, DT])
        abk_c = sb("abk_c", [P, DT])
        abl_c = sb("abl_c", [LAT, 1])
        gcb_b = sb("gcb_b", [P, 1])
        zero = sb("zero", [P, NT], BF16)
        mx0 = sb("mx0", [P, GROUP, TT, NCTX // 512])
        mxs = sb("mxs", [P, TT, NCTX // 512])
        negm = sb("negm", [P, GROUP, TT])
        mrem = sb("mrem", [P, 2, GROUP * TT])
        mp = sb("mp", [P, GROUP * TT, MROWS], BF16)
        xattn = ExitStack()
        kst = sb("kst", [P, H, NCTX], BF16, xattn)
        with ExitStack() as early:
            wn = sb("wn", [P, 3, DT, D], FP32, early)
            wqT = sb("wqT", [P, DT, D], FP32, early)
        qst = sb("qst", [P, H, NT], BF16, xattn)
        with ExitStack() as early:
            sb("values_before", [P, QTILE, D], FP32, early)
            qp = sb("qp", [P, DT, NB, NT], BF16, early)
            q1 = sb("q1", [P, DT, NT], FP32, early)
            onesb = sb("onesb", [P, NT], BF16, early)
            xT = sb("xT", [P, DT, NT], FP32, early)
        val = sb("val", [P, KT, D], FP32, xattn)
        kp = sb("kp", [P, DT, NB, SUPER], BF16, proj)
        cs = sb("cs", [P, 2, CHUNK // P, D], FP32, proj)
        cT = sb("cT", [P, 2, DT, CHUNK], FP32, proj)
        wT = sb("wT", [P, 2, DT, D], FP32, proj)
        r1 = sb("r1", [P, DT, CHUNK], FP32, proj)
        proj.close()
        attn = ExitStack()
        zq = sb("zq", [P, TT, D], FP32, attn)
        z = sb("z", [P, TT, D], FP32, attn)
        bv_b = sb("bv_b", [P, D], FP32, attn)
        gam_b = sb("gam_b", [P, D], FP32, attn)
        bet_b = sb("bet_b", [P, D], FP32, attn)
        pr = sb("pr", [P, 2, GROUP * NT], FP32, attn)
        vr = sb("vr", [P, 2, GROUP, VW], FP32, attn)
        zt = sb("zt", [P, NT], FP32, attn)
        rden = sb("rden", [P, TT, GROUP], FP32, attn)
        ln_t = sb("ln_t", [P, TT, D], FP32, attn)
        aWq_s = sb("aWq_s", [P, DT, D], FP32, attn)
        aWl_s = sb("aWl_s", [P, DT, LAT], FP32, attn)
        aWk_s = sb("aWk_s", [LAT, D], FP32, attn)
        aWv_s = sb("aWv_s", [LAT, D], FP32, attn)
        woP = sb("woP", [P, NG, D], FP32, attn)
        abv_b = sb("abv_b", [P, D], FP32, attn)
        abo_b = sb("abo_b", [P, D], FP32, attn)
        lng_b = sb("lng_b", [P, D], FP32, attn)
        lnb_b = sb("lnb_b", [P, D], FP32, attn)
        abb_b = sb("abb_b", [P, D], FP32, attn)
        gb_b = sb("gb_b", [P, E], FP32, attn)
        gcw_b = sb("gcw_b", [P, 2, D], FP32, attn)
        abw_s = sb("abw_s", [P, DT, D], FP32, attn)
        gw_s = sb("gw_s", [P, DT, E], FP32, attn)
        eb1_n = sb("eb1_n", [E * HT, P], FP32, attn)
        eb2_s = sb("eb2_s", [E, D], FP32, attn)
        rA = sb("rA", [P, NROT, DT, D], FP32, attn)
        attn.close()
        xattn.close()
        late = ExitStack()
        ew1r = sb("ew1r", [P, SLOTS, DT, HID], FP32, late)
        ew2r = sb("ew2r", [P, SLOTS, HT, D], FP32, late)
        n2 = sb("n2", [P, TT, D], FP32, late)
        xT2 = sb("xT2", [P, DT, NT], FP32, late)
        qf = sb("qf", [P, DT, NT], FP32, late)
        qm = sb("qm", [P, H, NT], FP32, late)
        latT = sb("latT", [LAT, NT], FP32, late)
        kT = sb("kT", [P, DT, NT], FP32, late)
        vp = sb("vp", [P, TT, H, VW], FP32, late)
        nm = sb("nm", [P, 2 * H], FP32, late)
        rs = sb("rs", [P, 2 * H], FP32, late)
        rr = sb("rr", [P, 2 * H], FP32, late)
        pa = sb("pa", [P, 2, 2, NT], FP32, late)
        pT = sb("pT", [P, TT, H, NT], FP32, late)
        zT = sb("zT", [P, NG, NT], FP32, late)
        rT = sb("rT", [P, NROT, DT, D], FP32, late)
        rA2 = sb("rA2", [P, NROT, DT, D], FP32, late)
        rU = sb("rU", [P, NROT, DT, D], FP32, late)
        rY = sb("rY", [P, NROT, DT, D], FP32, late)
        rL = sb("rL", [P, NROT, DT, D], FP32, late)
        xp = sb("xp", [P, TT, D], FP32, late)
        xg = sb("xg", [P, TT, D], FP32, late)
        xgT = sb("xgT", [P, DT, NT], FP32, late)
        abel = sb("abel", [P, TT, D], FP32, late)
        abin = sb("abin", [P, TT, D], FP32, late)
        lg = sb("lg", [P, TT, E], FP32, late)
        lm = sb("lm", [P, TT], FP32, late)
        ex = sb("ex", [P, TT, E], FP32, late)
        cgt = sb("cgt", [P, TT, E, E], FP32, late)
        ceq = sb("ceq", [P, TT, E, E], FP32, late)
        rank = sb("rank", [P, TT, E], FP32, late)
        wsum = sb("wsum", [P, TT], FP32, late)
        wd = sb("wd", [P, TT, E], FP32, late)
        wdT = sb("wdT", [E, NT], FP32, late)
        eb1_c = sb("eb1_c", [P, E * HT], FP32, late)
        hT = sb("hT", [P, 2, HT, NT], FP32, late)
        moe = sb("moe", [P, TT, D], FP32, late)
        moeT = sb("moeT", [P, DT, NT], FP32, late)
        moe2 = sb("moe2", [P, TT, D], FP32, late)
        junk = sb("junk", [P, D], FP32, late)
        gs = sb("gs", [P, 5, TT], FP32, late)
        late.close()

        psum = ctx.enter_context(nc.psum_tensor("psum", [P, 8, 512], FP32))
        ps_s = [psum[:, 0:2, :], psum[:, 2:4, :]]
        ps_pv = psum[:, 4, 0:NT]
        MB = (5, 6, 7)

        s_c = sem("s_c")
        s_in = sem("s_in")
        s_w = sem("s_w")
        s_b = sem("s_b")
        s_ob = sem("s_ob")
        s_par = sem("s_par")
        s_ones = sem("s_ones")
        s_ctx = sems("s_ctx", 2)
        s_wt = sem("s_wt")
        s_wtc = sem("s_wtc")
        s_lnv = sem("s_lnv")
        s_lnr = sem("s_lnr")
        s_ln = sem("s_ln")
        s_xt = sem("s_xt")
        s_xtc = sem("s_xtc")
        s_kb = sems("s_kb", 2)
        s_q = sem("s_q")
        s_q1 = sem("s_q1")
        s_qr = sem("s_qr")
        s_q2 = sem("s_q2")
        s_qp = sem("s_qp")
        s_qst = sem("s_qst")
        s_tr = sems("s_tr", 2)
        s_ta = sems("s_ta", 2)
        s_tv = sems("s_tv", 2)
        s_kmm = sems("s_kmm", 2)
        s_k1 = sems("s_k1", 2)
        s_r1 = sems("s_r1", 2)
        s_k2 = sems("s_k2", 2)
        s_kd = sems("s_kd", 2)
        s_vmm = sems("s_vmm", 2)
        s_v = sem("s_v")
        s_rs = sems("s_rs", 2)
        s_mmm = sems("s_mmm", 3)
        s_mx = sems("s_mx", 3)
        s_mxh = sem("s_mxh")
        s_mp = sem("s_mp")
        s_mr = sem("s_mr")
        s_mq = sem("s_mq")
        s_s = sems("s_s", 2)
        s_p = sems("s_p", 2)
        s_pv = sems("s_pv", 2)
        s_vr = sems("s_vr", 2)
        s_zt = sem("s_zt")
        s_zp = sem("s_zp")
        s_z = sem("s_z")
        s_prm = sem("s_prm")
        s_hm = sem("s_hm")
        s_woz = sem("s_woz")
        s_ew1 = sems("s_ew1", SLOTS)
        s_ew2 = sems("s_ew2", SLOTS)
        s_x2 = sem("s_x2")
        s_t2 = sem("s_t2")
        s_t2c = sem("s_t2c")
        s_aq = sem("s_aq")
        s_al = sem("s_al")
        s_alc = sem("s_alc")
        s_ak = sem("s_ak")
        s_akc = sem("s_akc")
        s_av = sem("s_av")
        s_avc = sem("s_avc")
        s_qf = sem("s_qf")
        s_qm = sem("s_qm")
        s_as = sem("s_as")
        s_anm = sem("s_anm")
        s_ae = sem("s_ae")
        s_ar = sem("s_ar")
        s_an = sem("s_an")
        s_at = sem("s_at")
        s_atA = sem("s_atA")
        s_atV = sem("s_atV")
        s_az = sem("s_az")
        s_azc = sem("s_azc")
        s_ao = sem("s_ao")
        s_rA = sem("s_rA")
        s_rt = sem("s_rt")
        s_rtc = sem("s_rtc")
        s_rm = sem("s_rm")
        s_rv = sem("s_rv")
        s_t3 = sem("s_t3")
        s_t3c = sem("s_t3c")
        s_ab = sem("s_ab")
        s_abi = sem("s_abi")
        s_lg = sem("s_lg")
        s_lm = sem("s_lm")
        s_abel = sem("s_abel")
        s_ex = sem("s_ex")
        s_wd = sem("s_wd")
        s_wt8 = sem("s_wt8")
        s_wt8c = sem("s_wt8c")
        s_b2 = sem("s_b2")
        s_acc = sem("s_acc")
        s_e1t = sem("s_e1t")
        s_e1c = sem("s_e1c")
        s_h = sems("s_h", 4)
        s_hc = sems("s_hc", 4)
        s_eo = sems("s_eo", 4)
        s_ea = sems("s_ea", 4)
        s_mt = sem("s_mt")
        s_mtc = sem("s_mtc")
        s_rot = sem("s_rot")
        s_gz = sem("s_gz")
        s_ge = sem("s_ge")
        s_zz = sem("s_zz")
        s_dve = sem("s_dve")
        s_out = sem("s_out")
        s_fin = sem("s_fin")

        def att_copy(copy, n, eng, wait, done):
            eng.wait_ge(wait, n + 1)
            h, t = 2 * (n // 2), n % 2
            to = pT[:, :, h:h + 2, t * P:(t + 1) * P].rearrange("p k j q -> p j k q")
            fro = psum[:, 2 + n % 2, :].rearrange("p (j k q) -> p j k q", j=2, k=TT)
            args = (ACT.Copy,) if done is s_atA else ()
            for j in range(2):
                copy(to[:, j], fro[:, j], *args).then_inc(done, 1)

        def free_at_first(eng, *counts):
            for c in counts:
                eng.sem_inc(c, 1)

        block = ctx.enter_context(nc.Block())

        ctx_v = ctx_in[0].rearrange("(n t p) d -> n p t d", t=CHUNK // P, p=P)

        ew1_v = ew1.rearrange("e (t p) h -> e p t h", p=P)
        ew2_v = ew2.rearrange("e (t p) d -> e p t d", p=P)

        @block.sync
        def _(sp):
            for i, w in ((1, xWk), (2, xWv)):
                sp.dma_start(wn[:, i], w.rearrange("(t p) i -> p t i", p=P)).then_inc(s_w, 16)
            for s in range(2):
                sp.dma_start(cs[:, s], ctx_v[s]).then_inc(s_ctx[s], 16)

            def restack(c, o):
                sp.wait_ge(s_kd[o], 4 * (c + 1))
                sp.wait_ge(s_kb[o], 4 * (c + 1))
                for j in range(P // DH):
                    h = o * (P // DH) + j
                    sp.dma_start(kst[0:ROWS, h, bass.ts(c, SUPER)],
                                 kp[DH * j:DH * (j + 1), o, :, :]).then_inc(s_rs[o], 16)

            def next_chunks(c):
                for s in range(2):
                    sp.wait_ge(s_tr[s], c + 1)
                    sp.dma_start(cs[:, s], ctx_v[bass.ds(2 * c + 2 + s, 1)][0]).then_inc(s_ctx[s], 16)

            sp.wait_ge(s_qp, 6)
            for h in range(H):
                o, j = divmod(h, P // DH)
                sp.dma_start(qst[0:ROWS, h, :], qp[DH * j:DH * (j + 1), o, :, :]).then_inc(s_qst, 16)
                if h == 1:
                    next_chunks(0)
            for o in range(DT):
                restack(0, o)
            with sp.Fori(1, NSUPER - 1) as c:
                next_chunks(c)
                for o in range(DT):
                    restack(c, o)
            for o in range(DT):
                restack(NSUPER - 1, o)
            sp.wait_ge(s_rs[0], 16 * NSUPER * (P // DH))
            sp.wait_ge(s_rs[1], 16 * NSUPER * (P // DH))
            sp.wait_ge(s_woz, 1)
            prm = [(rA[:, i], gens[i].rearrange("(t p) d -> p t d", p=P)) for i in range(NROT)]
            prm += [(aWq_s[:, :, :], aWq.rearrange("(t p) d -> p t d", p=P)),
                    (aWl_s[:, :, :], aWl.rearrange("(t p) d -> p t d", p=P)),
                    (aWk_s[:, :], aWk), (aWv_s[:, :], aWv),
                    (abw_s[:, :, :], abw.rearrange("(t p) d -> p t d", p=P)),
                    (gw_s[:, :, :], gw.rearrange("(t p) d -> p t d", p=P)),
                    (eb1_n[:, :], eb1.rearrange("e (t p) -> (e t) p", p=P)), (eb2_s[:, :], eb2),
                    (abv_b[:, :], bcast(abv)), (abo_b[:, :], bcast(abo)), (lng_b[:, :], bcast(lng)),
                    (lnb_b[:, :], bcast(lnb)), (abb_b[:, :], bcast(abb)), (gb_b[:, :], bcast(gb)),
                    (gcw_b[:, :, :], bcast(gcw.rearrange("(a d) one -> a (d one)", a=2)))]
            wo_v = aWo.rearrange("(g j d) n -> j d g n", j=GROUP, d=DH)
            prm += [(woP[VW * j:VW * j + DH, :, :], wo_v[j]) for j in range(GROUP)]
            assert len(prm) == NPRM
            for to, fro in prm:
                sp.dma_start(to, fro).then_inc(s_prm, 16)

            def expert(e, s):
                sp.dma_start(ew1r[:, s], ew1_v[bass.ds(e, 1)][0]).then_inc(s_ew1[s], 16)
                sp.dma_start(ew2r[:, s], ew2_v[bass.ds(e, 1)][0]).then_inc(s_ew2[s], 16)

            for g in range(NG):
                sp.wait_ge(s_z, 1 + ZSTEPS * (g + 1))
                for h in range(GROUP * g, GROUP * (g + 1)):
                    for t in range(TT):
                        row = DH * h + t * (P // DH)
                        sp.dma_start(z[row % P:row % P + P // DH, row // P, :],
                                     zq[:, t, h * DH:(h + 1) * DH]).then_inc(s_zz, 16)
            sp.wait_ge(s_pv[1], 1 + NG * NIT * (UN // 2))
            for s in range(SLOTS):
                expert(s, s)
            for r in range(1, E // SLOTS):
                for s in range(SLOTS):
                    sp.wait_ge(s_eo[s], 1 + r)
                    expert(r * SLOTS + s, s)
            sp.wait_ge(s_out, TT)
            sp.dma_start(out[0].rearrange("(t p) d -> p t d", p=P), moe2[:, :, :]).then_inc(s_fin, 16)
            sp.wait_ge(s_fin, 16)

        @block.gpsimd
        def _(pool):
            for m in (identf, identb):
                pool.memset(m[:, :], 0.0).then_inc(s_c, 1)
            pool.wait_ge(s_c, 2)
            for m in (identf, identb):
                pool.affine_select(out=m[:, :], in_=m[:, :], compare_op=ALU.not_equal, fill=1.0, base=0,
                                   pattern=[[-1, P]], channel_multiplier=1).then_inc(s_c, 1)
            pool.memset(mhalf[:, :], -0.5).then_inc(s_c, 1)
            pool.wait_ge(s_c, 5)
            pool.memset(hmask[:, :], DH ** -0.5).then_inc(s_hm, 1)
            pool.memset(tri[:, :, :], 1.0).then_inc(s_hm, 1)
            pool.wait_ge(s_hm, 2)
            pool.affine_select(out=hmask[:, :], in_=hmask[:, :], compare_op=ALU.is_ge, fill=0.0, base=0,
                               pattern=[[-DH, P // DH]], channel_multiplier=1).then_inc(s_hm, 1)
            pool.affine_select(out=tri[:, :, :], in_=tri[:, :, :], compare_op=ALU.is_gt, fill=0.0, base=0,
                               pattern=[[1, E], [-1, E]], channel_multiplier=0).then_inc(s_hm, 1)
            pool.wait_ge(s_hm, 4)
            pool.affine_select(out=hmask[:, :], in_=hmask[:, :], compare_op=ALU.is_ge, fill=0.0, base=DH - 1,
                               pattern=[[DH, P // DH]], channel_multiplier=-1).then_inc(s_hm, 1)

            def power(n):
                pool.wait_ge(s_lnv, n + 1)
                pool.tensor_tensor(rstd[:, :], vare[:, :], mhalf[:, :], ALU.pow).then_inc(s_lnr, 1)

            power(0)
            pool.memset(zero[:, :], 0.0).then_inc(s_c, 1)
            pool.wait_ge(s_v, NCTX // CHUNK)
            pool.wait_ge(s_rs[0], 16 * NSUPER * (P // DH))
            pool.wait_ge(s_rs[1], 16 * NSUPER * (P // DH))
            pool.memset(vr[:, :, :, :], 0.0).then_inc(s_c, 1)
            pool.wait_ge(s_c, 7)
            pool.memset(vr[:, :, :, DH:DH + 1], 1.0).then_inc(s_c, 1)
            pool.memset(woP[:, :, :], 0.0).then_inc(s_woz, 1)
            pool.wait_ge(s_c, 8)

            def ring(g, it):
                for u in range(UN):
                    s, k = u % 2, (g * NIT + it) * (UN // 2) + u // 2
                    pool.wait_ge(s_pv[s], 1 + k)
                    src = val[:, bass.ds(it * UN + u, 1), bass.ds(g * GROUP * DH, GROUP * DH)]
                    pool.tensor_copy(vr[:, s, :, 0:DH], src[:, 0].rearrange("p (j d) -> p j d", d=DH))\
                        .then_inc(s_vr[s], 1)

            with pool.Fori(0, NG) as g:
                with pool.Fori(0, NIT) as it:
                    ring(g, it)
            pool.wait_ge(s_pv[1], 1 + NG * NIT * (UN // 2))
            pool.memset(vp[:, :, :, :], 0.0).then_inc(s_woz, 1)
            for n in range(1, 5):
                power(n)

        @block.scalar
        def _(act):
            free_at_first(act, *s_p, s_zt, s_hc[2], s_hc[3])
            act.dma_start(x_sb[:, :, :], x[0].rearrange("(t p) d -> p t d", p=P)).then_inc(s_in, 16)
            act.dma_start(wn[:, 0], xWq.rearrange("(t p) i -> p t i", p=P)).then_inc(s_w, 16)
            for c, b in ((bq_c, xbq), (bk_c, xbk), (abq_c, abq), (abk_c, abk), (abl_c, abl)):
                act.dma_start(c[:, :], b.rearrange("(t p) -> p t", p=c.shape[0])).then_inc(s_b, 16)
            act.dma_start(gcb_b[:, :], bcast(gcb)).then_inc(s_b, 16)
            act.wait_ge(s_ob, 1)
            one = onesb[0:MROWS, :]
            act.dma_start(kst[ROWS:ROWS + MROWS, :, :].rearrange("p a b -> p (a b)"),
                          bass.AP(one.tensor, one.offset, [list(one.ap[0]), [0, H * NCTX // NT], list(one.ap[1])]))\
               .then_inc(s_ones, 16)
            for i, to in enumerate((wT[:, 0], wT[:, 1], wqT)):
                act.wait_ge(s_wt, i + 1)
                act.activation(to.rearrange("p k o -> p (k o)") if i < 2 else to[:, :, :].rearrange("p k o -> p (k o)"),
                               psum[:, 1 + i], ACT.Copy).then_inc(s_wtc, 1)

            def half(s, c):
                act.wait_ge(s_tr[s], c + 1)
                if not first(c):
                    act.wait_ge(s_kmm[1] if s == 0 else s_vmm[1], 2 * c - 1 if s == 0 else c)
                act.activation(cT[:, s, 0], psum[:, 0], ACT.Copy).then_inc(s_ta[s], 1)

            def values(s, c):
                act.wait_ge(s_vmm[s], c + 1)
                act.activation(val[:, bass.ds(4 * (2 * c + s), 4), :].rearrange("p a b -> p (a b)"),
                               psum[:, 4:6, :].rearrange("p a b -> p (a b)"), ACT.Copy).then_inc(s_v, 1)

            def keys(s, c):
                n = 2 * c + s
                sl = slice(s * CHUNK, (s + 1) * CHUNK)
                for o in range(DT):
                    act.wait_ge(s_kmm[o], n + 1)
                    if not first(c):
                        act.wait_ge(s_rs[o], 16 * (P // DH) * c)
                    act.activation(kp[:, o, 0, sl], psum[:, 2 + o], ACT.Identity, bias=bk_c[:, o:o + 1])\
                       .then_inc(s_k1[o], 1)
                for o in range(DT):
                    act.wait_ge(s_r1[o], n + 1)
                    act.activation(kp[:, o, 1, sl], r1[:, o], ACT.Copy).then_inc(s_k2[o], 1)
                for o in range(DT):
                    act.wait_ge(s_k1[o], n + 1)
                    part = kp[:, o, 0, sl]
                    act.activation(kp[:, o, 3:6:2, sl],
                                   bass.AP(part.tensor, part.offset, [list(part.ap[0]), [0, 2], list(part.ap[1])]),
                                   ACT.Copy).then_inc(s_kb[o], 2)

            def superchunk(c):
                half(1, c)
                values(0, c)
                keys(0, c)
                half(0, c + 1)
                keys(1, c)
                values(1, c)

            act.wait_ge(s_b, 16 * 6)
            half(0, 0)
            act.wait_ge(s_xt, 1)
            act.activation(xT[:, :, :], psum[:, 7].rearrange("p (k t) -> p k t", k=DT), ACT.Copy).then_inc(s_xtc, 1)
            for o in range(DT):
                act.wait_ge(s_q, o + 1)
                act.activation(qp[:, o, 0, :], psum[:, 4 + o, 0:NT], ACT.Identity,
                               bias=bq_c[:, o:o + 1]).then_inc(s_q1, 1)
            act.wait_ge(s_q1, 2)
            act.activation(qp[:, :, 1, :], qp[:, :, 0, :], ACT.Copy).then_inc(s_qp, 1)
            act.activation(qp[:, :, 2, :], qp[:, :, 0, :], ACT.Copy).then_inc(s_qp, 1)
            act.wait_ge(s_qr, 2)
            act.activation(qp[:, :, 3, :], q1[:, :, :], ACT.Copy).then_inc(s_q2, 1)
            act.wait_ge(s_q2, 1)
            act.activation(qp[:, :, 4, :], qp[:, :, 3, :], ACT.Copy).then_inc(s_qp, 1)
            superchunk(0)
            act.wait_ge(s_qst, 16 * H)
            act.wait_ge(s_ones, 16)
            with act.Fori(1, NSUPER - 1) as c:
                superchunk(c)
            half(1, NSUPER - 1)
            values(0, NSUPER - 1)
            keys(0, NSUPER - 1)
            keys(1, NSUPER - 1)
            values(1, NSUPER - 1)

            for o in range(DT):
                act.wait_ge(s_rs[o], 16 * NSUPER * (P // DH))
            for c, b in ((bv_b, xbv), (gam_b, xgamma), (bet_b, xbeta)):
                act.dma_start(c[:, :], bcast(b)).then_inc(s_par, 16)

            def m_rows(g):
                act.wait_ge(s_mr, g + 1)
                act.activation(qst[ROWS:ROWS + MROWS, bass.ds(g * GROUP, GROUP), :]
                               .rearrange("p a b -> p (a b)"),
                               psum[ROWS:ROWS + MROWS, 5:7, :].rearrange("p a b -> p (a b)"),
                               ACT.Copy).then_inc(s_mq, 1)

            def exps(g, it):
                for u in range(UN):
                    s, k = u % 2, (g * NIT + it) * (UN // 2) + u // 2
                    act.wait_ge(s_s[s], k + 1)
                    act.wait_ge(s_pv[s], 1 + k)
                    act.activation(pr[:, s], ps_s[s].rearrange("p a b -> p (a b)"), ACT.Exp).then_inc(s_p[s], 1)

            def sums(g):
                act.wait_ge(s_pv[1], 1 + (g + 1) * NIT * (UN // 2))
                act.wait_ge(s_zp, 1 + g)
                act.activation(zt[:, :], ps_pv, ACT.Copy).then_inc(s_zt, 1)

            m_rows(0)
            with act.Fori(0, NG - 1) as g:
                with act.Fori(0, NIT) as it:
                    exps(g, it)
                sums(g)
                m_rows(g + 1)
            with act.Fori(0, NIT) as it:
                exps(NG - 1, it)
            sums(NG - 1)

            act.wait_ge(s_prm, 16 * NPRM)

            def rot(a):
                return a.rearrange("p i k d -> p (i k d)")

            def rbank(i):
                return psum[:, i].rearrange("p (k d) -> p k d", k=DT)

            act.activation(rot(rL[:, :, :, :]), rot(rA[:, :, :, :]), ACT.Copy, scale=2.0 ** -SQUARINGS)\
               .then_inc(s_rA, 1)

            def rcopy(n0):
                for i in range(NROT):
                    act.wait_ge(s_rt, n0 + i + 1)
                    act.activation(rT[:, i], rbank(3 + i), ACT.Copy).then_inc(s_rtc, 1)

            for m in range(3):
                rcopy(NROT * m)
            with act.Fori(0, SQUARINGS) as m:
                rcopy(NROT * (m + 3))
            for i in (0, 1):
                act.wait_ge(s_rt, NROT * (3 + SQUARINGS) + i + 1)
                act.activation(rT[:, 0], rbank(3), ACT.Copy).then_inc(s_rtc, 1)

            act.wait_ge(s_t2, 1)
            act.activation(xT2[:, :, :], rbank(6), ACT.Copy).then_inc(s_t2c, 1)
            act.wait_ge(s_al, 1)
            act.activation(latT[:, :], psum[0:LAT, 2, 0:NT], ACT.Identity, bias=abl_c[:, 0:1]).then_inc(s_alc, 1)
            act.wait_ge(s_ak, 1)
            for o in range(DT):
                act.activation(kT[:, o], psum[:, 3, o * NT:(o + 1) * NT], ACT.Identity, bias=abk_c[:, o:o + 1])\
                   .then_inc(s_akc, 1)
            for n in range(STEPS):
                act.wait_ge(s_anm, n + 1)
                if n >= 2:
                    act.wait_ge(s_at, n - 1)
                for j in range(2):
                    act.activation(pa[:, n % 2, j], psum[:, n % 2, j * NT:(j + 1) * NT], ACT.Exp,
                                   bias=nm[:, 2 * n + j:2 * n + j + 1],
                                   accum_out=rs[:, 2 * n + j:2 * n + j + 1]).then_inc(s_ae, 1)
                if n >= 1 and (n - 1) % 2 == 0:
                    att_copy(act.activation, n - 1, act, s_at, s_atA)
            for g in range(NG):
                act.wait_ge(s_az, g + 1)
                act.activation(zT[:, g], psum[:, 5 + g // 2, (g % 2) * NT:(g % 2 + 1) * NT], ACT.Copy)\
                   .then_inc(s_azc, 1)

            act.wait_ge(s_e1t, 1)
            act.activation(eb1_c[:, :], psum[:, 4, 0:E * HT], ACT.Copy).then_inc(s_e1c, 1)
            act.wait_ge(s_t3, 1)
            act.activation(xgT[:, :, :], rbank(0), ACT.Copy).then_inc(s_t3c, 1)
            act.wait_ge(s_lm, 1)
            for t in range(TT):
                act.activation(ex[:, t], lg[:, t], ACT.Exp, bias=lm[:, t:t + 1]).then_inc(s_ex, 1)
            act.wait_ge(s_abi, 2)
            act.activation(abel[:, :, :], abin[:, :, :], ACT.Gelu).then_inc(s_abel, 1)
            act.wait_ge(s_wt8, 1)
            act.activation(wdT[:, :], psum[0:E, 3, 0:NT], ACT.Copy).then_inc(s_wt8c, 1)

            def hidden(r, s):
                act.wait_ge(s_h[s], r + 1)
                act.wait_ge(s_eo[(s + 2) % SLOTS], 1 + r + (s >= 2))
                for t in range(HT):
                    act.activation(hT[:, s % 2, t], psum[:, 4 + 2 * (s % 2) + t // 2, (t % 2) * NT:(t % 2 + 1) * NT],
                                   ACT.Gelu, bias=eb1_c[:, bass.ds((r * SLOTS + s) * HT + t, 1)]).then_inc(s_hc[s], 1)

            with act.Fori(0, E // SLOTS) as r:
                for s in range(SLOTS):
                    hidden(r, s)
            act.wait_ge(s_mt, 1)
            act.activation(moeT[:, :, :], rbank(0), ACT.Copy).then_inc(s_mtc, 1)
            act.wait_ge(s_gz, 1)
            act.activation(gs[:, 3], gs[:, 1], ACT.Sigmoid).then_inc(s_ge, 1)

        @block.vector
        def _(dve):
            ch = Chain(dve, s_dve)

            def norm(n, dst, src):
                for t in range(TT):
                    ch.step(dve.bn_stats(stats[:, t], src[:, t]))
                for t in range(TT):
                    ch.step(dve.bn_aggr(mv[:, t], stats[:, t]))
                dve.tensor_scalar(vare[:, :], mv[:, :, 1], EPS, None, ALU.add).then_inc(s_lnv, 1)
                dve.wait_ge(s_lnr, n + 1)
                for t in range(TT):
                    last = dve.tensor_scalar(dst[:, t], src[:, t], mv[:, t, 0:1], rstd[:, t:t + 1],
                                             ALU.subtract, ALU.mult)
                    last.then_inc(s_ln, 1)

            free_at_first(dve, *s_mx, s_z)
            dve.memset(onesb[:, :], 1.0).then_inc(s_ob, 1)
            dve.wait_ge(s_in, 16)
            norm(0, dec, x_sb)
            dve.wait_ge(s_b, 16 * 6)

            def half(s, c):
                dve.wait_ge(s_tr[s], c + 1)
                if not first(c):
                    dve.wait_ge(s_kmm[1] if s == 0 else s_vmm[1], 2 * c - 1 if s == 0 else c)
                dve.tensor_copy(cT[:, s, 1], psum[:, 1]).then_inc(s_tv[s], 1)

            def remainder(s, c, o):
                n = 2 * c + s
                dve.wait_ge(s_k1[o], n + 1)
                if not first(c) or s > 0:
                    dve.wait_ge(s_kd[o], 2 * n)
                dve.scalar_tensor_tensor(r1[:, o], psum[:, 2 + o], bk_c[:, o:o + 1],
                                         kp[:, o, 0, s * CHUNK:(s + 1) * CHUNK],
                                         ALU.add, ALU.subtract).then_inc(s_r1[o], 1)

            def last_parts(s, c, o):
                sl = slice(s * CHUNK, (s + 1) * CHUNK)
                dve.wait_ge(s_k2[o], 2 * c + s + 1)
                dve.wait_ge(s_r1[o], 2 * c + s + 1)
                dve.tensor_tensor(kp[:, o, 2, sl], r1[:, o], kp[:, o, 1, sl], ALU.subtract).then_inc(s_kd[o], 1)
                dve.tensor_copy(kp[:, o, 4, sl], kp[:, o, 1, sl]).then_inc(s_kd[o], 1)

            def first_maxima(c, pairs):
                for v in [v for pair in pairs for v in (2 * pair, 2 * pair + 1)]:
                    b, uses, before = (max_bank(v) if c is LAST_SUPER else (1 + v % 2, 8, v // 2))
                    j, t, half = v // 4, v // 2 % 2, v % 2
                    dve.wait_ge(s_mmm[b], (8 * (NSUPER - 1) * (b > 0) if c is LAST_SUPER else uses * c) + before + 1)
                    dve.tensor_reduce(mx0[:, j, t, bass.ds(2 * c + half, 1)], psum[:, MB[b]], AX.X, ALU.max)\
                        .then_inc(s_mx[b], 1)

            def project(s, c, m):
                if s == 0:
                    m(range(0, 2))
                remainder(s, c, 0)
                m(range(4 * s + 2 * (s == 0), 4 * s + 2 * (s == 0) + 1))
                remainder(s, c, 1)
                m(range(4 * s + 2 * (s == 0) + 1, 4 * s + 2 * (s == 0) + 2))
                last_parts(s, c, 0)
                if s == 1:
                    m(range(6, 7))
                last_parts(s, c, 1)
                if s == 1:
                    m(range(7, 8))

            def no_maxima(pairs):
                pass

            half(0, 0)
            for o in range(DT):
                dve.wait_ge(s_q1, o + 1)
                dve.scalar_tensor_tensor(q1[:, o, :], psum[:, 4 + o, 0:NT], bq_c[:, o:o + 1],
                                         qp[:, o, 0, :], ALU.add, ALU.subtract).then_inc(s_qr, 1)
            dve.wait_ge(s_q2, 1)
            dve.wait_ge(s_qr, 2)
            dve.tensor_tensor(qp[:, :, 5, :], q1[:, :, :], qp[:, :, 3, :], ALU.subtract).then_inc(s_qp, 3)
            half(1, 0)
            project(0, 0, no_maxima)
            half(0, 1)
            project(1, 0, no_maxima)
            with dve.Fori(1, NSUPER - 1) as c:
                def before(pairs):
                    first_maxima(c - 1, pairs)
                half(1, c)
                project(0, c, before)
                half(0, c + 1)
                project(1, c, before)

            def before_last(pairs):
                first_maxima(NSUPER - 2, pairs)
            half(1, NSUPER - 1)
            project(0, NSUPER - 1, before_last)
            project(1, NSUPER - 1, before_last)
            first_maxima(LAST_SUPER, range(8))
            for b in range(3):
                dve.wait_ge(s_mx[b], MX0[b])
            dve.tensor_reduce(negm[:, :, :].rearrange("p j t -> p (j t)"),
                              mx0[:, :, :, :].rearrange("p j t k -> p (j t) k"),
                              AX.X, ALU.max, negate=True).then_inc(s_mxh, 1)

            def maxima(body, it):
                for v in range(16):
                    b, uses, before = max_bank(v)
                    dve.wait_ge(s_mmm[b], FIRST_USES[b] + body * uses + before + 1)
                    if v == 0:
                        dve.wait_ge(s_mxh, 1 + body)
                    dve.tensor_reduce(mxs[:, v // 8, v % 8:v % 8 + 1], psum[:, MB[b]], AX.X, ALU.max)\
                        .then_inc(s_mx[b], 1)
                for b in range(3):
                    dve.wait_ge(s_mx[b], MX0[b] + (body + 1) * MAX_USES[b])
                dve.tensor_reduce(negm[:, bass.ds(it, 1), :].rearrange("p a t -> p (a t)"), mxs[:, :, :],
                                  AX.X, ALU.max, negate=True).then_inc(s_mxh, 1)

            def m_parts(g):
                nm = negm[:, :, :].rearrange("p j t -> p (j t)")
                dve.wait_ge(s_mxh, 1 + g * NIT)
                dve.tensor_copy(mp[:, :, 0], nm).then_inc(s_mp, 1)
                dve.wait_ge(s_mp, 5 * g + 1)
                dve.tensor_tensor(mrem[:, 0], nm, mp[:, :, 0], ALU.subtract).then_inc(s_mp, 1)
                dve.wait_ge(s_mp, 5 * g + 2)
                dve.tensor_copy(mp[:, :, 1], mrem[:, 0]).then_inc(s_mp, 1)
                dve.wait_ge(s_mp, 5 * g + 3)
                dve.tensor_tensor(mrem[:, 1], mrem[:, 0], mp[:, :, 1], ALU.subtract).then_inc(s_mp, 1)
                dve.wait_ge(s_mp, 5 * g + 4)
                dve.tensor_copy(mp[:, :, 2], mrem[:, 1]).then_inc(s_mp, 1)

            def divide(g):
                dve.wait_ge(s_zp, 1 + g + 1)
                zp = psum[:, 7, 0:TT * P].rearrange("p (t j c) -> p t j c", t=TT, c=VW)
                dve.reciprocal(rden[:, :, :], zp[:, :, :, DH]).then_inc(s_z, 1)
                dve.wait_ge(s_z, 1 + ZSTEPS * g + 1)
                cols = bass.ds(g * GROUP * DH, GROUP * DH)
                for t in range(TT):
                    dve.tensor_tensor(zq[:, t, cols].rearrange("p (j d) -> p j d", d=DH),
                                      zp[:, t, :, 0:DH], spread(rden[:, t], DH), ALU.mult).then_inc(s_z, 1)
                dve.wait_ge(s_z, 1 + ZSTEPS * g + 1 + TT)
                for t in range(TT):
                    dve.tensor_tensor(zq[:, t, cols], zq[:, t, cols], bv_b[:, cols], ALU.add).then_inc(s_z, 1)

            m_parts(0)
            dve.wait_ge(s_par, 16 * 3)
            with dve.Fori(0, NG - 1) as g:
                with dve.Fori(0, NIT) as it:
                    maxima(NIT * g + it, it)
                m_parts(g + 1)
                divide(g)
            divide(NG - 1)
            dve.wait_ge(s_zz, 16 * TT * H)
            ch.step(dve.tensor_tensor(z[:, :, :], z[:, :, :], dec[:, :, :], ALU.add))
            norm(1, ln_t, z)
            dve.wait_ge(s_ln, 4)
            for t in range(TT):
                ch.step(dve.tensor_tensor(ln_t[:, t], ln_t[:, t], gam_b[:, :], ALU.mult))
                ch.step(dve.tensor_tensor(ln_t[:, t], ln_t[:, t], bet_b[:, :], ALU.add))
            ch.step(dve.tensor_tensor(x_sb[:, :, :], x_sb[:, :, :], ln_t[:, :, :], ALU.add))

            def rot(a):
                return a.rearrange("p i k d -> p (i k d)")

            def flat(a):
                return a.rearrange("p k d -> p (k d)")

            dve.wait_ge(s_prm, 16 * NPRM)
            dve.wait_ge(s_rA, 1)
            dve.tensor_copy(rot(rA[:, :, :, :]), rot(rL[:, :, :, :])).then_inc(s_rv, 1)
            dve.wait_ge(s_rv, 1)
            for i in range(NROT):
                dve.wait_ge(s_rm, i + 1)
                ch.step(dve.tensor_copy(flat(rA2[:, i]), psum[:, i]))
                dve.scalar_tensor_tensor(flat(rU[:, i]), flat(rA2[:, i]), T1 / T2, flat(rA[:, i]), ALU.mult, ALU.add)\
                   .then_inc(s_rv, 1)
            for i in range(NROT):
                dve.wait_ge(s_rm, NROT + i + 1)
                y, a2, a, l, u = flat(rY[:, i]), flat(rA2[:, i]), flat(rA[:, i]), flat(rL[:, i]), flat(rU[:, i])
                ch.step(dve.tensor_scalar(y, psum[:, i], T2, None, ALU.mult))
                ch.step(dve.scalar_tensor_tensor(l, a, T4, y, ALU.mult, ALU.add))
                ch.step(dve.scalar_tensor_tensor(l, a2, T3, l, ALU.mult, ALU.add))
                ch.step(dve.scalar_tensor_tensor(u, a2, T5, y, ALU.mult, ALU.add))
                ch.step(dve.scalar_tensor_tensor(y, y, T6, a, ALU.mult, ALU.add))
                dve.scalar_tensor_tensor(y, a2, 0.5, y, ALU.mult, ALU.add).then_inc(s_rv, 1)
            for i in range(NROT):
                dve.wait_ge(s_rm, 2 * NROT + i + 1)
                dve.wait_ge(s_rv, 1 + NROT + i + 1)
                dve.tensor_tensor(flat(rY[:, i]), flat(rY[:, i]), psum[:, i], ALU.add).then_inc(s_rv, 1)
            with dve.Fori(0, SQUARINGS) as m:
                for i in range(NROT):
                    dve.wait_ge(s_rm, (m + 3) * NROT + i + 1)
                    dve.wait_ge(s_rv, (m + 3) * NROT + i + 1 - NROT + 1)
                    dve.scalar_tensor_tensor(flat(rY[:, i]), flat(rY[:, i]), 2.0, psum[:, i], ALU.mult, ALU.add)\
                       .then_inc(s_rv, 1)
            for i in (1, 2):
                n = NROT * (3 + SQUARINGS) + i - 1
                dve.wait_ge(s_rm, n + 1)
                dve.wait_ge(s_rv, 1 + n)
                ch.step(dve.tensor_tensor(flat(rY[:, 0]), flat(rY[:, 0]), flat(rY[:, i]), ALU.add))
                dve.tensor_tensor(flat(rY[:, 0]), flat(rY[:, 0]), psum[:, 0], ALU.add).then_inc(s_rv, 1)

            norm(2, n2, x_sb)
            dve.wait_ge(s_hm, 5)
            dve.wait_ge(s_aq, 1)
            for o in range(DT):
                dve.tensor_scalar(qf[:, o], psum[:, 1, o * NT:(o + 1) * NT], abq_c[:, o:o + 1], None, ALU.add)\
                   .then_inc(s_qf, 1)
            dve.wait_ge(s_qf, 2)
            for h in range(H):
                o, j = divmod(h, P // DH)
                dve.tensor_scalar(qm[:, h], qf[:, o], hmask[:, j:j + 1], None, ALU.mult).then_inc(s_qm, 1)
            dve.wait_ge(s_av, 1)
            dve.wait_ge(s_woz, 2)
            for t in range(TT):
                dve.tensor_tensor(vp[:, t, :, 0:DH], psum[:, 4, t * D:(t + 1) * D].rearrange("p (h d) -> p h d", d=DH),
                                  abv_b[:, :].rearrange("p (h d) -> p h d", d=DH), ALU.add).then_inc(s_avc, 1)

            def att_max(n):
                dve.wait_ge(s_as, n + 1)
                dve.tensor_reduce(nm[:, 2 * n:2 * n + 2], psum[:, n % 2, :].rearrange("p (j k) -> p j k", j=2),
                                  AX.X, ALU.max, negate=True).then_inc(s_anm, 1)

            att_max(0)
            for n in range(STEPS):
                if n + 1 < STEPS:
                    att_max(n + 1)
                dve.wait_ge(s_ae, 2 * n + 2)
                dve.reciprocal(rr[:, 2 * n:2 * n + 2], rs[:, 2 * n:2 * n + 2]).then_inc(s_ar, 1)
                dve.wait_ge(s_ar, n + 1)
                for j in range(2):
                    dve.tensor_scalar(pa[:, n % 2, j], pa[:, n % 2, j], rr[:, 2 * n + j:2 * n + j + 1], None, ALU.mult)\
                       .then_inc(s_an, 1)
                if n >= 1 and (n - 1) % 2 == 1:
                    att_copy(dve.tensor_copy, n - 1, dve, s_at, s_atV)
            att_copy(dve.tensor_copy, STEPS - 1, dve, s_at, s_atV)
            dve.wait_ge(s_ao, 1)
            for t in range(TT):
                ch.step(dve.tensor_tensor(x_sb[:, t], x_sb[:, t], abo_b[:, :], ALU.add))
                ch.step(dve.tensor_tensor(x_sb[:, t], x_sb[:, t], psum[:, 7, t * D:(t + 1) * D], ALU.add))

            norm(3, xp, x_sb)
            dve.wait_ge(s_ln, 8)
            norm(4, xg, xp)
            dve.wait_ge(s_ln, 10)
            for t in range(TT):
                ch.step(dve.tensor_tensor(xg[:, t], xg[:, t], lng_b[:, :], ALU.mult))
                dve.tensor_tensor(xg[:, t], xg[:, t], lnb_b[:, :], ALU.add).then_inc(s_x2, 1)
            ch.step(dve.tensor_tensor(x_sb[:, :, :], x_sb[:, :, :], xp[:, :, :], ALU.add))
            dve.wait_ge(s_lg, 1)
            for t in range(TT):
                ch.step(dve.tensor_tensor(lg[:, t], psum[:, 2, t * E:(t + 1) * E], gb_b[:, :], ALU.add))
            dve.tensor_reduce(lm[:, :], lg[:, :, :], AX.X, ALU.max, negate=True).then_inc(s_lm, 1)
            dve.wait_ge(s_ab, 1)
            for t in range(TT):
                dve.tensor_tensor(abin[:, t], psum[:, 1, t * D:(t + 1) * D], abb_b[:, :], ALU.add).then_inc(s_abi, 1)
            for t in range(TT):
                row = lg[:, t]
                other = bass.AP(row.tensor, row.offset, [list(row.ap[0]), [0, E], list(row.ap[1])])
                ch.step(dve.tensor_tensor(cgt[:, t], other, spread(row, E), ALU.is_gt))
                ch.step(dve.tensor_tensor(ceq[:, t], other, spread(row, E), ALU.is_equal))
                ch.step(dve.tensor_tensor(ceq[:, t], ceq[:, t], tri[:, :, :], ALU.mult))
                ch.step(dve.tensor_tensor(cgt[:, t], cgt[:, t], ceq[:, t], ALU.add))
            ch.step(dve.tensor_reduce(rank[:, :, :], cgt[:, :, :, :], AX.X, ALU.add))
            ch.step(dve.tensor_scalar(rank[:, :, :], rank[:, :, :], 2.0, None, ALU.is_lt))
            dve.wait_ge(s_ex, 2)
            ch.step(dve.tensor_tensor(wd[:, :, :], ex[:, :, :], rank[:, :, :], ALU.mult))
            ch.step(dve.tensor_reduce(wsum[:, :], wd[:, :, :], AX.X, ALU.add))
            ch.step(dve.reciprocal(wsum[:, :], wsum[:, :]))
            for t in range(TT):
                dve.tensor_scalar(wd[:, t], wd[:, t], wsum[:, t:t + 1], None, ALU.mult).then_inc(s_wd, 1)
            dve.wait_ge(s_b2, 1)
            dve.tensor_copy(moe[:, :, :].rearrange("p t d -> p (t d)"), psum[:, 0]).then_inc(s_acc, 1)
            dve.wait_ge(s_wd, 2)
            with dve.Fori(0, E // SLOTS) as r:
                for s in range(SLOTS):
                    dve.wait_ge(s_eo[s], 1 + r + 1)
                    for t in range(TT):
                        dve.wait_ge(s_acc, (r * SLOTS + s) * TT + t + (1 if t == 0 else 0))
                        dve.scalar_tensor_tensor(moe[:, t], psum[:, 2 + s % 2, t * D:(t + 1) * D],
                                                 wd[:, t, bass.ds(r * SLOTS + s, 1)], moe[:, t],
                                                 ALU.mult, ALU.add).then_inc(s_acc, 1)
            dve.wait_ge(s_rot, 1)
            dve.wait_ge(s_acc, 1 + E * TT)
            ch.step(dve.tensor_tensor(moe2[:, :, :].rearrange("p t d -> p (t d)"), psum[:, 1],
                                      moe[:, :, :].rearrange("p t d -> p (t d)"), ALU.add))
            dve.wait_ge(s_abel, 1)
            for t in range(TT):
                ch.step(dve.tensor_tensor_reduce(junk[:, :], abel[:, t], gcw_b[:, 0], 1.0, 0.0, ALU.mult, ALU.add,
                                                 gs[:, 0, t:t + 1]))
                ch.step(dve.tensor_tensor_reduce(junk[:, :], moe2[:, t], gcw_b[:, 1], 1.0, 0.0, ALU.mult, ALU.add,
                                                 gs[:, 1, t:t + 1]))
            ch.step(dve.tensor_tensor(gs[:, 1], gs[:, 0], gs[:, 1], ALU.add))
            dve.tensor_scalar(gs[:, 1], gs[:, 1], gcb_b[:, 0:1], None, ALU.add).then_inc(s_gz, 1)
            dve.wait_ge(s_ge, 1)
            ch.step(dve.tensor_scalar(gs[:, 4], gs[:, 3], -1.0, 1.0, ALU.mult, ALU.add))
            for t in range(TT):
                ch.step(dve.scalar_tensor_tensor(x_sb[:, t], abel[:, t], gs[:, 4, t:t + 1], x_sb[:, t], ALU.mult, ALU.add))
                ins = dve.scalar_tensor_tensor(moe2[:, t], moe2[:, t], gs[:, 3, t:t + 1], x_sb[:, t], ALU.mult, ALU.add)
                ins.then_inc(s_out, 1)

        @block.tensor
        def _(pe):
            def transpose4(dst, src):
                for k in range(2):
                    for t in range(2):
                        last = pe.transpose(dst[:, k * 256 + t * P:k * 256 + (t + 1) * P],
                                            src[:, t, k * P:(k + 1) * P], identf[:, :])
                return last

            free_at_first(pe, *s_pv, s_zp, *s_eo)
            pe.wait_ge(s_c, 4)
            pe.wait_ge(s_w, 16 * 3)
            for bank, i in ((1, 1), (2, 2), (3, 0)):
                transpose4(psum[:, bank], wn[:, i]).then_inc(s_wt, 1)

            def turn(s, c):
                pe.wait_ge(s_ctx[s], 16 * (c + 1))
                if s > 0 or not first(c):
                    pe.wait_ge(s_ta[1 - s], c + s)
                    pe.wait_ge(s_tv[1 - s], c + s)
                for k in range(DT):
                    for t in range(CHUNK // P):
                        last = pe.transpose(psum[:, k, t * P:(t + 1) * P],
                                            cs[:, s, t, k * P:(k + 1) * P], identf[:, :])
                last.then_inc(s_tr[s], 1)

            def project_keys(s, c, o):
                if s > 0 or not first(c):
                    pe.wait_ge(s_r1[o], 2 * c + s)
                for k in range(DT):
                    last = pe.matmul(psum[:, 2 + o], wT[:, 0, k, o * P:(o + 1) * P], cT[:, s, k],
                                     start=(k == 0), stop=(k == DT - 1))
                last.then_inc(s_kmm[o], 1)

            def project_values(s, c, half):
                if half == 0 and (s > 0 or not first(c)):
                    pe.wait_ge(s_v, 2 * c + s)
                for t in (2 * half, 2 * half + 1):
                    for k in range(DT):
                        last = pe.matmul(psum[:, 4 + t // 2, (t % 2) * D:(t % 2 + 1) * D],
                                         cT[:, s, k, t * P:(t + 1) * P], wT[:, 1, k, :],
                                         start=(k == 0), stop=(k == DT - 1))
                if half == 1:
                    last.then_inc(s_vmm[s], 1)

            def project(s, c, maxima):
                pe.wait_ge(s_ta[s], c + 1)
                pe.wait_ge(s_tv[s], c + 1)
                steps = [(project_values, 0), (project_values, 1), (project_keys, 0), (project_keys, 1)]
                for i, (step, which) in enumerate(steps if s == 0 else steps[2:] + steps[:2]):
                    step(s, c, which)
                    maxima(4 * s + i)

            def first_maxima(c, pair):
                for v in (2 * pair, 2 * pair + 1):
                    j, t, half = v // 4, v // 2 % 2, v % 2
                    if c is LAST_SUPER:
                        b, _, before = max_bank(v)
                        before += 8 * (NSUPER - 1) * (b > 0)
                    else:
                        b, before = 1 + v % 2, 8 * c + v // 2
                    pe.wait_ge(s_mx[b], 1 + before)
                    pe.matmul(psum[:, MB[b]], qst[0:ROWS, j, t * P:(t + 1) * P],
                              kst[0:ROWS, j, bass.ts(2 * c + half, 512)], start=True, stop=True)\
                      .then_inc(s_mmm[b], 1)

            def no_maxima(pair):
                pass

            pe.wait_ge(s_wtc, 3)
            turn(0, 0)
            pe.wait_ge(s_ln, 2)
            transpose4(psum[:, 7], dec).then_inc(s_xt, 1)
            pe.wait_ge(s_xtc, 1)
            for o in range(DT):
                for k in range(DT):
                    last = pe.matmul(psum[:, 4 + o, 0:NT], wqT[:, k, o * P:(o + 1) * P], xT[:, k],
                                     start=(k == 0), stop=(k == DT - 1))
                last.then_inc(s_q, 1)
            turn(1, 0)
            pe.wait_ge(s_q1, 2)
            pe.wait_ge(s_qr, 2)
            project(0, 0, no_maxima)
            turn(0, 1)
            project(1, 0, no_maxima)
            pe.wait_ge(s_qst, 16 * H)

            def restacked(c):
                for o in range(DT):
                    pe.wait_ge(s_rs[o], 16 * c * (P // DH))

            with pe.Fori(1, NSUPER - 1) as c:
                def before(pair):
                    if pair == 0:
                        pe.wait_ge(s_rs[0], 16 * c * (P // DH))
                    first_maxima(c - 1, pair)
                turn(1, c)
                project(0, c, before)
                turn(0, c + 1)
                project(1, c, before)

            def before_last(pair):
                if pair == 0:
                    pe.wait_ge(s_rs[0], 16 * (NSUPER - 1) * (P // DH))
                first_maxima(NSUPER - 2, pair)
            turn(1, NSUPER - 1)
            project(0, NSUPER - 1, before_last)
            project(1, NSUPER - 1, before_last)

            def maxima(body, h, vs):
                for v in vs:
                    b, uses, before = max_bank(v)
                    pe.wait_ge(s_mx[b], MX0[b] + body * uses + before)
                    pe.matmul(psum[:, MB[b]], qst[0:ROWS, bass.ds(h, 1), (v // 8) * P:(v // 8 + 1) * P][:, 0],
                              kst[0:ROWS, bass.ds(h, 1), (v % 8) * 512:(v % 8 + 1) * 512][:, 0],
                              start=True, stop=True).then_inc(s_mmm[b], 1)

            def m_rows(g):
                pe.wait_ge(s_mp, 5 * (g + 1))
                for j in range(GROUP):
                    for t in range(TT):
                        col = j * NT + t * P
                        last = pe.matmul(psum[ROWS:ROWS + MROWS, 5 + col // 512, col % 512:col % 512 + P],
                                         mp[:, j * TT + t, :], identb[:, :], start=True, stop=True)
                last.then_inc(s_mr, 1)

            def scores(g, kt, s, k):
                pe.wait_ge(s_p[s], 1 + k)
                for j in range(GROUP):
                    last = pe.matmul(ps_s[s][:, j // 2, (j % 2) * NT:(j % 2 + 1) * NT],
                                     kst[0:ROWS + MROWS, bass.ds(g * GROUP + j, 1), bass.ts(kt, P)][:, 0],
                                     qst[0:ROWS + MROWS, bass.ds(g * GROUP + j, 1), :][:, 0],
                                     start=True, stop=True)
                last.then_inc(s_s[s], 1)

            def weigh(s, k, last_of_group):
                pe.wait_ge(s_p[s], 1 + k + 1)
                pe.wait_ge(s_vr[s], k + 1)
                for j in range(GROUP):
                    last = pe.matmul(psum[VW * j:VW * (j + 1), 4, 0:NT], vr[:, s, j, :],
                                     pr[:, s, j * NT:(j + 1) * NT], start=False, stop=last_of_group,
                                     skip_group_check=True, tile_position=(0, VW * j))
                last.then_inc(s_pv[s], 1)

            def open_sums(g):
                pe.wait_ge(s_zt, 1 + g)
                for j in range(GROUP):
                    pe.matmul(psum[VW * j:VW * (j + 1), 4, 0:NT], zero[:, 0:VW], zero[:, :],
                              start=True, stop=False, skip_group_check=True, tile_position=(0, VW * j))

            def body(g, it, last, following):
                for u in range(UN):
                    e = (g * NIT + it) * UN + u
                    k, k1 = (g * NIT + it) * (UN // 2) + u // 2, (g * NIT + it) * (UN // 2) + (u + 1) // 2
                    if not (last and u == UN - 1):
                        scores(g, it * UN + u + 1, (u + 1) % 2, k1)
                    if following:
                        maxima(NIT * g + it, (g + 1) * GROUP + it, (2 * u, 2 * u + 1))
                    weigh(u % 2, k, last and u == UN - 1)

            def close_sums(g):
                pe.wait_ge(s_zt, 1 + g + 1)
                for t in range(TT):
                    last = pe.transpose(psum[:, 7, t * P:(t + 1) * P], zt[:, t * P:(t + 1) * P], identf[:, :])
                last.then_inc(s_zp, 1)

            def group(g, following):
                pe.wait_ge(s_mq, g + 1)
                pe.wait_ge(s_z, 1 + ZSTEPS * g)
                open_sums(g)
                scores(g, 0, 0, g * NIT * (UN // 2))
                with pe.Fori(0, NIT - 1) as it:
                    body(g, it, False, following)
                body(g, NIT - 1, True, following)
                if following:
                    m_rows(g + 1)
                close_sums(g)

            pe.wait_ge(s_ones, 16)
            restacked(NSUPER)
            pe.wait_ge(s_c, 8)
            pe.wait_ge(s_v, NCTX // CHUNK)
            for pair in range(8):
                first_maxima(LAST_SUPER, pair)
            m_rows(0)
            with pe.Fori(0, NG - 1) as g:
                group(g, True)
            group(NG - 1, False)

            def rtrans(i, src):
                for k in range(DT):
                    for t in range(DT):
                        last = pe.transpose(psum[:, 3 + i, k * D + t * P:k * D + (t + 1) * P],
                                            src[:, t, k * P:(k + 1) * P], identf[:, :])
                last.then_inc(s_rt, 1)

            def rmul(i, right):
                for o in range(DT):
                    for k in range(DT):
                        last = pe.matmul(psum[:, i, o * D:(o + 1) * D], rT[:, i, k, o * P:(o + 1) * P], right[:, k],
                                         start=(k == 0), stop=(k == DT - 1))
                last.then_inc(s_rm, 1)

            def rstep(m, left, right, ready):
                for i in range(NROT):
                    pe.wait_ge(s_rv, ready(i))
                    rtrans(i, left[:, i])
                for i in range(NROT):
                    pe.wait_ge(s_rtc, NROT * m + i + 1)
                    rmul(i, right[:, i])

            pe.wait_ge(s_z, 1 + ZSTEPS * NG)
            pe.wait_ge(s_rA, 1)
            rstep(0, rA, rA, lambda i: 1)
            rstep(1, rA2, rU, lambda i: 1 + i + 1)
            rstep(2, rL, rU, lambda i: 1 + NROT + i + 1)
            with pe.Fori(0, SQUARINGS) as m:
                rstep(m + 3, rY, rY, lambda i: 1 + NROT * (m + 2) + i + 1)
            for i in (1, 2):
                n = NROT * (3 + SQUARINGS) + i - 1
                pe.wait_ge(s_rv, 1 + n)
                rtrans(0, rY[:, 0])
                pe.wait_ge(s_rtc, n + 1)
                rmul(0, rY[:, i])

            def product(bank, cols, left, right, ks, width=P):
                for k in ks:
                    last = pe.matmul(psum[0:width, bank, cols], left(k), right(k),
                                     start=(k == ks[0]), stop=(k == ks[-1]))
                return last

            ks = list(range(DT))
            half = [slice(0, NT), slice(NT, 2 * NT)]
            tile = [slice(t * P, (t + 1) * P) for t in range(4)]
            pe.wait_ge(s_ln, 6)
            transpose4(psum[:, 6], n2).then_inc(s_t2, 1)
            pe.wait_ge(s_t2c, 1)
            pe.wait_ge(s_rv, 1 + NROT * (3 + SQUARINGS) + 2)
            product(2, slice(0, NT), lambda k: aWl_s[:, k, :], lambda k: xT2[:, k], ks, LAT).then_inc(s_al, 1)
            for o in range(DT):
                last = product(1, half[o], lambda k: aWq_s[:, k, tile[o]], lambda k: xT2[:, k], ks)
            last.then_inc(s_aq, 1)
            pe.wait_ge(s_alc, 1)
            pe.wait_ge(s_rtc, NROT * (3 + SQUARINGS) + 2)
            for o in range(DT):
                last = product(3, half[o], lambda k: aWk_s[:, tile[o]], lambda k: latT[:, :], [0])
            last.then_inc(s_ak, 1)
            for t in range(TT):
                last = product(4, half[t], lambda k: latT[:, tile[t]], lambda k: aWv_s[:, :], [0])
            last.then_inc(s_av, 1)
            pe.wait_ge(s_akc, 2)

            def att_scores(n):
                h, t = 2 * (n // 2), n % 2
                pe.wait_ge(s_qm, h + 2)
                if n == 1:
                    pe.wait_ge(s_qf, 2)
                if n >= 2:
                    pe.wait_ge(s_ae, 2 * (n - 1))
                for j in range(2):
                    last = product(n % 2, half[j], lambda k: qm[:, h + j, tile[t]],
                                   lambda k: kT[:, (h + j) // (P // DH)], [0])
                last.then_inc(s_as, 1)

            def att_turn(n):
                pe.wait_ge(s_an, 2 * n + 2)
                if n >= 2:
                    pe.wait_ge(s_atV if n % 2 else s_atA, 2 * (n // 2))
                for j in range(2):
                    for k in range(TT):
                        last = pe.transpose(psum[:, 2 + n % 2, tile[2 * j + k]], pa[:, n % 2, j, tile[k]], identf[:, :])
                last.then_inc(s_at, 1)

            att_scores(0)
            att_scores(1)
            pe.wait_ge(s_alc, 1)
            for n in range(STEPS):
                att_turn(n)
                if n + 2 < STEPS:
                    att_scores(n + 2)
            pe.wait_ge(s_avc, 2)
            pe.wait_ge(s_atA, STEPS)
            pe.wait_ge(s_atV, STEPS)
            for g in range(NG):
                if g % 2 == 1:
                    pe.wait_ge(s_azc, g)
                for k in range(TT):
                    for j in range(GROUP):
                        last = pe.matmul(psum[VW * j:VW * (j + 1), 5 + g // 2, half[g % 2]], vp[:, k, GROUP * g + j, :],
                                         pT[:, k, GROUP * g + j, :], start=(k == 0), stop=(k == TT - 1),
                                         tile_position=(0, VW * j))
                last.then_inc(s_az, 1)
            pe.wait_ge(s_azc, NG)
            for t in range(TT):
                last = product(7, half[t], lambda g: zT[:, g, tile[t]], lambda g: woP[:, g], list(range(NG)))
            last.then_inc(s_ao, 1)

            pe.transpose(psum[:, 4, 0:E * HT], eb1_n[:, :], identf[0:E * HT, 0:E * HT]).then_inc(s_e1t, 1)
            pe.wait_ge(s_x2, 2)
            transpose4(psum[:, 0], xg).then_inc(s_t3, 1)
            pe.wait_ge(s_t3c, 1)
            for t in range(TT):
                last = product(2, slice(t * E, (t + 1) * E), lambda k: xgT[:, k, tile[t]], lambda k: gw_s[:, k], ks)
            last.then_inc(s_lg, 1)
            for t in range(TT):
                last = product(1, half[t], lambda k: xgT[:, k, tile[t]], lambda k: abw_s[:, k], ks)
            last.then_inc(s_ab, 1)
            pe.wait_ge(s_wd, 2)
            for t in range(TT):
                last = pe.transpose(psum[0:E, 3, tile[t]], wd[:, t], identf[:, :])
            last.then_inc(s_wt8, 1)
            pe.wait_ge(s_wt8c, 1)
            for t in range(TT):
                last = product(0, half[t], lambda k: wdT[:, tile[t]], lambda k: eb2_s[:, :], [0])
            last.then_inc(s_b2, 1)
            pe.wait_ge(s_e1c, 1)
            pe.wait_ge(s_lm, 1)

            def hidden(r, s):
                pe.wait_ge(s_ew1[s], 16 * (r + 1))
                if s < 2:
                    pe.wait_ge(s_hc[s + 2], 1 + HT * r)
                else:
                    pe.wait_ge(s_hc[s - 2], HT * (r + 1))
                for t in range(HT):
                    last = product(4 + 2 * (s % 2) + t // 2, half[t % 2], lambda k: ew1r[:, s, k, tile[t]],
                                   lambda k: xgT[:, k], ks)
                last.then_inc(s_h[s], 1)

            def expert_out(r, s):
                pe.wait_ge(s_ew2[s], 16 * (r + 1))
                pe.wait_ge(s_hc[s], (s >= 2) + HT * (r + 1))
                pe.wait_ge(s_acc, (r * SLOTS + s) * TT + 1)
                for t in range(TT):
                    last = product(2 + s % 2, half[t], lambda k: hT[:, s % 2, k, tile[t]],
                                   lambda k: ew2r[:, s, k], list(range(HT)))
                last.then_inc(s_eo[s], 1)

            with pe.Fori(0, E // SLOTS) as r:
                hidden(r, 0)
                for s in range(SLOTS):
                    if s + 1 < SLOTS:
                        hidden(r, s + 1)
                    expert_out(r, s)
            pe.wait_ge(s_acc, 1 + E * TT)
            transpose4(psum[:, 0], moe).then_inc(s_mt, 1)
            pe.wait_ge(s_mtc, 1)
            for t in range(TT):
                last = product(1, half[t], lambda k: moeT[:, k, tile[t]], lambda k: rY[:, 0, k], ks)
            last.then_inc(s_rot, 1)


ZSTEPS = 1 + 2 * TT
STEPS = 2 * H // 2
NPRM = 22


MAX_BANK = [v % 3 for v in range(15)] + [1]
MAX_USES = [MAX_BANK.count(b) for b in range(3)]


LAST_SUPER = NSUPER - 1
FIRST_USES = [8 * (NSUPER - 1) * (b > 0) + MAX_USES[b] for b in range(3)]
MX0 = [1 + n for n in FIRST_USES]


def first(c):
    return isinstance(c, int) and c == 0


def max_bank(v):
    b = MAX_BANK[v]
    return b, MAX_USES[b], MAX_BANK[:v].count(b)


_INS = ['x', 'ctx_1024', 'L0_xattn_Wq', 'L0_xattn_bq', 'L0_xattn_Wk', 'L0_xattn_bk', 'L0_xattn_Wv', 'L0_xattn_bv',
        'L0_xattn_gamma', 'L0_xattn_beta', 'L0_attn_Wq', 'L0_attn_bq', 'L0_attn_Wl', 'L0_attn_bl', 'L0_attn_Wk',
        'L0_attn_bk', 'L0_attn_Wv', 'L0_attn_bv', 'L0_attn_Wo', 'L0_attn_bo', 'L0_ffn_ln_gamma', 'L0_ffn_ln_beta',
        'L0_ffn_abel_w', 'L0_ffn_abel_b', 'L0_ffn_moe_gate_w', 'L0_ffn_moe_gate_b', 'L0_ffn_ew1', 'L0_ffn_eb1',
        'L0_ffn_ew2', 'L0_ffn_eb2', 'L0_ffn_gens', 'L0_ffn_gc_w', 'L0_ffn_gc_b']
_OUTS = [((1, NT, D), 'float32')]


def kernel(**inputs):
    import numpy as _np
    import concourse.bacc as _bacc
    from concourse import mybir as _mybir
    from concourse.bass_utils import run_bass_kernel_spmd as _run

    nc = _bacc.Bacc("TRN2", target_bir_lowering=False, num_devices=1, dynamic_dma_scratch_size=1024)
    arrays, args = {}, []
    for name in _INS:
        a = _np.ascontiguousarray(inputs[name])
        arrays[f"in_{name}_dram"] = a
        args.append(nc.dram_tensor(f"in_{name}_dram", a.shape, _mybir.dt.from_np(a.dtype), kind="ExternalInput").ap())
    for i, (shape, dtype) in enumerate(_OUTS):
        dt = _mybir.dt.from_np(_np.dtype(dtype))
        args.append(nc.dram_tensor(f"out_{i}_dram", shape, dt, kind="ExternalOutput").ap())
    build(nc, *args)
    r = _run(nc, [arrays], core_ids=[0])
    return r.results[0]["out_0_dram"]
```

```python
import concourse.bass as bass
from concourse import mybir
from contextlib import ExitStack

FP32 = mybir.dt.float32
BF16 = mybir.dt.bfloat16
ALU = mybir.AluOpType
ACT = mybir.ActivationFunctionType
AX = mybir.AxisListType

P = 128
D = 256
NT = 256
NCTX = 4096
H = 16
DH = D // H
DT = D // P
TT = NT // P
EPS = 1e-5

KPART = (0, 1, 2, 0, 1, 0)
QPART = (0, 0, 0, 1, 1, 2)
NB = len(KPART)
ROWS = NB * DH
MROWS = 3

CHUNK = 512
SUPER = 2 * CHUNK
NSUPER = NCTX // SUPER
GROUP = 4
NG = H // GROUP
KT = NCTX // P
UN = 8
NIT = KT // UN
LAT = D // 4
E = 8
HID = 2 * D
HT = HID // P
QTILE = 5 * KT // 8
SLOTS = 4
NROT = 3
ROT = NROT * DT * D
SQUARINGS = 6
T1, T2, T3 = 4.980119205559973e-3, 1.992047682223989e-2, 7.665265321119147e-2
T4, T5, T6 = 8.765009801785554e-1, 1.225521150112075e-1, 2.974307204847627
VW = 32


def bcast(ap, n=P):
    return bass.AP(ap.tensor, ap.offset, [[0, n]] + [list(x) for x in ap.ap])


def spread(ap, n):
    return bass.AP(ap.tensor, ap.offset, [list(x) for x in ap.ap] + [[0, n]])


class Chain:

    def __init__(self, eng, sem):
        self.eng, self.sem, self.n = eng, sem, 0

    def step(self, ins):
        self.n += 1
        ins.then_inc(self.sem, 1)
        self.eng.wait_ge(self.sem, self.n)


def build(nc, x, ctx_in, xWq, xbq, xWk, xbk, xWv, xbv, xgamma, xbeta,
          aWq, abq, aWl, abl, aWk, abk, aWv, abv, aWo, abo,
          lng, lnb, abw, abb, gw, gb, ew1, eb1, ew2, eb2, gens, gcw, gcb, out, stop=None):
    ctx = ExitStack()
    proj = ExitStack()
    with ctx:
        ctx.enter_context(nc.allow_non_contiguous_dma("biases laid along partitions"))

        def sem(name):
            return ctx.enter_context(nc.semaphore(name))

        def sems(name, n):
            return [sem(f"{name}{i}") for i in range(n)]

        def sb(name, shape, dt=FP32, where=ctx):
            return where.enter_context(nc.sbuf_tensor(name, shape, dt))

        x_sb = sb("x_sb", [P, TT, D])
        dec = sb("dec", [P, TT, D])
        identf = sb("identf", [P, P])
        identb = sb("identb", [P, P], BF16)
        stats = sb("stats", [P, TT, 6])
        mv = sb("mv", [P, TT, 2])
        vare = sb("vare", [P, TT])
        mhalf = sb("mhalf", [P, TT])
        rstd = sb("rstd", [P, TT])
        bq_c = sb("bq_c", [P, DT])
        bk_c = sb("bk_c", [P, DT])
        hmask = sb("hmask", [P, P // DH])
        tri = sb("tri", [P, E, E])
        abq_c = sb("abq_c", [P, DT])
        abk_c = sb("abk_c", [P, DT])
        abl_c = sb("abl_c", [LAT, 1])
        gcb_b = sb("gcb_b", [P, 1])
        zero = sb("zero", [P, NT], BF16)
        mx0 = sb("mx0", [P, GROUP, TT, NCTX // 512])
        mxs = sb("mxs", [P, TT, NCTX // 512])
        negm = sb("negm", [P, GROUP, TT])
        mrem = sb("mrem", [P, 2, GROUP * TT])
        mp = sb("mp", [P, GROUP * TT, MROWS], BF16)
        xattn = ExitStack()
        kst = sb("kst", [P, H, NCTX], BF16, xattn)
        with ExitStack() as early:
            wn = sb("wn", [P, 3, DT, D], FP32, early)
            wqT = sb("wqT", [P, DT, D], FP32, early)
        qst = sb("qst", [P, H, NT], BF16, xattn)
        with ExitStack() as early:
            sb("values_before", [P, QTILE, D], FP32, early)
            qp = sb("qp", [P, DT, NB, NT], BF16, early)
            q1 = sb("q1", [P, DT, NT], FP32, early)
            onesb = sb("onesb", [P, NT], BF16, early)
            xT = sb("xT", [P, DT, NT], FP32, early)
        val = sb("val", [P, KT, D], FP32, xattn)
        kp = sb("kp", [P, DT, NB, SUPER], BF16, proj)
        cs = sb("cs", [P, 2, CHUNK // P, D], FP32, proj)
        cT = sb("cT", [P, 2, DT, CHUNK], FP32, proj)
        wT = sb("wT", [P, 2, DT, D], FP32, proj)
        r1 = sb("r1", [P, DT, CHUNK], FP32, proj)
        proj.close()
        attn = ExitStack()
        zq = sb("zq", [P, TT, D], FP32, attn)
        z = sb("z", [P, TT, D], FP32, attn)
        bv_b = sb("bv_b", [P, D], FP32, attn)
        gam_b = sb("gam_b", [P, D], FP32, attn)
        bet_b = sb("bet_b", [P, D], FP32, attn)
        pr = sb("pr", [P, 2, GROUP * NT], FP32, attn)
        vr = sb("vr", [P, 2, GROUP, VW], FP32, attn)
        zt = sb("zt", [P, NT], FP32, attn)
        rden = sb("rden", [P, TT, GROUP], FP32, attn)
        aWq_s = sb("aWq_s", [P, DT, D], FP32, attn)
        aWl_s = sb("aWl_s", [P, DT, LAT], FP32, attn)
        aWk_s = sb("aWk_s", [LAT, D], FP32, attn)
        aWv_s = sb("aWv_s", [LAT, D], FP32, attn)
        woP = sb("woP", [P, NG, D], FP32, attn)
        abv_b = sb("abv_b", [P, D], FP32, attn)
        abo_b = sb("abo_b", [P, D], FP32, attn)
        lng_b = sb("lng_b", [P, D], FP32, attn)
        lnb_b = sb("lnb_b", [P, D], FP32, attn)
        abb_b = sb("abb_b", [P, D], FP32, attn)
        gb_b = sb("gb_b", [P, E], FP32, attn)
        gcw_b = sb("gcw_b", [P, 2, D], FP32, attn)
        abw_s = sb("abw_s", [P, DT, D], FP32, attn)
        gw_s = sb("gw_s", [P, DT, E], FP32, attn)
        eb1_n = sb("eb1_n", [E * HT, P], FP32, attn)
        eb2_s = sb("eb2_s", [E, D], FP32, attn)
        rA = sb("rA", [P, NROT, DT, D], FP32, attn)
        attn.close()
        xattn.close()
        late = ExitStack()
        ew1r = sb("ew1r", [P, SLOTS, DT, HID], FP32, late)
        ew2r = sb("ew2r", [P, SLOTS, HT, D], FP32, late)
        n2 = sb("n2", [P, TT, D], FP32, late)
        xT2 = sb("xT2", [P, DT, NT], FP32, late)
        qf = sb("qf", [P, DT, NT], FP32, late)
        qm = sb("qm", [P, H, NT], FP32, late)
        latT = sb("latT", [LAT, NT], FP32, late)
        kT = sb("kT", [P, DT, NT], FP32, late)
        vp = sb("vp", [P, TT, H, VW], FP32, late)
        nm = sb("nm", [P, 2 * H], FP32, late)
        rs = sb("rs", [P, 2 * H], FP32, late)
        rr = sb("rr", [P, 2 * H], FP32, late)
        pa = sb("pa", [P, 2, 2, NT], FP32, late)
        pT = sb("pT", [P, TT, H, NT], FP32, late)
        zT = sb("zT", [P, NG, NT], FP32, late)
        rT = sb("rT", [P, NROT, DT, D], FP32, late)
        rA2 = sb("rA2", [P, NROT, DT, D], FP32, late)
        rU = sb("rU", [P, NROT, DT, D], FP32, late)
        rY = sb("rY", [P, NROT, DT, D], FP32, late)
        rL = sb("rL", [P, NROT, DT, D], FP32, late)
        xp = sb("xp", [P, TT, D], FP32, late)
        xg = sb("xg", [P, TT, D], FP32, late)
        xgT = sb("xgT", [P, DT, NT], FP32, late)
        abel = sb("abel", [P, TT, D], FP32, late)
        abin = sb("abin", [P, TT, D], FP32, late)
        lg = sb("lg", [P, TT, E], FP32, late)
        lm = sb("lm", [P, TT], FP32, late)
        ex = sb("ex", [P, TT, E], FP32, late)
        cgt = sb("cgt", [P, TT, E, E], FP32, late)
        ceq = sb("ceq", [P, TT, E, E], FP32, late)
        rank = sb("rank", [P, TT, E], FP32, late)
        wsum = sb("wsum", [P, TT], FP32, late)
        wd = sb("wd", [P, TT, E], FP32, late)
        wdT = sb("wdT", [E, NT], FP32, late)
        eb1_c = sb("eb1_c", [P, E * HT], FP32, late)
        hT = sb("hT", [P, 2, HT, NT], FP32, late)
        moe = sb("moe", [P, TT, D], FP32, late)
        moeT = sb("moeT", [P, DT, NT], FP32, late)
        moe2 = sb("moe2", [P, TT, D], FP32, late)
        junk = sb("junk", [P, D], FP32, late)
        gs = sb("gs", [P, 5, TT], FP32, late)
        late.close()

        psum = ctx.enter_context(nc.psum_tensor("psum", [P, 8, 512], FP32))
        ps_s = [psum[:, 0:2, :], psum[:, 2:4, :]]
        ps_pv = psum[:, 4, 0:NT]
        MB = (5, 6, 7)

        s_c = sem("s_c")
        s_in = sem("s_in")
        s_w = sem("s_w")
        s_b = sem("s_b")
        s_ob = sem("s_ob")
        s_par = sem("s_par")
        s_ones = sem("s_ones")
        s_ctx = sems("s_ctx", 2)
        s_wt = sem("s_wt")
        s_wtc = sem("s_wtc")
        s_lnv = sem("s_lnv")
        s_lnr = sem("s_lnr")
        s_ln = sem("s_ln")
        s_xt = sem("s_xt")
        s_xtc = sem("s_xtc")
        s_kb = sems("s_kb", 2)
        s_q = sem("s_q")
        s_q1 = sem("s_q1")
        s_qr = sem("s_qr")
        s_q2 = sem("s_q2")
        s_qp = sem("s_qp")
        s_qst = sem("s_qst")
        s_tr = sems("s_tr", 2)
        s_ta = sems("s_ta", 2)
        s_tv = sems("s_tv", 2)
        s_kmm = sems("s_kmm", 2)
        s_k1 = sems("s_k1", 2)
        s_r1 = sems("s_r1", 2)
        s_k2 = sems("s_k2", 2)
        s_kd = sems("s_kd", 2)
        s_vmm = sems("s_vmm", 2)
        s_v = sem("s_v")
        s_rs = sems("s_rs", 2)
        s_mmm = sems("s_mmm", 3)
        s_mx = sems("s_mx", 3)
        s_mxh = sem("s_mxh")
        s_mp = sem("s_mp")
        s_mr = sem("s_mr")
        s_mq = sem("s_mq")
        s_s = sems("s_s", 2)
        s_p = sems("s_p", 2)
        s_pv = sems("s_pv", 2)
        s_vr = sems("s_vr", 2)
        s_zt = sem("s_zt")
        s_zp = sem("s_zp")
        s_z = sem("s_z")
        s_prm = sem("s_prm")
        s_hm = sem("s_hm")
        s_woz = sem("s_woz")
        s_ew1 = sems("s_ew1", SLOTS)
        s_ew2 = sems("s_ew2", SLOTS)
        s_t2 = sem("s_t2")
        s_t2c = sem("s_t2c")
        s_aq = sem("s_aq")
        s_al = sem("s_al")
        s_alc = sem("s_alc")
        s_ak = sem("s_ak")
        s_akc = sem("s_akc")
        s_av = sem("s_av")
        s_avc = sem("s_avc")
        s_qf = sem("s_qf")
        s_qm = sem("s_qm")
        s_as = sem("s_as")
        s_anm = sem("s_anm")
        s_ae = sem("s_ae")
        s_ar = sem("s_ar")
        s_an = sem("s_an")
        s_at = sem("s_at")
        s_atA = sem("s_atA")
        s_atV = sem("s_atV")
        s_az = sem("s_az")
        s_azc = sem("s_azc")
        s_ao = sem("s_ao")
        s_rA = sem("s_rA")
        s_rt = sem("s_rt")
        s_rtc = sem("s_rtc")
        s_rm = sem("s_rm")
        s_rv = sem("s_rv")
        s_t3 = sem("s_t3")
        s_t3c = sem("s_t3c")
        s_ab = sem("s_ab")
        s_abi = sem("s_abi")
        s_lg = sem("s_lg")
        s_lm = sem("s_lm")
        s_abel = sem("s_abel")
        s_ex = sem("s_ex")
        s_wd = sem("s_wd")
        s_wt8 = sem("s_wt8")
        s_wt8c = sem("s_wt8c")
        s_b2 = sem("s_b2")
        s_acc = sem("s_acc")
        s_e1t = sem("s_e1t")
        s_e1c = sem("s_e1c")
        s_h = sems("s_h", 4)
        s_hc = sems("s_hc", 4)
        s_eo = sems("s_eo", 4)
        s_ea = sems("s_ea", 4)
        s_mt = sem("s_mt")
        s_mtc = sem("s_mtc")
        s_rot = sem("s_rot")
        s_gz = sem("s_gz")
        s_ge = sem("s_ge")
        s_zz = sem("s_zz")
        s_dve = sem("s_dve")
        s_out = sem("s_out")
        s_fin = sem("s_fin")

        def att_copy(copy, n, eng, wait, done):
            eng.wait_ge(wait, n + 1)
            h, t = 2 * (n // 2), n % 2
            to = pT[:, :, h:h + 2, t * P:(t + 1) * P].rearrange("p k j q -> p j k q")
            fro = psum[:, 2 + n % 2, :].rearrange("p (j k q) -> p j k q", j=2, k=TT)
            args = (ACT.Copy,) if done is s_atA else ()
            for j in range(2):
                copy(to[:, j], fro[:, j], *args).then_inc(done, 1)

        def free_at_first(eng, *counts):
            for c in counts:
                eng.sem_inc(c, 1)

        block = ctx.enter_context(nc.Block())

        ctx_v = ctx_in[0].rearrange("(n t p) d -> n p t d", t=CHUNK // P, p=P)

        ew1_v = ew1.rearrange("e (t p) h -> e p t h", p=P)
        ew2_v = ew2.rearrange("e (t p) d -> e p t d", p=P)

        @block.sync
        def _(sp):
            for i, w in ((1, xWk), (2, xWv)):
                sp.dma_start(wn[:, i], w.rearrange("(t p) i -> p t i", p=P)).then_inc(s_w, 16)
            for s in range(2):
                sp.dma_start(cs[:, s], ctx_v[s]).then_inc(s_ctx[s], 16)

            def restack(c, o):
                sp.wait_ge(s_kd[o], 4 * (c + 1))
                sp.wait_ge(s_kb[o], 4 * (c + 1))
                for j in range(P // DH):
                    h = o * (P // DH) + j
                    sp.dma_start(kst[0:ROWS, h, bass.ts(c, SUPER)],
                                 kp[DH * j:DH * (j + 1), o, :, :]).then_inc(s_rs[o], 16)

            def next_chunks(c):
                for s in range(2):
                    sp.wait_ge(s_tr[s], c + 1)
                    sp.dma_start(cs[:, s], ctx_v[bass.ds(2 * c + 2 + s, 1)][0]).then_inc(s_ctx[s], 16)

            sp.wait_ge(s_qp, 6)
            for h in range(H):
                o, j = divmod(h, P // DH)
                sp.dma_start(qst[0:ROWS, h, :], qp[DH * j:DH * (j + 1), o, :, :]).then_inc(s_qst, 16)
                if h == 1:
                    next_chunks(0)
            for o in range(DT):
                restack(0, o)
            with sp.Fori(1, NSUPER - 1) as c:
                next_chunks(c)
                for o in range(DT):
                    restack(c, o)
            for o in range(DT):
                restack(NSUPER - 1, o)
            sp.wait_ge(s_rs[0], 16 * NSUPER * (P // DH))
            sp.wait_ge(s_rs[1], 16 * NSUPER * (P // DH))
            sp.wait_ge(s_woz, 1)
            prm = [(rA[:, i], gens[i].rearrange("(t p) d -> p t d", p=P)) for i in range(NROT)]
            prm += [(aWq_s[:, :, :], aWq.rearrange("(t p) d -> p t d", p=P)),
                    (aWl_s[:, :, :], aWl.rearrange("(t p) d -> p t d", p=P)),
                    (aWk_s[:, :], aWk), (aWv_s[:, :], aWv),
                    (abw_s[:, :, :], abw.rearrange("(t p) d -> p t d", p=P)),
                    (gw_s[:, :, :], gw.rearrange("(t p) d -> p t d", p=P)),
                    (eb1_n[:, :], eb1.rearrange("e (t p) -> (e t) p", p=P)), (eb2_s[:, :], eb2),
                    (abv_b[:, :], bcast(abv)), (abo_b[:, :], bcast(abo)), (lng_b[:, :], bcast(lng)),
                    (lnb_b[:, :], bcast(lnb)), (abb_b[:, :], bcast(abb)), (gb_b[:, :], bcast(gb)),
                    (gcw_b[:, :, :], bcast(gcw.rearrange("(a d) one -> a (d one)", a=2)))]
            wo_v = aWo.rearrange("(g j d) n -> j d g n", j=GROUP, d=DH)
            prm += [(woP[VW * j:VW * j + DH, :, :], wo_v[j]) for j in range(GROUP)]
            assert len(prm) == NPRM
            for to, fro in prm:
                sp.dma_start(to, fro).then_inc(s_prm, 16)

            def expert(e, s):
                sp.dma_start(ew1r[:, s], ew1_v[bass.ds(e, 1)][0]).then_inc(s_ew1[s], 16)
                sp.dma_start(ew2r[:, s], ew2_v[bass.ds(e, 1)][0]).then_inc(s_ew2[s], 16)

            for g in range(NG):
                sp.wait_ge(s_z, 1 + ZSTEPS * (g + 1))
                for h in range(GROUP * g, GROUP * (g + 1)):
                    for t in range(TT):
                        row = DH * h + t * (P // DH)
                        sp.dma_start(z[row % P:row % P + P // DH, row // P, :],
                                     zq[:, t, h * DH:(h + 1) * DH]).then_inc(s_zz, 16)
            sp.wait_ge(s_pv[1], 1 + NG * NIT * (UN // 2))
            for s in range(SLOTS):
                expert(s, s)
            for r in range(1, E // SLOTS):
                for s in range(SLOTS):
                    sp.wait_ge(s_eo[s], 1 + r)
                    expert(r * SLOTS + s, s)
            for t in range(TT):
                sp.wait_ge(s_out, t + 1)
                sp.dma_start(out[0, t * P:(t + 1) * P], moe2[:, t]).then_inc(s_fin, 16)
            sp.wait_ge(s_fin, 16 * TT)

        @block.gpsimd
        def _(pool):
            for m in (identf, identb):
                pool.memset(m[:, :], 0.0).then_inc(s_c, 1)
            pool.wait_ge(s_c, 2)
            for m in (identf, identb):
                pool.affine_select(out=m[:, :], in_=m[:, :], compare_op=ALU.not_equal, fill=1.0, base=0,
                                   pattern=[[-1, P]], channel_multiplier=1).then_inc(s_c, 1)
            pool.memset(mhalf[:, :], -0.5).then_inc(s_c, 1)
            pool.wait_ge(s_c, 5)
            pool.memset(hmask[:, :], DH ** -0.5).then_inc(s_hm, 1)
            pool.memset(tri[:, :, :], 1.0).then_inc(s_hm, 1)
            pool.wait_ge(s_hm, 2)
            pool.affine_select(out=hmask[:, :], in_=hmask[:, :], compare_op=ALU.is_ge, fill=0.0, base=0,
                               pattern=[[-DH, P // DH]], channel_multiplier=1).then_inc(s_hm, 1)
            pool.affine_select(out=tri[:, :, :], in_=tri[:, :, :], compare_op=ALU.is_gt, fill=0.0, base=0,
                               pattern=[[1, E], [-1, E]], channel_multiplier=0).then_inc(s_hm, 1)
            pool.wait_ge(s_hm, 4)
            pool.affine_select(out=hmask[:, :], in_=hmask[:, :], compare_op=ALU.is_ge, fill=0.0, base=DH - 1,
                               pattern=[[DH, P // DH]], channel_multiplier=-1).then_inc(s_hm, 1)

            def power(n):
                pool.wait_ge(s_lnv, n + 1)
                pool.tensor_tensor(rstd[:, :], vare[:, :], mhalf[:, :], ALU.pow).then_inc(s_lnr, 1)

            power(0)
            pool.memset(zero[:, :], 0.0).then_inc(s_c, 1)
            pool.wait_ge(s_v, NCTX // CHUNK)
            pool.wait_ge(s_rs[0], 16 * NSUPER * (P // DH))
            pool.wait_ge(s_rs[1], 16 * NSUPER * (P // DH))
            pool.memset(vr[:, :, :, :], 0.0).then_inc(s_c, 1)
            pool.wait_ge(s_c, 7)
            pool.memset(vr[:, :, :, DH:DH + 1], 1.0).then_inc(s_c, 1)
            pool.memset(woP[:, :, :], 0.0).then_inc(s_woz, 1)
            pool.wait_ge(s_c, 8)

            def ring(g, it):
                for u in range(UN):
                    s, k = u % 2, (g * NIT + it) * (UN // 2) + u // 2
                    pool.wait_ge(s_pv[s], 1 + k)
                    src = val[:, bass.ds(it * UN + u, 1), bass.ds(g * GROUP * DH, GROUP * DH)]
                    pool.tensor_copy(vr[:, s, :, 0:DH], src[:, 0].rearrange("p (j d) -> p j d", d=DH))\
                        .then_inc(s_vr[s], 1)

            with pool.Fori(0, NG) as g:
                with pool.Fori(0, NIT) as it:
                    ring(g, it)
            pool.wait_ge(s_pv[1], 1 + NG * NIT * (UN // 2))
            pool.memset(vp[:, :, :, :], 0.0).then_inc(s_woz, 1)
            for n in range(1, 5):
                power(n)

        @block.scalar
        def _(act):
            free_at_first(act, *s_p, s_zt, s_hc[2], s_hc[3])
            act.dma_start(x_sb[:, :, :], x[0].rearrange("(t p) d -> p t d", p=P)).then_inc(s_in, 16)
            act.dma_start(wn[:, 0], xWq.rearrange("(t p) i -> p t i", p=P)).then_inc(s_w, 16)
            for c, b in ((bq_c, xbq), (bk_c, xbk), (abq_c, abq), (abk_c, abk), (abl_c, abl)):
                act.dma_start(c[:, :], b.rearrange("(t p) -> p t", p=c.shape[0])).then_inc(s_b, 16)
            act.dma_start(gcb_b[:, :], bcast(gcb)).then_inc(s_b, 16)
            act.wait_ge(s_ob, 1)
            one = onesb[0:MROWS, :]
            act.dma_start(kst[ROWS:ROWS + MROWS, :, :].rearrange("p a b -> p (a b)"),
                          bass.AP(one.tensor, one.offset, [list(one.ap[0]), [0, H * NCTX // NT], list(one.ap[1])]))\
               .then_inc(s_ones, 16)
            for i, to in enumerate((wT[:, 0], wT[:, 1], wqT)):
                act.wait_ge(s_wt, i + 1)
                act.activation(to.rearrange("p k o -> p (k o)") if i < 2 else to[:, :, :].rearrange("p k o -> p (k o)"),
                               psum[:, 1 + i], ACT.Copy).then_inc(s_wtc, 1)

            def half(s, c):
                act.wait_ge(s_tr[s], c + 1)
                if not first(c):
                    act.wait_ge(s_kmm[1] if s == 0 else s_vmm[1], 2 * c - 1 if s == 0 else c)
                act.activation(cT[:, s, 0], psum[:, 0], ACT.Copy).then_inc(s_ta[s], 1)

            def values(s, c):
                act.wait_ge(s_vmm[s], c + 1)
                act.activation(val[:, bass.ds(4 * (2 * c + s), 4), :].rearrange("p a b -> p (a b)"),
                               psum[:, 4:6, :].rearrange("p a b -> p (a b)"), ACT.Copy).then_inc(s_v, 1)

            def keys(s, c):
                n = 2 * c + s
                sl = slice(s * CHUNK, (s + 1) * CHUNK)
                for o in range(DT):
                    act.wait_ge(s_kmm[o], n + 1)
                    if not first(c):
                        act.wait_ge(s_rs[o], 16 * (P // DH) * c)
                    act.activation(kp[:, o, 0, sl], psum[:, 2 + o], ACT.Identity, bias=bk_c[:, o:o + 1])\
                       .then_inc(s_k1[o], 1)
                for o in range(DT):
                    act.wait_ge(s_r1[o], n + 1)
                    act.activation(kp[:, o, 1, sl], r1[:, o], ACT.Copy).then_inc(s_k2[o], 1)
                for o in range(DT):
                    act.wait_ge(s_k1[o], n + 1)
                    part = kp[:, o, 0, sl]
                    act.activation(kp[:, o, 3:6:2, sl],
                                   bass.AP(part.tensor, part.offset, [list(part.ap[0]), [0, 2], list(part.ap[1])]),
                                   ACT.Copy).then_inc(s_kb[o], 2)

            def superchunk(c):
                half(1, c)
                values(0, c)
                keys(0, c)
                half(0, c + 1)
                keys(1, c)
                values(1, c)

            act.wait_ge(s_b, 16 * 6)
            half(0, 0)
            act.wait_ge(s_xt, 1)
            act.activation(xT[:, :, :], psum[:, 7].rearrange("p (k t) -> p k t", k=DT), ACT.Copy).then_inc(s_xtc, 1)
            for o in range(DT):
                act.wait_ge(s_q, o + 1)
                act.activation(qp[:, o, 0, :], psum[:, 4 + o, 0:NT], ACT.Identity,
                               bias=bq_c[:, o:o + 1]).then_inc(s_q1, 1)
            act.wait_ge(s_q1, 2)
            act.activation(qp[:, :, 1, :], qp[:, :, 0, :], ACT.Copy).then_inc(s_qp, 1)
            act.activation(qp[:, :, 2, :], qp[:, :, 0, :], ACT.Copy).then_inc(s_qp, 1)
            act.wait_ge(s_qr, 2)
            act.activation(qp[:, :, 3, :], q1[:, :, :], ACT.Copy).then_inc(s_q2, 1)
            act.wait_ge(s_q2, 1)
            act.activation(qp[:, :, 4, :], qp[:, :, 3, :], ACT.Copy).then_inc(s_qp, 1)
            superchunk(0)
            act.wait_ge(s_qst, 16 * H)
            act.wait_ge(s_ones, 16)
            with act.Fori(1, NSUPER - 1) as c:
                superchunk(c)
            half(1, NSUPER - 1)
            values(0, NSUPER - 1)
            keys(0, NSUPER - 1)
            keys(1, NSUPER - 1)
            values(1, NSUPER - 1)

            for o in range(DT):
                act.wait_ge(s_rs[o], 16 * NSUPER * (P // DH))
            for c, b in ((bv_b, xbv), (gam_b, xgamma), (bet_b, xbeta)):
                act.dma_start(c[:, :], bcast(b)).then_inc(s_par, 16)

            def m_rows(g):
                act.wait_ge(s_mr, g + 1)
                act.activation(qst[ROWS:ROWS + MROWS, bass.ds(g * GROUP, GROUP), :]
                               .rearrange("p a b -> p (a b)"),
                               psum[ROWS:ROWS + MROWS, 5:7, :].rearrange("p a b -> p (a b)"),
                               ACT.Copy).then_inc(s_mq, 1)

            def exps(g, it):
                for u in range(UN):
                    s, k = u % 2, (g * NIT + it) * (UN // 2) + u // 2
                    act.wait_ge(s_s[s], k + 1)
                    act.wait_ge(s_pv[s], 1 + k)
                    act.activation(pr[:, s], ps_s[s].rearrange("p a b -> p (a b)"), ACT.Exp).then_inc(s_p[s], 1)

            def sums(g):
                act.wait_ge(s_pv[1], 1 + (g + 1) * NIT * (UN // 2))
                act.wait_ge(s_zp, 1 + g)
                act.activation(zt[:, :], ps_pv, ACT.Copy).then_inc(s_zt, 1)

            m_rows(0)
            with act.Fori(0, NG - 1) as g:
                with act.Fori(0, NIT) as it:
                    exps(g, it)
                sums(g)
                m_rows(g + 1)
            with act.Fori(0, NIT) as it:
                exps(NG - 1, it)
            sums(NG - 1)

            def rbank(i):
                return psum[:, i].rearrange("p (k d) -> p k d", k=DT)

            def rot_copy(u):
                act.wait_ge(s_rt, u + 1)
                if u >= NROT:
                    act.wait_ge(s_rm, u - NROT + 1)
                act.activation(rT[:, rot_of(u)], rbank(4), ACT.Copy).then_inc(s_rtc, 1)

            for u in range(EARLY):
                rot_copy(u)

            act.wait_ge(s_t2, 1)
            act.activation(xT2[:, :, :], rbank(0), ACT.Copy).then_inc(s_t2c, 1)
            act.wait_ge(s_al, 1)
            act.activation(latT[:, :], psum[0:LAT, 2, 0:NT], ACT.Identity, bias=abl_c[:, 0:1]).then_inc(s_alc, 1)
            act.wait_ge(s_ak, 1)
            for o in range(DT):
                act.activation(kT[:, o], psum[:, 3, o * NT:(o + 1) * NT], ACT.Identity, bias=abk_c[:, o:o + 1])\
                   .then_inc(s_akc, 1)
            rot_copy(EARLY)
            def sums_out(g):
                act.wait_ge(s_az, g + 1)
                act.activation(zT[:, g], psum[:, 5, 0:NT], ACT.Copy).then_inc(s_azc, 1)

            for n in range(STEPS):
                act.wait_ge(s_anm, n + 1)
                if n >= 2:
                    act.wait_ge(s_at, n - 1)
                for j in range(2):
                    act.activation(pa[:, n % 2, j], psum[:, n % 2, j * NT:(j + 1) * NT], ACT.Exp,
                                   bias=nm[:, 2 * n + j:2 * n + j + 1],
                                   accum_out=rs[:, 2 * n + j:2 * n + j + 1]).then_inc(s_ae, 1)
                for u in product_at(2 * n, 1, LAST_AT):
                    rot_copy(u)
                if n % GROUP == 2 and n > 2:
                    sums_out(n // GROUP - 1)
                if n >= 1 and (n - 1) % 2 == 0:
                    att_copy(act.activation, n - 1, act, s_at, s_atA)
                for u in product_at(2 * n + 1, 1, LAST_AT):
                    rot_copy(u)
            sums_out(NG - 1)

            act.wait_ge(s_e1t, 1)
            act.activation(eb1_c[:, :], psum[:, 4, 0:E * HT], ACT.Copy).then_inc(s_e1c, 1)
            act.wait_ge(s_t3, 1)
            act.activation(xgT[:, :, :], rbank(0), ACT.Copy).then_inc(s_t3c, 1)
            act.wait_ge(s_lm, 1)
            for t in range(TT):
                act.activation(ex[:, t], lg[:, t], ACT.Exp, bias=lm[:, t:t + 1]).then_inc(s_ex, 1)
            act.wait_ge(s_abi, 2)
            act.activation(abel[:, :, :], abin[:, :, :], ACT.Gelu).then_inc(s_abel, 1)
            act.wait_ge(s_wt8, 1)
            act.activation(wdT[:, :], psum[0:E, 3, 0:NT], ACT.Copy).then_inc(s_wt8c, 1)

            def hidden(r, s):
                act.wait_ge(s_h[s], r + 1)
                act.wait_ge(s_eo[(s + 2) % SLOTS], 1 + r + (s >= 2))
                for t in range(HT):
                    act.activation(hT[:, s % 2, t], psum[:, 4 + 2 * (s % 2) + t // 2, (t % 2) * NT:(t % 2 + 1) * NT],
                                   ACT.Gelu, bias=eb1_c[:, bass.ds((r * SLOTS + s) * HT + t, 1)]).then_inc(s_hc[s], 1)

            with act.Fori(0, E // SLOTS) as r:
                for s in range(SLOTS):
                    hidden(r, s)
            for t in range(TT):
                act.wait_ge(s_mt, t + 1)
                act.activation(moeT[:, :, t * P:(t + 1) * P], psum[:, 4 + t, 0:DT * P].rearrange("p (k d) -> p k d", k=DT),
                               ACT.Copy).then_inc(s_mtc, 1)
            for t in range(TT):
                act.wait_ge(s_gz, t + 1)
                act.activation(gs[:, 2, t:t + 1], gs[:, 1, t:t + 1], ACT.Tanh, scale=0.5).then_inc(s_ge, 1)

        @block.vector
        def _(dve):
            ch = Chain(dve, s_dve)

            def moments(src):
                for t in range(TT):
                    ch.step(dve.bn_stats(stats[:, t], src[:, t]))
                for t in range(TT):
                    ch.step(dve.bn_aggr(mv[:, t], stats[:, t]))
                dve.tensor_scalar(vare[:, :], mv[:, :, 1], EPS, None, ALU.add).then_inc(s_lnv, 1)

            def norm(n, dst, src, meanwhile=lambda: None):
                moments(src)
                meanwhile()
                dve.wait_ge(s_lnr, n + 1)
                for t in range(TT):
                    last = dve.tensor_scalar(dst[:, t], src[:, t], mv[:, t, 0:1], rstd[:, t:t + 1],
                                             ALU.subtract, ALU.mult)
                    last.then_inc(s_ln, 1)

            def norm_affine(n, dst, src, tmp, gamma, beta, meanwhile=lambda: None):
                moments(src)
                for t in range(TT):
                    ch.step(dve.scalar_tensor_tensor(tmp[:, t], src[:, t], mv[:, t, 0:1], gamma,
                                                     ALU.subtract, ALU.mult))
                meanwhile()
                dve.wait_ge(s_lnr, n + 1)
                for t in range(TT):
                    dve.scalar_tensor_tensor(dst[:, t], tmp[:, t], rstd[:, t:t + 1], beta(t), ALU.mult, ALU.add)\
                       .then_inc(s_ln, 1)

            free_at_first(dve, *s_mx, s_z, *[s_acc] * TT)
            dve.memset(onesb[:, :], 1.0).then_inc(s_ob, 1)
            dve.wait_ge(s_in, 16)
            norm(0, dec, x_sb)
            dve.wait_ge(s_b, 16 * 6)

            def half(s, c):
                dve.wait_ge(s_tr[s], c + 1)
                if not first(c):
                    dve.wait_ge(s_kmm[1] if s == 0 else s_vmm[1], 2 * c - 1 if s == 0 else c)
                dve.tensor_copy(cT[:, s, 1], psum[:, 1]).then_inc(s_tv[s], 1)

            def remainder(s, c, o):
                n = 2 * c + s
                dve.wait_ge(s_k1[o], n + 1)
                if not first(c) or s > 0:
                    dve.wait_ge(s_kd[o], 2 * n)
                dve.scalar_tensor_tensor(r1[:, o], psum[:, 2 + o], bk_c[:, o:o + 1],
                                         kp[:, o, 0, s * CHUNK:(s + 1) * CHUNK],
                                         ALU.add, ALU.subtract).then_inc(s_r1[o], 1)

            def last_parts(s, c, o):
                sl = slice(s * CHUNK, (s + 1) * CHUNK)
                dve.wait_ge(s_k2[o], 2 * c + s + 1)
                dve.wait_ge(s_r1[o], 2 * c + s + 1)
                dve.tensor_tensor(kp[:, o, 2, sl], r1[:, o], kp[:, o, 1, sl], ALU.subtract).then_inc(s_kd[o], 1)
                dve.tensor_copy(kp[:, o, 4, sl], kp[:, o, 1, sl]).then_inc(s_kd[o], 1)

            def first_maxima(c, pairs):
                for v in [v for pair in pairs for v in (2 * pair, 2 * pair + 1)]:
                    b, uses, before = (max_bank(v) if c is LAST_SUPER else (1 + v % 2, 8, v // 2))
                    j, t, half = v // 4, v // 2 % 2, v % 2
                    dve.wait_ge(s_mmm[b], (8 * (NSUPER - 1) * (b > 0) if c is LAST_SUPER else uses * c) + before + 1)
                    dve.tensor_reduce(mx0[:, j, t, bass.ds(2 * c + half, 1)], psum[:, MB[b]], AX.X, ALU.max)\
                        .then_inc(s_mx[b], 1)

            def project(s, c, m):
                if s == 0:
                    m(range(0, 2))
                remainder(s, c, 0)
                m(range(4 * s + 2 * (s == 0), 4 * s + 2 * (s == 0) + 1))
                remainder(s, c, 1)
                m(range(4 * s + 2 * (s == 0) + 1, 4 * s + 2 * (s == 0) + 2))
                last_parts(s, c, 0)
                if s == 1:
                    m(range(6, 7))
                last_parts(s, c, 1)
                if s == 1:
                    m(range(7, 8))

            def no_maxima(pairs):
                pass

            half(0, 0)
            for o in range(DT):
                dve.wait_ge(s_q1, o + 1)
                dve.scalar_tensor_tensor(q1[:, o, :], psum[:, 4 + o, 0:NT], bq_c[:, o:o + 1],
                                         qp[:, o, 0, :], ALU.add, ALU.subtract).then_inc(s_qr, 1)
            dve.wait_ge(s_q2, 1)
            dve.wait_ge(s_qr, 2)
            dve.tensor_tensor(qp[:, :, 5, :], q1[:, :, :], qp[:, :, 3, :], ALU.subtract).then_inc(s_qp, 3)
            half(1, 0)
            project(0, 0, no_maxima)
            half(0, 1)
            project(1, 0, no_maxima)
            with dve.Fori(1, NSUPER - 1) as c:
                def before(pairs):
                    first_maxima(c - 1, pairs)
                half(1, c)
                project(0, c, before)
                half(0, c + 1)
                project(1, c, before)

            def before_last(pairs):
                first_maxima(NSUPER - 2, pairs)
            half(1, NSUPER - 1)
            project(0, NSUPER - 1, before_last)
            project(1, NSUPER - 1, before_last)
            first_maxima(LAST_SUPER, range(8))
            for b in range(3):
                dve.wait_ge(s_mx[b], MX0[b])
            dve.tensor_reduce(negm[:, :, :].rearrange("p j t -> p (j t)"),
                              mx0[:, :, :, :].rearrange("p j t k -> p (j t) k"),
                              AX.X, ALU.max, negate=True).then_inc(s_mxh, 1)

            def maxima(body, it):
                for v in range(16):
                    b, uses, before = max_bank(v)
                    dve.wait_ge(s_mmm[b], FIRST_USES[b] + body * uses + before + 1)
                    if v == 0:
                        dve.wait_ge(s_mxh, 1 + body)
                    dve.tensor_reduce(mxs[:, v // 8, v % 8:v % 8 + 1], psum[:, MB[b]], AX.X, ALU.max)\
                        .then_inc(s_mx[b], 1)
                for b in range(3):
                    dve.wait_ge(s_mx[b], MX0[b] + (body + 1) * MAX_USES[b])
                dve.tensor_reduce(negm[:, bass.ds(it, 1), :].rearrange("p a t -> p (a t)"), mxs[:, :, :],
                                  AX.X, ALU.max, negate=True).then_inc(s_mxh, 1)

            def m_parts(g):
                nm = negm[:, :, :].rearrange("p j t -> p (j t)")
                dve.wait_ge(s_mxh, 1 + g * NIT)
                dve.tensor_copy(mp[:, :, 0], nm).then_inc(s_mp, 1)
                dve.wait_ge(s_mp, 5 * g + 1)
                dve.tensor_tensor(mrem[:, 0], nm, mp[:, :, 0], ALU.subtract).then_inc(s_mp, 1)
                dve.wait_ge(s_mp, 5 * g + 2)
                dve.tensor_copy(mp[:, :, 1], mrem[:, 0]).then_inc(s_mp, 1)
                dve.wait_ge(s_mp, 5 * g + 3)
                dve.tensor_tensor(mrem[:, 1], mrem[:, 0], mp[:, :, 1], ALU.subtract).then_inc(s_mp, 1)
                dve.wait_ge(s_mp, 5 * g + 4)
                dve.tensor_copy(mp[:, :, 2], mrem[:, 1]).then_inc(s_mp, 1)

            def divide(g):
                dve.wait_ge(s_zp, 1 + g + 1)
                zp = psum[:, 7, 0:TT * P].rearrange("p (t j c) -> p t j c", t=TT, c=VW)
                dve.reciprocal(rden[:, :, :], zp[:, :, :, DH]).then_inc(s_z, 1)
                dve.wait_ge(s_z, 1 + ZSTEPS * g + 1)
                cols = bass.ds(g * GROUP * DH, GROUP * DH)
                for t in range(TT):
                    dve.tensor_tensor(zq[:, t, cols].rearrange("p (j d) -> p j d", d=DH),
                                      zp[:, t, :, 0:DH], spread(rden[:, t], DH), ALU.mult).then_inc(s_z, 1)
                dve.wait_ge(s_z, 1 + ZSTEPS * g + 1 + TT)
                for t in range(TT):
                    dve.tensor_tensor(zq[:, t, cols], zq[:, t, cols], bv_b[:, cols], ALU.add).then_inc(s_z, 1)

            m_parts(0)
            dve.wait_ge(s_par, 16 * 3)
            with dve.Fori(0, NG - 1) as g:
                with dve.Fori(0, NIT) as it:
                    maxima(NIT * g + it, it)
                m_parts(g + 1)
                divide(g)
            dve.wait_ge(s_prm, 16 * NPRM)
            dve.tensor_scalar(rA[:, :, :, :], rA[:, :, :, :], 2.0 ** -SQUARINGS, None, ALU.mult).then_inc(s_rA, 1)
            for t in range(TT):
                ch.step(dve.tensor_tensor(x_sb[:, t], x_sb[:, t], bet_b[:, :], ALU.add))
            divide(NG - 1)

            def flat(a):
                return a.rearrange("p k d -> p (k d)")

            def rot_combine(u):
                m, i, b = u // NROT, rot_of(u), 6 + u % 2
                y, a2, a, l, r = (flat(w[:, i]) for w in (rY, rA2, rA, rL, rU))
                dve.wait_ge(s_rm, u + 1)
                if u >= NROT:
                    dve.wait_ge(s_rv, u - NROT + 1)
                if m == 0:
                    ch.step(dve.tensor_copy(a2, psum[:, b]))
                    dve.scalar_tensor_tensor(r, a2, T1 / T2, a, ALU.mult, ALU.add).then_inc(s_rv, 1)
                elif m == 1:
                    ch.step(dve.tensor_scalar(y, psum[:, b], T2, None, ALU.mult))
                    ch.step(dve.scalar_tensor_tensor(l, a, T4, y, ALU.mult, ALU.add))
                    ch.step(dve.scalar_tensor_tensor(l, a2, T3, l, ALU.mult, ALU.add))
                    ch.step(dve.scalar_tensor_tensor(r, a2, T5, y, ALU.mult, ALU.add))
                    ch.step(dve.scalar_tensor_tensor(y, y, T6, a, ALU.mult, ALU.add))
                    dve.scalar_tensor_tensor(y, a2, 0.5, y, ALU.mult, ALU.add).then_inc(s_rv, 1)
                elif m == 2:
                    dve.tensor_tensor(y, y, psum[:, b], ALU.add).then_inc(s_rv, 1)
                elif u < NROT * (3 + SQUARINGS):
                    dve.scalar_tensor_tensor(y, y, 2.0, psum[:, b], ALU.mult, ALU.add).then_inc(s_rv, 1)
                else:
                    dve.wait_ge(s_rv, u)
                    ch.step(dve.tensor_tensor(flat(rY[:, 0]), flat(rY[:, 0]), flat(rY[:, right_of(u)]), ALU.add))
                    dve.tensor_tensor(flat(rY[:, 0]), flat(rY[:, 0]), psum[:, b], ALU.add).then_inc(s_rv, 1)

            for u in range(EARLY - 3):
                rot_combine(u)
            dve.wait_ge(s_zz, 16 * TT * H)
            for t in range(TT):
                ch.step(dve.tensor_tensor(z[:, t], z[:, t], dec[:, t], ALU.add))
            norm_affine(1, x_sb, z, z, gam_b[:, :], lambda t: x_sb[:, t], lambda: rot_combine(EARLY - 3))
            dve.wait_ge(s_ln, 4)

            norm(2, n2, x_sb, lambda: rot_combine(EARLY - 2))
            dve.wait_ge(s_hm, 5)
            dve.wait_ge(s_aq, 1)
            for o in range(DT):
                dve.tensor_scalar(qf[:, o], psum[:, 1, o * NT:(o + 1) * NT], abq_c[:, o:o + 1], None, ALU.add)\
                   .then_inc(s_qf, 1)
            dve.wait_ge(s_qf, 2)
            for h in range(H):
                o, j = divmod(h, P // DH)
                dve.tensor_scalar(qm[:, h], qf[:, o], hmask[:, j:j + 1], None, ALU.mult).then_inc(s_qm, 1)
            dve.wait_ge(s_av, 1)
            dve.wait_ge(s_woz, 2)
            for t in range(TT):
                dve.tensor_tensor(vp[:, t, :, 0:DH], psum[:, 2, t * D:(t + 1) * D].rearrange("p (h d) -> p h d", d=DH),
                                  abv_b[:, :].rearrange("p (h d) -> p h d", d=DH), ALU.add).then_inc(s_avc, 1)

            def att_max(n):
                dve.wait_ge(s_as, n + 1)
                dve.tensor_reduce(nm[:, 2 * n:2 * n + 2], psum[:, n % 2, :].rearrange("p (j k) -> p j k", j=2),
                                  AX.X, ALU.max, negate=True).then_inc(s_anm, 1)

            att_max(0)
            for n in range(STEPS):
                if n + 1 < STEPS:
                    att_max(n + 1)
                for u in product_at(2 * n, -1, LAST_AT + 1):
                    rot_combine(u)
                dve.wait_ge(s_ae, 2 * n + 2)
                dve.reciprocal(rr[:, 2 * n:2 * n + 2], rs[:, 2 * n:2 * n + 2]).then_inc(s_ar, 1)
                dve.wait_ge(s_ar, n + 1)
                for j in range(2):
                    dve.tensor_scalar(pa[:, n % 2, j], pa[:, n % 2, j], rr[:, 2 * n + j:2 * n + j + 1], None, ALU.mult)\
                       .then_inc(s_an, 1)
                if n >= 1 and (n - 1) % 2 == 1:
                    att_copy(dve.tensor_copy, n - 1, dve, s_at, s_atV)
                for u in product_at(2 * n + 1, -1, LAST_AT + 1):
                    rot_combine(u)
            att_copy(dve.tensor_copy, STEPS - 1, dve, s_at, s_atV)
            for t in range(TT):
                ch.step(dve.tensor_tensor(x_sb[:, t], x_sb[:, t], abo_b[:, :], ALU.add))
            for t in range(TT):
                dve.wait_ge(s_ao, t + 1)
                ch.step(dve.tensor_tensor(x_sb[:, t], x_sb[:, t], psum[:, 7 - t, 0:D], ALU.add))

            norm(3, xp, x_sb)
            dve.wait_ge(s_ln, 8)
            norm_affine(4, xg, xp, n2, lng_b[:, :], lambda t: lnb_b[:, :], lambda: [
                ch.step(dve.tensor_tensor(x_sb[:, t], x_sb[:, t], xp[:, t], ALU.add)) for t in range(TT)])
            dve.wait_ge(s_lg, 1)
            for t in range(TT):
                ch.step(dve.tensor_tensor(lg[:, t], psum[:, 2, t * E:(t + 1) * E], gb_b[:, :], ALU.add))
            dve.tensor_reduce(lm[:, :], lg[:, :, :], AX.X, ALU.max, negate=True).then_inc(s_lm, 1)
            dve.wait_ge(s_ab, 1)
            for t in range(TT):
                dve.tensor_tensor(abin[:, t], psum[:, 1, t * D:(t + 1) * D], abb_b[:, :], ALU.add).then_inc(s_abi, 1)
            for t in range(TT):
                row = lg[:, t]
                other = bass.AP(row.tensor, row.offset, [list(row.ap[0]), [0, E], list(row.ap[1])])
                ch.step(dve.tensor_tensor(cgt[:, t], other, spread(row, E), ALU.is_gt))
                ch.step(dve.tensor_tensor(ceq[:, t], other, spread(row, E), ALU.is_equal))
                ch.step(dve.tensor_tensor(ceq[:, t], ceq[:, t], tri[:, :, :], ALU.mult))
                ch.step(dve.tensor_tensor(cgt[:, t], cgt[:, t], ceq[:, t], ALU.add))
            ch.step(dve.tensor_reduce(rank[:, :, :], cgt[:, :, :, :], AX.X, ALU.add))
            ch.step(dve.tensor_scalar(rank[:, :, :], rank[:, :, :], 2.0, None, ALU.is_lt))
            dve.wait_ge(s_ex, 2)
            ch.step(dve.tensor_tensor(wd[:, :, :], ex[:, :, :], rank[:, :, :], ALU.mult))
            ch.step(dve.tensor_reduce(wsum[:, :], wd[:, :, :], AX.X, ALU.add))
            ch.step(dve.reciprocal(wsum[:, :], wsum[:, :]))
            for t in range(TT):
                dve.tensor_scalar(wd[:, t], wd[:, t], wsum[:, t:t + 1], None, ALU.mult).then_inc(s_wd, 1)
            dve.wait_ge(s_abel, 1)
            for t in range(TT):
                ch.step(dve.tensor_tensor(x_sb[:, t], x_sb[:, t], abel[:, t], ALU.add))
                ch.step(dve.tensor_tensor_reduce(junk[:, :], abel[:, t], gcw_b[:, 0], 1.0, 0.0, ALU.mult, ALU.add,
                                                 gs[:, 0, t:t + 1]))
            ch.step(dve.tensor_scalar(gs[:, 0], gs[:, 0], gcb_b[:, 0:1], None, ALU.add))
            dve.wait_ge(s_b2, 1)
            dve.tensor_copy(moe[:, :, :].rearrange("p t d -> p (t d)"), psum[:, 0]).then_inc(s_acc, 1)
            dve.wait_ge(s_wd, 2)
            with dve.Fori(0, E // SLOTS) as r:
                for s in range(SLOTS):
                    dve.wait_ge(s_eo[s], 1 + r + 1)
                    for t in range(TT):
                        dve.wait_ge(s_acc, TT + (r * SLOTS + s) * TT + t + (1 if t == 0 else 0))
                        dve.scalar_tensor_tensor(moe[:, t], psum[:, 2 + s % 2, t * D:(t + 1) * D],
                                                 wd[:, t, bass.ds(r * SLOTS + s, 1)], moe[:, t],
                                                 ALU.mult, ALU.add).then_inc(s_acc, 1)
            for t in range(TT):
                dve.wait_ge(s_rot, t + 1)
                dve.wait_ge(s_acc, TT + 1 + E * TT)
                ch.step(dve.tensor_tensor(moe2[:, t], psum[:, 6 + t, 0:D], moe[:, t], ALU.add))
                ch.step(dve.tensor_tensor_reduce(junk[:, :], moe2[:, t], gcw_b[:, 1], 1.0, 0.0, ALU.mult, ALU.add,
                                                 gs[:, 3, t:t + 1]))
                dve.tensor_tensor(gs[:, 1, t:t + 1], gs[:, 0, t:t + 1], gs[:, 3, t:t + 1], ALU.add).then_inc(s_gz, 1)
                ch.step(dve.tensor_tensor(moe2[:, t], moe2[:, t], abel[:, t], ALU.subtract))
            for t in range(TT):
                dve.wait_ge(s_ge, t + 1)
                ch.step(dve.tensor_scalar(gs[:, 4, t:t + 1], gs[:, 2, t:t + 1], 0.5, 0.5, ALU.mult, ALU.add))
                dve.scalar_tensor_tensor(moe2[:, t], moe2[:, t], gs[:, 4, t:t + 1], x_sb[:, t], ALU.mult, ALU.add)\
                   .then_inc(s_out, 1)

        @block.tensor
        def _(pe):
            def transpose4(dst, src):
                for k in range(2):
                    for t in range(2):
                        last = pe.transpose(dst[:, k * 256 + t * P:k * 256 + (t + 1) * P],
                                            src[:, t, k * P:(k + 1) * P], identf[:, :])
                return last

            free_at_first(pe, *s_pv, s_zp, *s_eo)
            pe.wait_ge(s_c, 4)
            pe.wait_ge(s_w, 16 * 3)
            for bank, i in ((1, 1), (2, 2), (3, 0)):
                transpose4(psum[:, bank], wn[:, i]).then_inc(s_wt, 1)

            def turn(s, c):
                pe.wait_ge(s_ctx[s], 16 * (c + 1))
                if s > 0 or not first(c):
                    pe.wait_ge(s_ta[1 - s], c + s)
                    pe.wait_ge(s_tv[1 - s], c + s)
                for k in range(DT):
                    for t in range(CHUNK // P):
                        last = pe.transpose(psum[:, k, t * P:(t + 1) * P],
                                            cs[:, s, t, k * P:(k + 1) * P], identf[:, :])
                last.then_inc(s_tr[s], 1)

            def project_keys(s, c, o):
                if s > 0 or not first(c):
                    pe.wait_ge(s_r1[o], 2 * c + s)
                for k in range(DT):
                    last = pe.matmul(psum[:, 2 + o], wT[:, 0, k, o * P:(o + 1) * P], cT[:, s, k],
                                     start=(k == 0), stop=(k == DT - 1))
                last.then_inc(s_kmm[o], 1)

            def project_values(s, c, half):
                if half == 0 and (s > 0 or not first(c)):
                    pe.wait_ge(s_v, 2 * c + s)
                for t in (2 * half, 2 * half + 1):
                    for k in range(DT):
                        last = pe.matmul(psum[:, 4 + t // 2, (t % 2) * D:(t % 2 + 1) * D],
                                         cT[:, s, k, t * P:(t + 1) * P], wT[:, 1, k, :],
                                         start=(k == 0), stop=(k == DT - 1))
                if half == 1:
                    last.then_inc(s_vmm[s], 1)

            def project(s, c, maxima):
                pe.wait_ge(s_ta[s], c + 1)
                pe.wait_ge(s_tv[s], c + 1)
                steps = [(project_values, 0), (project_values, 1), (project_keys, 0), (project_keys, 1)]
                for i, (step, which) in enumerate(steps if s == 0 else steps[2:] + steps[:2]):
                    step(s, c, which)
                    maxima(4 * s + i)

            def first_maxima(c, pair):
                for v in (2 * pair, 2 * pair + 1):
                    j, t, half = v // 4, v // 2 % 2, v % 2
                    if c is LAST_SUPER:
                        b, _, before = max_bank(v)
                        before += 8 * (NSUPER - 1) * (b > 0)
                    else:
                        b, before = 1 + v % 2, 8 * c + v // 2
                    pe.wait_ge(s_mx[b], 1 + before)
                    pe.matmul(psum[:, MB[b]], qst[0:ROWS, j, t * P:(t + 1) * P],
                              kst[0:ROWS, j, bass.ts(2 * c + half, 512)], start=True, stop=True)\
                      .then_inc(s_mmm[b], 1)

            def no_maxima(pair):
                pass

            pe.wait_ge(s_wtc, 3)
            turn(0, 0)
            pe.wait_ge(s_ln, 2)
            transpose4(psum[:, 7], dec).then_inc(s_xt, 1)
            pe.wait_ge(s_xtc, 1)
            for o in range(DT):
                for k in range(DT):
                    last = pe.matmul(psum[:, 4 + o, 0:NT], wqT[:, k, o * P:(o + 1) * P], xT[:, k],
                                     start=(k == 0), stop=(k == DT - 1))
                last.then_inc(s_q, 1)
            turn(1, 0)
            pe.wait_ge(s_q1, 2)
            pe.wait_ge(s_qr, 2)
            project(0, 0, no_maxima)
            turn(0, 1)
            project(1, 0, no_maxima)
            pe.wait_ge(s_qst, 16 * H)

            def restacked(c):
                for o in range(DT):
                    pe.wait_ge(s_rs[o], 16 * c * (P // DH))

            with pe.Fori(1, NSUPER - 1) as c:
                def before(pair):
                    if pair == 0:
                        pe.wait_ge(s_rs[0], 16 * c * (P // DH))
                    first_maxima(c - 1, pair)
                turn(1, c)
                project(0, c, before)
                turn(0, c + 1)
                project(1, c, before)

            def before_last(pair):
                if pair == 0:
                    pe.wait_ge(s_rs[0], 16 * (NSUPER - 1) * (P // DH))
                first_maxima(NSUPER - 2, pair)
            turn(1, NSUPER - 1)
            project(0, NSUPER - 1, before_last)
            project(1, NSUPER - 1, before_last)

            def maxima(body, h, vs):
                for v in vs:
                    b, uses, before = max_bank(v)
                    pe.wait_ge(s_mx[b], MX0[b] + body * uses + before)
                    pe.matmul(psum[:, MB[b]], qst[0:ROWS, bass.ds(h, 1), (v // 8) * P:(v // 8 + 1) * P][:, 0],
                              kst[0:ROWS, bass.ds(h, 1), (v % 8) * 512:(v % 8 + 1) * 512][:, 0],
                              start=True, stop=True).then_inc(s_mmm[b], 1)

            def m_rows(g):
                pe.wait_ge(s_mp, 5 * (g + 1))
                for j in range(GROUP):
                    for t in range(TT):
                        col = j * NT + t * P
                        last = pe.matmul(psum[ROWS:ROWS + MROWS, 5 + col // 512, col % 512:col % 512 + P],
                                         mp[:, j * TT + t, :], identb[:, :], start=True, stop=True)
                last.then_inc(s_mr, 1)

            def scores(g, kt, s, k):
                pe.wait_ge(s_p[s], 1 + k)
                for j in range(GROUP):
                    last = pe.matmul(ps_s[s][:, j // 2, (j % 2) * NT:(j % 2 + 1) * NT],
                                     kst[0:ROWS + MROWS, bass.ds(g * GROUP + j, 1), bass.ts(kt, P)][:, 0],
                                     qst[0:ROWS + MROWS, bass.ds(g * GROUP + j, 1), :][:, 0],
                                     start=True, stop=True)
                last.then_inc(s_s[s], 1)

            def weigh(s, k, last_of_group):
                pe.wait_ge(s_p[s], 1 + k + 1)
                pe.wait_ge(s_vr[s], k + 1)
                for j in range(GROUP):
                    last = pe.matmul(psum[VW * j:VW * (j + 1), 4, 0:NT], vr[:, s, j, :],
                                     pr[:, s, j * NT:(j + 1) * NT], start=False, stop=last_of_group,
                                     skip_group_check=True, tile_position=(0, VW * j))
                last.then_inc(s_pv[s], 1)

            def open_sums(g):
                pe.wait_ge(s_zt, 1 + g)
                for j in range(GROUP):
                    pe.matmul(psum[VW * j:VW * (j + 1), 4, 0:NT], zero[:, 0:VW], zero[:, :],
                              start=True, stop=False, skip_group_check=True, tile_position=(0, VW * j))

            def body(g, it, last, following):
                for u in range(UN):
                    e = (g * NIT + it) * UN + u
                    k, k1 = (g * NIT + it) * (UN // 2) + u // 2, (g * NIT + it) * (UN // 2) + (u + 1) // 2
                    if not (last and u == UN - 1):
                        scores(g, it * UN + u + 1, (u + 1) % 2, k1)
                    if following:
                        maxima(NIT * g + it, (g + 1) * GROUP + it, (2 * u, 2 * u + 1))
                    weigh(u % 2, k, last and u == UN - 1)

            def close_sums(g):
                pe.wait_ge(s_zt, 1 + g + 1)
                for t in range(TT):
                    last = pe.transpose(psum[:, 7, t * P:(t + 1) * P], zt[:, t * P:(t + 1) * P], identf[:, :])
                last.then_inc(s_zp, 1)

            def group(g, following):
                pe.wait_ge(s_mq, g + 1)
                pe.wait_ge(s_z, 1 + ZSTEPS * g)
                open_sums(g)
                scores(g, 0, 0, g * NIT * (UN // 2))
                with pe.Fori(0, NIT - 1) as it:
                    body(g, it, False, following)
                body(g, NIT - 1, True, following)
                if following:
                    m_rows(g + 1)
                close_sums(g)

            pe.wait_ge(s_ones, 16)
            restacked(NSUPER)
            pe.wait_ge(s_c, 8)
            pe.wait_ge(s_v, NCTX // CHUNK)
            for pair in range(8):
                first_maxima(LAST_SUPER, pair)
            m_rows(0)
            with pe.Fori(0, NG - 1) as g:
                group(g, True)
            group(NG - 1, False)

            def rot_trans(u):
                m, i = u // NROT, rot_of(u)
                pe.wait_ge(s_rv if u >= NROT else s_rA, 1 if u < NROT else u if right_of(u) != i else u - NROT + 1)
                if u >= 1:
                    pe.wait_ge(s_rtc, u)
                src = (rA, rA2, rL)[m][:, i] if m < 3 else rY[:, i]
                for k in range(DT):
                    for t in range(DT):
                        last = pe.transpose(psum[:, 4, k * D + t * P:k * D + (t + 1) * P],
                                            src[:, t, k * P:(k + 1) * P], identf[:, :])
                last.then_inc(s_rt, 1)

            def rot_mul(u):
                m, i = u // NROT, rot_of(u)
                right = (rA, rU, rU)[m][:, i] if m < 3 else rY[:, right_of(u)]
                pe.wait_ge(s_rtc, u + 1)
                if u >= 2:
                    pe.wait_ge(s_rv, u - 1)
                for o in range(DT):
                    for k in range(DT):
                        last = pe.matmul(psum[:, 6 + u % 2, o * D:(o + 1) * D], rT[:, i, k, o * P:(o + 1) * P],
                                         right[:, k], start=(k == 0), stop=(k == DT - 1))
                last.then_inc(s_rm, 1)

            pe.wait_ge(s_z, 1 + ZSTEPS * NG)
            for u in range(EARLY):
                rot_trans(u)
                if u > 0:
                    rot_mul(u - 1)

            def product(bank, cols, left, right, ks, width=P):
                for k in ks:
                    last = pe.matmul(psum[0:width, bank, cols], left(k), right(k),
                                     start=(k == ks[0]), stop=(k == ks[-1]))
                return last

            ks = list(range(DT))
            half = [slice(0, NT), slice(NT, 2 * NT)]
            tile = [slice(t * P, (t + 1) * P) for t in range(4)]
            pe.wait_ge(s_ln, 6)
            transpose4(psum[:, 0], n2).then_inc(s_t2, 1)
            rot_mul(EARLY - 1)
            pe.wait_ge(s_t2c, 1)
            product(2, slice(0, NT), lambda k: aWl_s[:, k, :], lambda k: xT2[:, k], ks, LAT).then_inc(s_al, 1)
            for o in range(DT):
                last = product(1, half[o], lambda k: aWq_s[:, k, tile[o]], lambda k: xT2[:, k], ks)
            last.then_inc(s_aq, 1)
            pe.wait_ge(s_alc, 1)
            for o in range(DT):
                last = product(3, half[o], lambda k: aWk_s[:, tile[o]], lambda k: latT[:, :], [0])
            last.then_inc(s_ak, 1)
            for t in range(TT):
                last = product(2, half[t], lambda k: latT[:, tile[t]], lambda k: aWv_s[:, :], [0])
            last.then_inc(s_av, 1)
            rot_trans(EARLY)
            rot_trans(EARLY + 1)
            pe.wait_ge(s_akc, 2)

            def att_scores(n):
                h, t = 2 * (n // 2), n % 2
                pe.wait_ge(s_qm, h + 2)
                if n == 1:
                    pe.wait_ge(s_qf, 2)
                if n >= 2:
                    pe.wait_ge(s_ae, 2 * (n - 1))
                for j in range(2):
                    last = product(n % 2, half[j], lambda k: qm[:, h + j, tile[t]],
                                   lambda k: kT[:, (h + j) // (P // DH)], [0])
                last.then_inc(s_as, 1)

            def att_turn(n):
                pe.wait_ge(s_an, 2 * n + 2)
                if n == 0:
                    pe.wait_ge(s_avc, 2)
                if n >= 2:
                    pe.wait_ge(s_atV if n % 2 else s_atA, 2 * (n // 2))
                for j in range(2):
                    for k in range(TT):
                        last = pe.transpose(psum[:, 2 + n % 2, tile[2 * j + k]], pa[:, n % 2, j, tile[k]], identf[:, :])
                last.then_inc(s_at, 1)

            def rot_slot(k):
                for u in product_at(k, 0, LAST_AT):
                    rot_mul(u)
                for u in product_at(k, 2, LAST_AT - 1):
                    rot_trans(u)

            def att_weigh(g):
                steps = (g + 1) * GROUP
                pe.wait_ge(s_atA, steps)
                pe.wait_ge(s_atV, steps)
                if g > 0:
                    pe.wait_ge(s_azc, g)
                for k in range(TT):
                    for j in range(GROUP):
                        last = pe.matmul(psum[VW * j:VW * (j + 1), 5, 0:NT], vp[:, k, GROUP * g + j, :],
                                         pT[:, k, GROUP * g + j, :], start=(k == 0), stop=(k == TT - 1),
                                         tile_position=(0, VW * j))
                last.then_inc(s_az, 1)

            def att_out(g):
                pe.wait_ge(s_azc, g + 1)
                for t in range(TT):
                    last = pe.matmul(psum[:, 7 - t, 0:D], zT[:, g, tile[t]], woP[:, g], start=(g == 0),
                                     stop=(g == NG - 1))
                    if g == NG - 1:
                        last.then_inc(s_ao, 1)

            att_scores(0)
            att_scores(1)
            for n in range(STEPS):
                rot_slot(2 * n)
                att_turn(n)
                if n + 2 < STEPS:
                    att_scores(n + 2)
                rot_slot(2 * n + 1)
                if n % GROUP == 1 and n > 1:
                    att_weigh(n // GROUP - 1)
            pe.wait_ge(s_rv, RPROD)
            for g in range(NG - 1):
                att_out(g)
            att_weigh(NG - 1)
            att_out(NG - 1)

            def hidden(r, s):
                pe.wait_ge(s_ew1[s], 16 * (r + 1))
                if s < 2:
                    pe.wait_ge(s_hc[s + 2], 1 + HT * r)
                else:
                    pe.wait_ge(s_hc[s - 2], HT * (r + 1))
                for t in range(HT):
                    last = product(4 + 2 * (s % 2) + t // 2, half[t % 2], lambda k: ew1r[:, s, k, tile[t]],
                                   lambda k: xgT[:, k], ks)
                last.then_inc(s_h[s], 1)

            def expert_out(r, s):
                pe.wait_ge(s_ew2[s], 16 * (r + 1))
                pe.wait_ge(s_hc[s], (s >= 2) + HT * (r + 1))
                pe.wait_ge(s_acc, 1 + (r * SLOTS + s) * TT)
                for t in range(TT):
                    last = product(2 + s % 2, half[t], lambda k: hT[:, s % 2, k, tile[t]],
                                   lambda k: ew2r[:, s, k], list(range(HT)))
                last.then_inc(s_eo[s], 1)

            pe.transpose(psum[:, 4, 0:E * HT], eb1_n[:, :], identf[0:E * HT, 0:E * HT]).then_inc(s_e1t, 1)
            pe.wait_ge(s_ln, 10)
            transpose4(psum[:, 0], xg).then_inc(s_t3, 1)
            pe.wait_ge(s_t3c, 1)
            for t in range(TT):
                last = product(2, slice(t * E, (t + 1) * E), lambda k: xgT[:, k, tile[t]], lambda k: gw_s[:, k], ks)
            last.then_inc(s_lg, 1)
            for t in range(TT):
                last = product(1, half[t], lambda k: xgT[:, k, tile[t]], lambda k: abw_s[:, k], ks)
            last.then_inc(s_ab, 1)
            pe.wait_ge(s_e1c, 1)
            hidden(0, 0)
            pe.wait_ge(s_wd, 2)
            for t in range(TT):
                last = pe.transpose(psum[0:E, 3, tile[t]], wd[:, t], identf[:, :])
            last.then_inc(s_wt8, 1)
            pe.wait_ge(s_wt8c, 1)
            for t in range(TT):
                last = product(0, half[t], lambda k: wdT[:, tile[t]], lambda k: eb2_s[:, :], [0])
            last.then_inc(s_b2, 1)
            pe.wait_ge(s_lm, 1)

            def experts(r, last):
                for s in range(SLOTS):
                    if not (last and s == SLOTS - 1):
                        hidden(r + (s + 1) // SLOTS, (s + 1) % SLOTS)
                    expert_out(r, s)

            def rotated(t):
                pe.wait_ge(s_mtc, t + 1)
                product(6 + t, half[0], lambda k: moeT[:, k, tile[t]], lambda k: rY[:, 0, k], ks).then_inc(s_rot, 1)

            with pe.Fori(0, E // SLOTS - 1) as r:
                experts(r, False)
            experts(E // SLOTS - 1, True)
            for t in range(TT):
                pe.wait_ge(s_acc, TT + 1 + (E - 1) * TT + t + 1)
                for k in range(DT):
                    last = pe.transpose(psum[:, 4 + t, k * P:(k + 1) * P],
                                        moe[:, t, k * P:(k + 1) * P], identf[:, :])
                last.then_inc(s_mt, 1)
                if t > 0:
                    rotated(t - 1)
            rotated(TT - 1)


ZSTEPS = 1 + 2 * TT
STEPS = 2 * H // 2
RPROD = NROT * (3 + SQUARINGS) + NROT - 1
EARLY = 7
LAST_AT = RPROD - EARLY + 1
NPRM = 22


def rot_of(u):
    return u % NROT if u < NROT * (3 + SQUARINGS) else 0


def right_of(u):
    return u % NROT if u < NROT * (3 + SQUARINGS) else u - NROT * (3 + SQUARINGS) + 1


def product_at(k, lead, last):
    u = EARLY + lead + k
    return [u] if u < RPROD - 2 else [RPROD - 2] if k == last else [RPROD - 1] if k == last + 3 else []


MAX_BANK = [v % 3 for v in range(15)] + [1]
MAX_USES = [MAX_BANK.count(b) for b in range(3)]


LAST_SUPER = NSUPER - 1
FIRST_USES = [8 * (NSUPER - 1) * (b > 0) + MAX_USES[b] for b in range(3)]
MX0 = [1 + n for n in FIRST_USES]


def first(c):
    return isinstance(c, int) and c == 0


def max_bank(v):
    b = MAX_BANK[v]
    return b, MAX_USES[b], MAX_BANK[:v].count(b)


_INS = ['x', 'ctx_1024', 'L0_xattn_Wq', 'L0_xattn_bq', 'L0_xattn_Wk', 'L0_xattn_bk', 'L0_xattn_Wv', 'L0_xattn_bv',
        'L0_xattn_gamma', 'L0_xattn_beta', 'L0_attn_Wq', 'L0_attn_bq', 'L0_attn_Wl', 'L0_attn_bl', 'L0_attn_Wk',
        'L0_attn_bk', 'L0_attn_Wv', 'L0_attn_bv', 'L0_attn_Wo', 'L0_attn_bo', 'L0_ffn_ln_gamma', 'L0_ffn_ln_beta',
        'L0_ffn_abel_w', 'L0_ffn_abel_b', 'L0_ffn_moe_gate_w', 'L0_ffn_moe_gate_b', 'L0_ffn_ew1', 'L0_ffn_eb1',
        'L0_ffn_ew2', 'L0_ffn_eb2', 'L0_ffn_gens', 'L0_ffn_gc_w', 'L0_ffn_gc_b']
_OUTS = [((1, NT, D), 'float32')]


def kernel(**inputs):
    import numpy as _np
    import concourse.bacc as _bacc
    from concourse import mybir as _mybir
    from concourse.bass_utils import run_bass_kernel_spmd as _run

    nc = _bacc.Bacc("TRN2", target_bir_lowering=False, num_devices=1, dynamic_dma_scratch_size=1024)
    arrays, args = {}, []
    for name in _INS:
        a = _np.ascontiguousarray(inputs[name])
        arrays[f"in_{name}_dram"] = a
        args.append(nc.dram_tensor(f"in_{name}_dram", a.shape, _mybir.dt.from_np(a.dtype), kind="ExternalInput").ap())
    for i, (shape, dtype) in enumerate(_OUTS):
        dt = _mybir.dt.from_np(_np.dtype(dtype))
        args.append(nc.dram_tensor(f"out_{i}_dram", shape, dt, kind="ExternalOutput").ap())
    build(nc, *args)
    r = _run(nc, [arrays], core_ids=[0])
    return r.results[0]["out_0_dram"]
```

```python
import concourse.bass as bass
from concourse import mybir
from contextlib import ExitStack

FP32 = mybir.dt.float32
BF16 = mybir.dt.bfloat16
ALU = mybir.AluOpType
ACT = mybir.ActivationFunctionType
AX = mybir.AxisListType

P = 128
D = 256
NT = 256
NCTX = 4096
H = 16
DH = D // H
DT = D // P
TT = NT // P
EPS = 1e-5

KPART = (0, 1, 2, 0, 1, 0)
QPART = (0, 0, 0, 1, 1, 2)
NB = len(KPART)
ROWS = NB * DH
MROWS = 3

CHUNK = 512
SUPER = 2 * CHUNK
NSUPER = NCTX // SUPER
GROUP = 4
NG = H // GROUP
KT = NCTX // P
PRS = 4
UN = 8
NIT = KT // UN
LAT = D // 4
E = 8
HID = 2 * D
HT = HID // P
QTILE = 5 * KT // 8
SLOTS = 4
NROT = 3
ROT = NROT * DT * D
SQUARINGS = 6
T1, T2, T3 = 4.980119205559973e-3, 1.992047682223989e-2, 7.665265321119147e-2
T4, T5, T6 = 8.765009801785554e-1, 1.225521150112075e-1, 2.974307204847627
VW = 32


def bcast(ap, n=P):
    return bass.AP(ap.tensor, ap.offset, [[0, n]] + [list(x) for x in ap.ap])


def spread(ap, n):
    return bass.AP(ap.tensor, ap.offset, [list(x) for x in ap.ap] + [[0, n]])




class Chain:

    def __init__(self, eng, sem):
        self.eng, self.sem, self.n = eng, sem, 0

    def step(self, ins):
        self.n += 1
        ins.then_inc(self.sem, 1)
        self.eng.wait_ge(self.sem, self.n)


def build(nc, x, ctx_in, xWq, xbq, xWk, xbk, xWv, xbv, xgamma, xbeta,
          aWq, abq, aWl, abl, aWk, abk, aWv, abv, aWo, abo,
          lng, lnb, abw, abb, gw, gb, ew1, eb1, ew2, eb2, gens, gcw, gcb, out):
    ctx = ExitStack()
    proj = ExitStack()
    with ctx:
        ctx.enter_context(nc.allow_non_contiguous_dma("biases laid along partitions"))

        def sem(name):
            return ctx.enter_context(nc.semaphore(name))

        def sems(name, n):
            return [sem(f"{name}{i}") for i in range(n)]

        def sb(name, shape, dt=FP32, where=ctx):
            return where.enter_context(nc.sbuf_tensor(name, shape, dt))

        x_sb = sb("x_sb", [P, TT, D])
        dec = sb("dec", [P, TT, D])
        identf = sb("identf", [P, P])
        identb = sb("identb", [P, P], BF16)
        stats = sb("stats", [P, TT, 6])
        mv = sb("mv", [P, TT, 2])
        vare = sb("vare", [P, TT])
        mhalf = sb("mhalf", [P, TT])
        rstd = sb("rstd", [P, TT])
        bq_c = sb("bq_c", [P, DT])
        bk_c = sb("bk_c", [P, DT])
        hmask = sb("hmask", [P, P // DH])
        tri = sb("tri", [P, E, E])
        abq_c = sb("abq_c", [P, DT])
        abk_c = sb("abk_c", [P, DT])
        abl_c = sb("abl_c", [LAT, 1])
        gcb_b = sb("gcb_b", [P, 1])
        zero = sb("zero", [P, NT], BF16)
        onesb = sb("onesb", [P, P], BF16)
        first_exp = sb("first_exp", [P, 1])
        mx0 = sb("mx0", [P, GROUP, TT, NCTX // 512])
        mxs = sb("mxs", [P, TT, NCTX // 512])
        negm = sb("negm", [P, GROUP, TT])
        mrem = sb("mrem", [P, GROUP * TT])
        mp = sb("mp", [P, GROUP * TT, MROWS], BF16)
        xattn = ExitStack()
        kst = sb("kst", [P, H, NCTX], BF16, xattn)
        with ExitStack() as early:
            wn = sb("wn", [P, 3, DT, D], FP32, early)
            wqT = sb("wqT", [P, DT, D], FP32, early)
        qst = sb("qst", [P, H, NT], BF16, xattn)
        with ExitStack() as early:
            sb("values_before", [P, QTILE, D], FP32, early)
            qp = sb("qp", [P, DT, NB, NT], BF16, early)
            q1 = sb("q1", [P, DT, NT], FP32, early)
            xT = sb("xT", [P, DT, NT], FP32, early)
        val = sb("val", [P, KT, D], FP32, xattn)
        kp = sb("kp", [P, DT, NB, SUPER], BF16, proj)
        kp_even = kst[:, 0:DT * NB, (NSUPER - 1) * SUPER:NSUPER * SUPER].rearrange("p (o b) n -> p o b n", b=NB)
        cs = sb("cs", [P, 2, CHUNK // P, D], FP32, proj)
        cT = sb("cT", [P, 2, DT, CHUNK], FP32, proj)
        wT = sb("wT", [P, 2, DT, D], FP32, proj)
        r1 = sb("r1", [P, DT, CHUNK], FP32, proj)
        proj.close()
        attn = ExitStack()
        zq = sb("zq", [P, TT, D], FP32, attn)
        z = sb("z", [P, TT, D], FP32, attn)
        bv_b = sb("bv_b", [P, D], FP32, attn)
        gam_b = sb("gam_b", [P, D], FP32, attn)
        bet_b = sb("bet_b", [P, D], FP32, attn)
        pr = sb("pr", [P, PRS, GROUP * NT], FP32, attn)
        vr = sb("vr", [P, 2, GROUP, VW], FP32, attn)
        zt = sb("zt", [P, NT], FP32, attn)
        rden = sb("rden", [P, TT, GROUP], FP32, attn)
        aWq_s = sb("aWq_s", [P, DT, D], FP32, attn)
        aWl_s = sb("aWl_s", [P, DT, LAT], FP32, attn)
        aWk_s = sb("aWk_s", [LAT, D], FP32, attn)
        aWv_s = sb("aWv_s", [LAT, D], FP32, attn)
        woP = sb("woP", [P, NG, D], FP32, attn)
        abv_b = sb("abv_b", [P, D], FP32, attn)
        abo_b = sb("abo_b", [P, D], FP32, attn)
        lng_b = sb("lng_b", [P, D], FP32, attn)
        lnb_b = sb("lnb_b", [P, D], FP32, attn)
        abb_b = sb("abb_b", [P, D], FP32, attn)
        gb_b = sb("gb_b", [P, E], FP32, attn)
        abw_s = sb("abw_s", [P, DT, D], FP32, attn)
        gw_s = sb("gw_s", [P, DT, E], FP32, attn)
        eb1_n = sb("eb1_n", [E * HT, P], FP32, attn)
        eb2_s = sb("eb2_s", [E, D], FP32, attn)
        rA = sb("rA", [P, NROT, DT, D], FP32, attn)
        attn.close()
        xattn.close()
        late = ExitStack()
        rT = sb("rT", [P, NROT, DT, D], FP32, late)
        rA2 = sb("rA2", [P, NROT, DT, D], FP32, late)
        rU = sb("rU", [P, NROT, DT, D], FP32, late)
        rY = sb("rY", [P, NROT, DT, D], FP32, late)
        rL = sb("rL", [P, NROT, DT, D], FP32, late)
        ew1r = sb("ew1r", [P, SLOTS, DT, HID], FP32, late)
        ew2r = sb("ew2r", [P, SLOTS, HT, D], FP32, late)
        n2 = sb("n2", [P, TT, D], FP32, late)
        xT2 = sb("xT2", [P, DT, NT], FP32, late)
        qf = sb("qf", [P, DT, NT], FP32, late)
        qm = sb("qm", [P, H, NT], FP32, late)
        latT = sb("latT", [LAT, NT], FP32, late)
        kT = sb("kT", [P, DT, NT], FP32, late)
        vp = sb("vp", [P, TT, H, VW], FP32, late)
        nm = sb("nm", [P, 2 * H], FP32, late)
        rs = sb("rs", [P, 2 * H], FP32, late)
        rr = sb("rr", [P, 2 * H], FP32, late)
        pa = sb("pa", [P, 2, 2, NT], FP32, late)
        pT = sb("pT", [P, TT, H, NT], FP32, late)
        zT = sb("zT", [P, NG, NT], FP32, late)
        xp = sb("xp", [P, TT, D], FP32, late)
        xg = sb("xg", [P, TT, D], FP32, late)
        xgT = sb("xgT", [P, DT, NT], FP32, late)
        abel = sb("abel", [P, TT, D], FP32, late)
        abin = sb("abin", [P, TT, D], FP32, late)
        lg = sb("lg", [P, TT, E], FP32, late)
        lm = sb("lm", [P, TT], FP32, late)
        ex = sb("ex", [P, TT, E], FP32, late)
        cgt = sb("cgt", [P, TT, E, E], FP32, late)
        ceq = sb("ceq", [P, TT, E, E], FP32, late)
        rank = sb("rank", [P, TT, E], FP32, late)
        wsum = sb("wsum", [P, TT], FP32, late)
        wd = sb("wd", [P, TT, E], FP32, late)
        wdT = sb("wdT", [E, NT], FP32, late)
        eb1_c = sb("eb1_c", [P, E * HT], FP32, late)
        hT = sb("hT", [P, 2, HT, NT], FP32, late)
        moe = sb("moe", [P, TT, D], FP32, late)
        moeT = sb("moeT", [P, DT, NT], FP32, late)
        moe2 = sb("moe2", [P, TT, D], FP32, late)
        prod = sb("prod", [P, D], FP32, late)
        gs = sb("gs", [P, 5, TT], FP32, late)
        gcw_b = sb("gcw_b", [P, 2, D], FP32, late)
        late.close()

        psum = ctx.enter_context(nc.psum_tensor("psum", [P, 8, 512], FP32))
        ps_s = [psum[:, 0:2, :], psum[:, 2:4, :]]
        ps_pv = psum[:, 4, 0:NT]
        MB = (5, 6, 7)

        s_c = sem("s_c")
        s_in = sem("s_in")
        s_w = sem("s_w")
        s_b = sem("s_b")
        s_ob = sem("s_ob")
        s_par = sem("s_par")
        s_ones = sem("s_ones")
        s_ctx = sems("s_ctx", 2)
        s_wt = sem("s_wt")
        s_wtc = sem("s_wtc")
        s_lnv = sem("s_lnv")
        s_lnr = sem("s_lnr")
        s_ln = sem("s_ln")
        s_xt = sem("s_xt")
        s_xtc = sem("s_xtc")
        s_q = sem("s_q")
        s_q1 = sem("s_q1")
        s_qr = sem("s_qr")
        s_q2 = sem("s_q2")
        s_qp = sem("s_qp")
        s_qst = sem("s_qst")
        s_tr = sems("s_tr", 2)
        s_ta = sems("s_ta", 2)
        s_tv = sems("s_tv", 2)
        s_kmm = sems("s_kmm", 2)
        s_k1 = sems("s_k1", 2)
        s_r1 = sems("s_r1", 2)
        s_k2 = sems("s_k2", 2)
        s_kd = sems("s_kd", 2)
        s_kb = sems("s_kb", 2)
        s_vmm = sems("s_vmm", 2)
        s_v = sem("s_v")
        s_rg = sem("s_rg")
        s_rs = sems("s_rs", 2)
        s_rh = sem("s_rh")
        s_mmm = sems("s_mmm", 3)
        s_mx = sems("s_mx", 3)
        s_mxh = sem("s_mxh")
        s_mp = sem("s_mp")
        s_mr = sem("s_mr")
        s_mq = sem("s_mq")
        s_mw = sem("s_mw")
        s_s = sems("s_s", 2)
        s_p = sems("s_p", 2)
        s_pv = sems("s_pv", 2)
        s_vr = sems("s_vr", 2)
        s_zt = sem("s_zt")
        s_zp = sem("s_zp")
        s_z = sem("s_z")
        s_prm = sem("s_prm")
        s_hm = sem("s_hm")
        s_woz = sem("s_woz")
        s_ew1 = sems("s_ew1", SLOTS)
        s_ew2 = sems("s_ew2", SLOTS)
        s_t2 = sem("s_t2")
        s_t2c = sem("s_t2c")
        s_aq = sem("s_aq")
        s_al = sem("s_al")
        s_alc = sem("s_alc")
        s_ak = sem("s_ak")
        s_akc = sem("s_akc")
        s_av = sem("s_av")
        s_avc = sem("s_avc")
        s_qf = sem("s_qf")
        s_qm = sem("s_qm")
        s_as = sem("s_as")
        s_anm = sem("s_anm")
        s_ae = sem("s_ae")
        s_ar = sem("s_ar")
        s_an = sem("s_an")
        s_at = sem("s_at")
        s_atA = sem("s_atA")
        s_atV = sem("s_atV")
        s_az = sem("s_az")
        s_azc = sem("s_azc")
        s_ao = sem("s_ao")
        s_rA = sem("s_rA")
        s_rt = sem("s_rt")
        s_rtc = sem("s_rtc")
        s_rm = sem("s_rm")
        s_rv = sem("s_rv")
        s_t3 = sem("s_t3")
        s_t3c = sem("s_t3c")
        s_ab = sem("s_ab")
        s_abi = sem("s_abi")
        s_lg = sem("s_lg")
        s_lm = sem("s_lm")
        s_abel = sem("s_abel")
        s_ex = sem("s_ex")
        s_wd = sem("s_wd")
        s_wt8 = sem("s_wt8")
        s_wt8c = sem("s_wt8c")
        s_b2 = sem("s_b2")
        s_acc = sem("s_acc")
        s_e1t = sem("s_e1t")
        s_e1c = sem("s_e1c")
        s_h = sems("s_h", 4)
        s_hc = sems("s_hc", 4)
        s_eo = sems("s_eo", 4)
        s_mt = sem("s_mt")
        s_mtc = sem("s_mtc")
        s_rot = sem("s_rot")
        s_gcw = sem("s_gcw")
        s_gz = sem("s_gz")
        s_ge = sem("s_ge")
        s_zz = sem("s_zz")
        s_dve = sem("s_dve")
        s_out = sem("s_out")
        s_fin = sem("s_fin")

        def att_copy(copy, n, eng, wait, done):
            eng.wait_ge(wait, n + 1)
            h, t = 2 * (n // 2), n % 2
            to = pT[:, :, h:h + 2, t * P:(t + 1) * P].rearrange("p k j q -> p j k q")
            fro = psum[:, 2 + n % 2, :].rearrange("p (j k q) -> p j k q", j=2, k=TT)
            args = (ACT.Copy,) if done is s_atA else ()
            for j in range(2):
                copy(to[:, j], fro[:, j], *args).then_inc(done, 1)

        def keys_stacked(eng, c, halves=range(DT)):
            for o in halves:
                if o == 0:
                    eng.wait_ge(s_rg, 1 + 16 * GROUP * c)
                if o == 0 and c is NSUPER:
                    eng.wait_ge(s_rh, 16 * GROUP)
                eng.wait_ge(s_rs[o], 1 + 16 * (P // DH - (GROUP if o == 0 else 0)) * c)

        def free_at_first(eng, *counts):
            for c in counts:
                eng.sem_inc(c, 1)

        block = ctx.enter_context(nc.Block())

        ctx_v = ctx_in[0].rearrange("(n t p) d -> n p t d", t=CHUNK // P, p=P)

        ew1_v = ew1.rearrange("e (t p) h -> e p t h", p=P)
        ew2_v = ew2.rearrange("e (t p) d -> e p t d", p=P)

        @block.sync
        def _(sp):
            for i, w in ((1, xWk), (2, xWv)):
                sp.dma_start(wn[:, i], w.rearrange("(t p) i -> p t i", p=P)).then_inc(s_w, 16)
            for s in range(2):
                sp.dma_start(cs[:, s], ctx_v[s]).then_inc(s_ctx[s], 16)

            def restack(c, o, buf):
                sp.wait_ge(s_kd[o], 4 * (c + 1))
                sp.wait_ge(s_kb[o], 4 * (c + 1))
                for j in range(P // DH):
                    h = o * (P // DH) + j
                    if h < GROUP and c is LAST_SUPER:
                        sp.dma_start(kst[0:ROWS, h, NCTX - CHUNK:NCTX],
                                     buf[DH * h:DH * (h + 1), 0, :, CHUNK:SUPER]).then_inc(s_rg, 16)
                        continue
                    sp.dma_start(kst[0:ROWS, h, bass.ts(c, SUPER)],
                                 buf[DH * j:DH * (j + 1), o]).then_inc(s_rg if h < GROUP else s_rs[o], 16)

            sp.wait_ge(s_qp, 6)
            for h in range(H):
                o, j = divmod(h, P // DH)
                sp.dma_start(qst[0:ROWS, h, :], qp[DH * j:DH * (j + 1), o, :, :]).then_inc(s_qst, 16)
            for o in range(DT):
                restack(0, o, kp_even)
            with sp.Fori(0, NSUPER // 2 - 1) as i:
                for c, buf in ((2 * i + 1, kp), (2 * i + 2, kp_even)):
                    for o in range(DT):
                        restack(c, o, buf)
            keys_stacked(sp, NSUPER - 1)
            sp.wait_ge(s_ones, 16)
            sp.dma_start(kst[ROWS:ROWS + MROWS, :, LAST_SUPER * SUPER:], kst[ROWS:ROWS + MROWS, :, 0:SUPER])\
              .then_inc(s_ones, 16)
            sp.wait_ge(s_kd[0], 4 * NSUPER - 2)
            sp.wait_ge(s_kb[0], 4 * NSUPER - 2)
            for h in range(GROUP):
                sp.dma_start(kst[0:ROWS, h, LAST_SUPER * SUPER:LAST_SUPER * SUPER + CHUNK],
                             kp[DH * h:DH * (h + 1), 0, :, 0:CHUNK]).then_inc(s_rh, 16)
            for o in range(DT):
                restack(LAST_SUPER, o, kp)
            keys_stacked(sp, NSUPER)
            sp.wait_ge(s_woz, 1)
            prm = [(rA[:, i], gens[i].rearrange("(t p) d -> p t d", p=P)) for i in range(NROT)]
            prm += [(aWq_s[:, :, :], aWq.rearrange("(t p) d -> p t d", p=P)),
                    (aWl_s[:, :, :], aWl.rearrange("(t p) d -> p t d", p=P)),
                    (aWk_s[:, :], aWk), (aWv_s[:, :], aWv),
                    (abw_s[:, :, :], abw.rearrange("(t p) d -> p t d", p=P)),
                    (gw_s[:, :, :], gw.rearrange("(t p) d -> p t d", p=P)),
                    (eb1_n[:, :], eb1.rearrange("e (t p) -> (e t) p", p=P)), (eb2_s[:, :], eb2),
                    (abv_b[:, :], bcast(abv)), (abo_b[:, :], bcast(abo)), (lng_b[:, :], bcast(lng)),
                    (lnb_b[:, :], bcast(lnb)), (abb_b[:, :], bcast(abb)), (gb_b[:, :], bcast(gb))]
            wo_v = aWo.rearrange("(g j d) n -> j d g n", j=GROUP, d=DH)
            prm += [(woP[VW * j:VW * j + DH, :, :], wo_v[j]) for j in range(GROUP)]
            assert len(prm) == NPRM
            for to, fro in prm:
                sp.dma_start(to, fro).then_inc(s_prm, 16)

            def expert(e, s):
                sp.dma_start(ew1r[:, s], ew1_v[bass.ds(e, 1)][0]).then_inc(s_ew1[s], 16)
                sp.dma_start(ew2r[:, s], ew2_v[bass.ds(e, 1)][0]).then_inc(s_ew2[s], 16)

            for g in range(NG):
                sp.wait_ge(s_z, 1 + ZSTEPS * (g + 1))
                for h in range(GROUP * g, GROUP * (g + 1)):
                    for t in range(TT):
                        row = DH * h + t * (P // DH)
                        sp.dma_start(z[row % P:row % P + P // DH, row // P, :],
                                     zq[:, t, h * DH:(h + 1) * DH]).then_inc(s_zz, 16)
            sp.wait_ge(s_pv[1], 2 + NG * NIT * (UN // 2))
            for s in range(SLOTS):
                expert(s, s)
            sp.dma_start(gcw_b[:, :, :], bcast(gcw.rearrange("(a d) one -> a (d one)", a=2))).then_inc(s_gcw, 16)
            for r in range(1, E // SLOTS):
                for s in range(SLOTS):
                    sp.wait_ge(s_eo[s], 1 + r)
                    expert(r * SLOTS + s, s)
            for t in range(TT):
                sp.wait_ge(s_out, t + 1)
                sp.dma_start(out[0, t * P:(t + 1) * P], moe2[:, t]).then_inc(s_fin, 16)
            sp.wait_ge(s_fin, 16 * TT)

        @block.gpsimd
        def _(pool):
            for m in (identf, identb):
                pool.memset(m[:, :], 0.0).then_inc(s_c, 1)
            pool.wait_ge(s_c, 2)
            for m in (identf, identb):
                pool.affine_select(out=m[:, :], in_=m[:, :], compare_op=ALU.not_equal, fill=1.0, base=0,
                                   pattern=[[-1, P]], channel_multiplier=1).then_inc(s_c, 1)
            pool.memset(mhalf[:, :], -0.5).then_inc(s_c, 1)
            pool.wait_ge(s_c, 5)
            pool.memset(hmask[:, :], DH ** -0.5).then_inc(s_hm, 1)
            pool.memset(tri[:, :, :], 1.0).then_inc(s_hm, 1)
            pool.wait_ge(s_hm, 2)
            pool.affine_select(out=hmask[:, :], in_=hmask[:, :], compare_op=ALU.is_ge, fill=0.0, base=0,
                               pattern=[[-DH, P // DH]], channel_multiplier=1).then_inc(s_hm, 1)
            pool.affine_select(out=tri[:, :, :], in_=tri[:, :, :], compare_op=ALU.is_gt, fill=0.0, base=0,
                               pattern=[[1, E], [-1, E]], channel_multiplier=0).then_inc(s_hm, 1)
            pool.wait_ge(s_hm, 4)
            pool.affine_select(out=hmask[:, :], in_=hmask[:, :], compare_op=ALU.is_ge, fill=0.0, base=DH - 1,
                               pattern=[[DH, P // DH]], channel_multiplier=-1).then_inc(s_hm, 1)

            def power(n):
                pool.wait_ge(s_lnv, n + 1)
                pool.tensor_tensor(rstd[:, :], vare[:, :], mhalf[:, :], ALU.pow).then_inc(s_lnr, 1)

            power(0)
            pool.memset(zero[:, :], 0.0).then_inc(s_c, 1)
            pool.wait_ge(s_v, NCTX // CHUNK)
            keys_stacked(pool, NSUPER)
            pool.memset(vr[:, :, :, :], 0.0).then_inc(s_c, 1)
            pool.wait_ge(s_c, 7)
            pool.memset(vr[:, :, :, DH:DH + 1], 1.0).then_inc(s_c, 1)
            pool.memset(woP[:, :, :], 0.0).then_inc(s_woz, 1)
            pool.wait_ge(s_c, 8)

            def ring(g, it):
                for u in range(UN):
                    s, k = u % 2, (g * NIT + it) * (UN // 2) + u // 2
                    pool.wait_ge(s_pv[s], 2 + k)
                    src = val[:, bass.ds(it * UN + u, 1), bass.ds(g * GROUP * DH, GROUP * DH)]
                    pool.tensor_copy(vr[:, s, :, 0:DH], src[:, 0].rearrange("p (j d) -> p j d", d=DH))\
                        .then_inc(s_vr[s], 1)

            with pool.Fori(0, NG) as g:
                with pool.Fori(0, NIT) as it:
                    ring(g, it)
            pool.wait_ge(s_pv[1], 2 + NG * NIT * (UN // 2))
            pool.memset(vp[:, :, :, :], 0.0).then_inc(s_woz, 1)
            for n in range(1, 5):
                power(n)

        @block.scalar
        def _(act):
            free_at_first(act, s_rg, *s_rs, *s_p, s_zt, s_hc[2], s_hc[3])
            act.dma_start(x_sb[:, :, :], x[0].rearrange("(t p) d -> p t d", p=P)).then_inc(s_in, 16)
            act.dma_start(wn[:, 0], xWq.rearrange("(t p) i -> p t i", p=P)).then_inc(s_w, 16)
            for c, b in ((bq_c, xbq), (bk_c, xbk), (abq_c, abq), (abk_c, abk), (abl_c, abl)):
                act.dma_start(c[:, :], b.rearrange("(t p) -> p t", p=c.shape[0])).then_inc(s_b, 16)
            act.dma_start(gcb_b[:, :], bcast(gcb)).then_inc(s_b, 16)
            act.wait_ge(s_ob, 1)
            one = onesb[0:MROWS, :]
            act.dma_start(kst[ROWS:ROWS + MROWS, :, :].rearrange("p a b -> p (a b)"),
                          bass.AP(one.tensor, one.offset, [list(one.ap[0]), [0, H * NCTX // P], list(one.ap[1])]))\
               .then_inc(s_ones, 16)
            act.activation(first_exp[:, :], onesb[:, 0:1], ACT.Exp).then_inc(s_ob, 1)
            for i, to in enumerate((wT[:, 0], wT[:, 1], wqT)):
                act.wait_ge(s_wt, i + 1)
                act.activation(to.rearrange("p k o -> p (k o)") if i < 2 else to[:, :, :].rearrange("p k o -> p (k o)"),
                               psum[:, 1 + i], ACT.Copy).then_inc(s_wtc, 1)

            def half(s, c):
                act.wait_ge(s_tr[s], c + 1)
                if not first(c):
                    act.wait_ge(s_kmm[1] if s == 0 else s_vmm[1], 2 * c - 1 if s == 0 else c)
                act.activation(cT[:, s, 0], psum[:, 0], ACT.Copy).then_inc(s_ta[s], 1)

            def values(s, c):
                act.wait_ge(s_vmm[s], c + 1)
                act.activation(val[:, bass.ds(4 * (2 * c + s), 4), :].rearrange("p a b -> p (a b)"),
                               psum[:, 4:6, :].rearrange("p a b -> p (a b)"), ACT.Copy).then_inc(s_v, 1)

            def keys(s, c, buf):
                n = 2 * c + s
                sl = slice(s * CHUNK, (s + 1) * CHUNK)
                for o in range(DT):
                    act.wait_ge(s_kmm[o], n + 1)
                    if not first(c):
                        keys_stacked(act, c - 1, (o,))
                    act.activation(buf[:, o, 0, sl], psum[:, 2 + o], ACT.Identity, bias=bk_c[:, o:o + 1])\
                       .then_inc(s_k1[o], 1)
                for o in range(DT):
                    act.wait_ge(s_r1[o], n + 1)
                    act.activation(buf[:, o, 1, sl], r1[:, o], ACT.Copy).then_inc(s_k2[o], 1)
                for o in range(DT):
                    act.wait_ge(s_k1[o], n + 1)
                    part = buf[:, o, 0, sl]
                    act.activation(buf[:, o, 3:6:2, sl],
                                   bass.AP(part.tensor, part.offset, [list(part.ap[0]), [0, 2], list(part.ap[1])]),
                                   ACT.Copy).then_inc(s_kb[o], 2)

            def next_chunk(s, c):
                act.wait_ge(s_tr[s], c + 1)
                act.dma_start(cs[:, s], ctx_v[bass.ds(2 * c + 2 + s, 1)][0]).then_inc(s_ctx[s], 16)

            def superchunk(c, buf):
                if not first(c):
                    next_chunk(0, c)
                half(1, c)
                next_chunk(1, c)
                values(0, c)
                keys(0, c, buf)
                half(0, c + 1)
                keys(1, c, buf)
                values(1, c)

            act.wait_ge(s_b, 16 * 6)
            half(0, 0)
            next_chunk(0, 0)
            act.wait_ge(s_xt, 1)
            act.activation(xT[:, :, :], psum[:, 7].rearrange("p (k t) -> p k t", k=DT), ACT.Copy).then_inc(s_xtc, 1)
            for o in range(DT):
                act.wait_ge(s_q, o + 1)
                act.activation(qp[:, o, 0, :], psum[:, 4 + o, 0:NT], ACT.Identity,
                               bias=bq_c[:, o:o + 1]).then_inc(s_q1, 1)
            act.wait_ge(s_q1, 2)
            act.activation(qp[:, :, 1, :], qp[:, :, 0, :], ACT.Copy).then_inc(s_qp, 1)
            act.activation(qp[:, :, 2, :], qp[:, :, 0, :], ACT.Copy).then_inc(s_qp, 1)
            act.wait_ge(s_qr, 2)
            act.activation(qp[:, :, 3, :], q1[:, :, :], ACT.Copy).then_inc(s_q2, 1)
            act.wait_ge(s_q2, 1)
            act.activation(qp[:, :, 4, :], qp[:, :, 3, :], ACT.Copy).then_inc(s_qp, 1)
            act.wait_ge(s_ones, 16)
            superchunk(0, kp_even)
            act.wait_ge(s_qst, 16 * H)
            with act.Fori(0, NSUPER // 2 - 1) as i:
                superchunk(2 * i + 1, kp)
                superchunk(2 * i + 2, kp_even)
            half(1, NSUPER - 1)
            values(0, NSUPER - 1)
            keys(0, NSUPER - 1, kp)
            keys(1, NSUPER - 1, kp)
            values(1, NSUPER - 1)

            keys_stacked(act, NSUPER)
            for c, b in ((bv_b, xbv), (gam_b, xgamma), (bet_b, xbeta)):
                act.dma_start(c[:, :], bcast(b)).then_inc(s_par, 16)

            def m_rows(g):
                act.wait_ge(s_mr, g + 1)
                act.activation(qst[ROWS:ROWS + MROWS, bass.ds(g * GROUP, 2), :].rearrange("p a b -> p (a b)"),
                               psum[ROWS:ROWS + MROWS, 5], ACT.Copy).then_inc(s_mq, 1)

            def rbank(i):
                return psum[:, i].rearrange("p (k d) -> p k d", k=DT)

            def rot_copy(u):
                act.wait_ge(s_rt, u + 1)
                if u >= NROT:
                    act.wait_ge(s_rm, u - NROT + 1)
                act.activation(rT[:, rot_of(u)], rbank(5), ACT.Copy).then_inc(s_rtc, 1)

            def exps(g, it, last=False):
                for u in range(UN):
                    s, k = u % 2, (g * NIT + it) * (UN // 2) + u // 2
                    act.wait_ge(s_s[s], k + 1)
                    act.wait_ge(s_pv[s], 1 + k)
                    act.activation(pr[:, u % PRS], ps_s[s].rearrange("p a b -> p (a b)"), ACT.Exp).then_inc(s_p[s], 1)
                    if last and 0 < u <= BESIDE:
                        rot_copy(u - 1)

            def sums(g):
                act.wait_ge(s_pv[1], 2 + (g + 1) * NIT * (UN // 2))
                act.wait_ge(s_zp, 1 + g)
                act.activation(zt[:, :], ps_pv, ACT.Copy).then_inc(s_zt, 1)

            m_rows(0)
            with act.Fori(0, NG - 1) as g:
                with act.Fori(0, NIT) as it:
                    exps(g, it)
                sums(g)
                m_rows(g + 1)
            with act.Fori(0, NIT - 1) as it:
                exps(NG - 1, it)
            exps(NG - 1, NIT - 1, True)
            sums(NG - 1)

            for u in range(BESIDE, EARLY):
                rot_copy(u)

            act.wait_ge(s_t2, 1)
            act.activation(xT2[:, :, :], rbank(0), ACT.Copy).then_inc(s_t2c, 1)
            act.wait_ge(s_al, 1)
            act.activation(latT[:, :], psum[0:LAT, 2, 0:NT], ACT.Identity, bias=abl_c[:, 0:1]).then_inc(s_alc, 1)
            act.wait_ge(s_ak, 1)
            for o in range(DT):
                act.activation(kT[:, o], psum[:, 3, o * NT:(o + 1) * NT], ACT.Identity, bias=abk_c[:, o:o + 1])\
                   .then_inc(s_akc, 1)
            rot_copy(EARLY)
            def sums_out(g):
                act.wait_ge(s_az, g + 1)
                act.activation(zT[:, g], psum[:, 4, 0:NT], ACT.Copy).then_inc(s_azc, 1)

            for n in range(STEPS):
                act.wait_ge(s_anm, n + 1)
                if n >= 2:
                    act.wait_ge(s_at, n - 1)
                for j in range(2):
                    act.activation(pa[:, n % 2, j], psum[:, n % 2, j * NT:(j + 1) * NT], ACT.Exp,
                                   bias=nm[:, 2 * n + j:2 * n + j + 1],
                                   accum_out=rs[:, 2 * n + j:2 * n + j + 1]).then_inc(s_ae, 1)
                if n % GROUP == 2 and n > 2:
                    sums_out(n // GROUP - 1)
                if n >= 1 and (n - 1) % 2 == 0:
                    att_copy(act.activation, n - 1, act, s_at, s_atA)
                for u in product_at(n, 1):
                    rot_copy(u)
            sums_out(NG - 1)
            for u in (RPROD - 2, RPROD - 1):
                rot_copy(u)

            act.wait_ge(s_e1t, 1)
            act.activation(eb1_c[:, :], psum[:, 4, 0:E * HT], ACT.Copy).then_inc(s_e1c, 1)
            act.wait_ge(s_t3, 1)
            act.activation(xgT[:, :, :], rbank(0), ACT.Copy).then_inc(s_t3c, 1)
            act.wait_ge(s_lm, 1)
            for t in range(TT):
                act.activation(ex[:, t], lg[:, t], ACT.Exp, bias=lm[:, t:t + 1]).then_inc(s_ex, 1)
            act.wait_ge(s_abi, 2)
            act.activation(abel[:, :, :], abin[:, :, :], ACT.Gelu).then_inc(s_abel, 1)
            act.wait_ge(s_wt8, 1)
            act.activation(wdT[:, :], psum[0:E, 3, 0:NT], ACT.Copy).then_inc(s_wt8c, 1)

            def hidden(r, s):
                act.wait_ge(s_h[s], r + 1)
                act.wait_ge(s_eo[(s + 2) % SLOTS], 1 + r + (s >= 2))
                for t in range(HT):
                    act.activation(hT[:, s % 2, t], psum[:, 4 + 2 * (s % 2) + t // 2, (t % 2) * NT:(t % 2 + 1) * NT],
                                   ACT.Gelu, bias=eb1_c[:, bass.ds((r * SLOTS + s) * HT + t, 1)]).then_inc(s_hc[s], 1)

            with act.Fori(0, E // SLOTS) as r:
                for s in range(SLOTS):
                    hidden(r, s)
            for t in range(TT):
                act.wait_ge(s_mt, t + 1)
                act.activation(moeT[:, :, t * P:(t + 1) * P],
                               psum[:, 4 + t, 0:DT * P].rearrange("p (k d) -> p k d", k=DT), ACT.Copy)\
                   .then_inc(s_mtc, 1)
            for t in range(TT):
                act.wait_ge(s_gz, t + 1)
                act.activation(gs[:, 2, t:t + 1], gs[:, 1, t:t + 1], ACT.Tanh, scale=0.5).then_inc(s_ge, 1)

        @block.vector
        def _(dve):
            ch = Chain(dve, s_dve)

            def moments(src):
                for t in range(TT):
                    ch.step(dve.bn_stats(stats[:, t], src[:, t]))
                for t in range(TT):
                    ch.step(dve.bn_aggr(mv[:, t], stats[:, t]))
                dve.tensor_scalar(vare[:, :], mv[:, :, 1], EPS, None, ALU.add).then_inc(s_lnv, 1)

            def norm(n, dst, src, meanwhile=lambda: None):
                moments(src)
                meanwhile()
                dve.wait_ge(s_lnr, n + 1)
                for t in range(TT):
                    last = dve.tensor_scalar(dst[:, t], src[:, t], mv[:, t, 0:1], rstd[:, t:t + 1],
                                             ALU.subtract, ALU.mult)
                    last.then_inc(s_ln, 1)

            def norm_affine(n, dst, src, tmp, gamma, beta, meanwhile=lambda: None):
                moments(src)
                for t in range(TT):
                    ch.step(dve.scalar_tensor_tensor(tmp[:, t], src[:, t], mv[:, t, 0:1], gamma,
                                                     ALU.subtract, ALU.mult))
                meanwhile()
                dve.wait_ge(s_lnr, n + 1)
                for t in range(TT):
                    dve.scalar_tensor_tensor(dst[:, t], tmp[:, t], rstd[:, t:t + 1], beta(t), ALU.mult, ALU.add)\
                       .then_inc(s_ln, 1)

            free_at_first(dve, *s_mx, s_z, *[s_acc] * TT)
            dve.memset(onesb[:, :], 1.0).then_inc(s_ob, 1)
            dve.wait_ge(s_in, 16)
            norm(0, dec, x_sb)
            dve.wait_ge(s_b, 16 * 6)

            def half(s, c):
                dve.wait_ge(s_tr[s], c + 1)
                if not first(c):
                    dve.wait_ge(s_kmm[1] if s == 0 else s_vmm[1], 2 * c - 1 if s == 0 else c)
                dve.tensor_copy(cT[:, s, 1], psum[:, 1]).then_inc(s_tv[s], 1)

            def remainder(s, c, o, buf):
                n = 2 * c + s
                dve.wait_ge(s_k1[o], n + 1)
                if not first(c) or s > 0:
                    dve.wait_ge(s_kd[o], 2 * n)
                dve.scalar_tensor_tensor(r1[:, o], psum[:, 2 + o], bk_c[:, o:o + 1],
                                         buf[:, o, 0, s * CHUNK:(s + 1) * CHUNK],
                                         ALU.add, ALU.subtract).then_inc(s_r1[o], 1)

            def last_parts(s, c, o, buf):
                sl = slice(s * CHUNK, (s + 1) * CHUNK)
                dve.wait_ge(s_k2[o], 2 * c + s + 1)
                dve.wait_ge(s_r1[o], 2 * c + s + 1)
                dve.tensor_tensor(buf[:, o, 2, sl], r1[:, o], buf[:, o, 1, sl], ALU.subtract).then_inc(s_kd[o], 1)
                dve.tensor_copy(buf[:, o, 4, sl], buf[:, o, 1, sl]).then_inc(s_kd[o], 1)

            def first_maxima(c, pairs):
                for v in [v for pair in pairs for v in (2 * pair, 2 * pair + 1)]:
                    b, uses, before = (max_bank(v) if c is LAST_SUPER else (1 + v % 2, 8, v // 2))
                    j, t, half = (v // 2 % 4, v % 2, v // 8) if c is LAST_SUPER else (v // 4, v // 2 % 2, v % 2)
                    dve.wait_ge(s_mmm[b], (8 * (NSUPER - 1) * (b > 0) if c is LAST_SUPER else uses * c) + before + 1)
                    dve.tensor_reduce(mx0[:, j, t, bass.ds(2 * c + half, 1)], psum[:, MB[b]], AX.X, ALU.max)\
                        .then_inc(s_mx[b], 1)

            def project(s, c, buf, m):
                if s == 0:
                    m(range(0, 2))
                    remainder(s, c, 0, buf)
                    m(range(2, 3))
                    remainder(s, c, 1, buf)
                    m(range(3, 4))
                    last_parts(s, c, 0, buf)
                    last_parts(s, c, 1, buf)
                else:
                    remainder(s, c, 0, buf)
                    m(range(4, 5))
                    remainder(s, c, 1, buf)
                    last_parts(s, c, 0, buf)
                    m(range(5, 6))
                    last_parts(s, c, 1, buf)
                    m(range(6, 8))

            def no_maxima(pairs):
                pass

            half(0, 0)
            for o in range(DT):
                dve.wait_ge(s_q1, o + 1)
                dve.scalar_tensor_tensor(q1[:, o, :], psum[:, 4 + o, 0:NT], bq_c[:, o:o + 1],
                                         qp[:, o, 0, :], ALU.add, ALU.subtract).then_inc(s_qr, 1)
            dve.wait_ge(s_q2, 1)
            dve.wait_ge(s_qr, 2)
            dve.tensor_tensor(qp[:, :, 5, :], q1[:, :, :], qp[:, :, 3, :], ALU.subtract).then_inc(s_qp, 3)
            half(1, 0)
            project(0, 0, kp_even, no_maxima)
            half(0, 1)
            project(1, 0, kp_even, no_maxima)
            with dve.Fori(0, NSUPER // 2 - 1) as i:
                for c, buf in ((2 * i + 1, kp), (2 * i + 2, kp_even)):
                    def before(pairs):
                        first_maxima(c - 1, pairs)
                    half(1, c)
                    project(0, c, buf, before)
                    half(0, c + 1)
                    project(1, c, buf, before)

            def before_last(pairs):
                first_maxima(NSUPER - 2, pairs)
            half(1, NSUPER - 1)
            project(0, NSUPER - 1, kp, before_last)
            project(1, NSUPER - 1, kp, before_last)
            first_maxima(LAST_SUPER, range(8))
            for b in range(3):
                dve.wait_ge(s_mx[b], MX0[b])
            dve.tensor_reduce(negm[:, :, :].rearrange("p j t -> p (j t)"),
                              mx0[:, :, :, :].rearrange("p j t k -> p (j t) k"),
                              AX.X, ALU.max, negate=True).then_inc(s_mxh, 1)

            def maxima(body, it):
                for v in range(16):
                    b, uses, before = max_bank(v)
                    dve.wait_ge(s_mmm[b], FIRST_USES[b] + body * uses + before + 1)
                    if v == 0:
                        dve.wait_ge(s_mxh, 1 + body)
                    dve.tensor_reduce(mxs[:, v // 8, v % 8:v % 8 + 1], psum[:, MB[b]], AX.X, ALU.max)\
                        .then_inc(s_mx[b], 1)
                for b in range(3):
                    dve.wait_ge(s_mx[b], MX0[b] + (body + 1) * MAX_USES[b])
                dve.tensor_reduce(negm[:, bass.ds(it, 1), :].rearrange("p a t -> p (a t)"), mxs[:, :, :],
                                  AX.X, ALU.max, negate=True).then_inc(s_mxh, 1)

            def m_parts(g):
                nm = negm[:, :, :].rearrange("p j t -> p (j t)")
                dve.wait_ge(s_mxh, 1 + g * NIT)
                dve.tensor_copy(mp[:, :, 0], nm).then_inc(s_mp, 1)
                dve.wait_ge(s_mp, 4 * g + 1)
                dve.tensor_tensor(mrem[:, :], nm, mp[:, :, 0], ALU.subtract).then_inc(s_mp, 1)
                dve.wait_ge(s_mp, 4 * g + 2)
                dve.tensor_copy(mp[:, :, 1], mrem[:, :]).then_inc(s_mp, 1)
                dve.wait_ge(s_mp, 4 * g + 3)
                dve.tensor_tensor(mp[:, :, 2], mrem[:, :], mp[:, :, 1], ALU.subtract).then_inc(s_mp, 1)

            def m_rows(g):
                dve.wait_ge(s_mr, g + 1)
                dve.tensor_copy(qst[ROWS:ROWS + MROWS, bass.ds(g * GROUP + 2, 2), :].rearrange("p a b -> p (a b)"),
                                psum[ROWS:ROWS + MROWS, 6]).then_inc(s_mw, 1)

            def divide(g):
                dve.wait_ge(s_zp, 1 + g + 1)
                zp = psum[:, 7, 0:TT * P].rearrange("p (t j c) -> p t j c", t=TT, c=VW)
                dve.reciprocal(rden[:, :, :], zp[:, :, :, DH]).then_inc(s_z, 1)
                dve.wait_ge(s_z, 1 + ZSTEPS * g + 1)
                cols = bass.ds(g * GROUP * DH, GROUP * DH)
                for t in range(TT):
                    dve.tensor_tensor(zq[:, t, cols].rearrange("p (j d) -> p j d", d=DH),
                                      zp[:, t, :, 0:DH], spread(rden[:, t], DH), ALU.mult).then_inc(s_z, 1)
                dve.wait_ge(s_z, 1 + ZSTEPS * g + 1 + TT)
                for t in range(TT):
                    dve.tensor_tensor(zq[:, t, cols], zq[:, t, cols], bv_b[:, cols], ALU.add).then_inc(s_z, 1)

            m_parts(0)
            m_rows(0)
            dve.wait_ge(s_par, 16 * 3)
            with dve.Fori(0, NG - 1) as g:
                with dve.Fori(0, NIT) as it:
                    maxima(NIT * g + it, it)
                m_parts(g + 1)
                m_rows(g + 1)
                divide(g)
            def flat(a):
                return a.rearrange("p k d -> p (k d)")

            def rot_combine(u):
                m, i, b = u // NROT, rot_of(u), rot_bank(u)
                y, a2, a, l, r = (flat(w[:, i]) for w in (rY, rA2, rA, rL, rU))
                dve.wait_ge(s_rm, u + 1)
                if u >= NROT:
                    dve.wait_ge(s_rv, u - NROT + 1)
                if m == 0:
                    ch.step(dve.tensor_copy(a2, psum[:, b]))
                    dve.scalar_tensor_tensor(r, a2, T1 / T2, a, ALU.mult, ALU.add).then_inc(s_rv, 1)
                    dve.wait_ge(s_rv, u + 1)
                    ch.step(dve.tensor_scalar(l, a, T4, None, ALU.mult))
                    ch.step(dve.scalar_tensor_tensor(l, a2, T3, l, ALU.mult, ALU.add))
                    ch.step(dve.scalar_tensor_tensor(y, a2, 0.5, a, ALU.mult, ALU.add))
                    ch.step(dve.tensor_scalar(a, a2, T5, None, ALU.mult))
                elif m == 1:
                    dve.wait_ge(s_dve, ch.n)
                    ch.step(dve.scalar_tensor_tensor(l, psum[:, b], T2, l, ALU.mult, ALU.add))
                    ch.step(dve.scalar_tensor_tensor(r, psum[:, b], T2, a, ALU.mult, ALU.add))
                    dve.scalar_tensor_tensor(y, psum[:, b], T6 * T2, y, ALU.mult, ALU.add).then_inc(s_rv, 1)
                elif m == 2:
                    dve.tensor_tensor(y, y, psum[:, b], ALU.add).then_inc(s_rv, 1)
                elif u < NROT * (3 + SQUARINGS):
                    dve.scalar_tensor_tensor(y, y, 2.0, psum[:, b], ALU.mult, ALU.add).then_inc(s_rv, 1)
                else:
                    dve.wait_ge(s_rv, u)
                    ch.step(dve.tensor_tensor(flat(rY[:, 0]), flat(rY[:, 0]), flat(rY[:, right_of(u)]), ALU.add))
                    dve.tensor_tensor(flat(rY[:, 0]), flat(rY[:, 0]), psum[:, b], ALU.add).then_inc(s_rv, 1)

            dve.wait_ge(s_prm, 16 * NPRM)
            dve.tensor_scalar(rA[:, :, :, :], rA[:, :, :, :], 2.0 ** -SQUARINGS, None, ALU.mult).then_inc(s_rA, 1)
            for t in range(TT):
                ch.step(dve.tensor_tensor(x_sb[:, t], x_sb[:, t], bet_b[:, :], ALU.add))
            for u in range(BESIDE - 2):
                rot_combine(u)
            divide(NG - 1)
            for u in range(BESIDE - 2, COMBINED_FIRST):
                rot_combine(u)
            dve.wait_ge(s_zz, 16 * TT * H)
            for t in range(TT):
                ch.step(dve.tensor_tensor(z[:, t], z[:, t], dec[:, t], ALU.add))
            norm_affine(1, x_sb, z, z, gam_b[:, :], lambda t: x_sb[:, t], lambda:
                        [rot_combine(u) for u in range(COMBINED_FIRST, COMBINED_NEXT)])
            dve.wait_ge(s_ln, 4)

            norm(2, n2, x_sb, lambda: [rot_combine(u) for u in range(COMBINED_NEXT, EARLY - 1)])
            dve.wait_ge(s_hm, 5)
            dve.wait_ge(s_aq, 1)
            for o in range(DT):
                dve.tensor_scalar(qf[:, o], psum[:, 1, o * NT:(o + 1) * NT], abq_c[:, o:o + 1], None, ALU.add)\
                   .then_inc(s_qf, 1)
            dve.wait_ge(s_qf, 2)
            for h in range(H):
                o, j = divmod(h, P // DH)
                dve.tensor_scalar(qm[:, h], qf[:, o], hmask[:, j:j + 1], None, ALU.mult).then_inc(s_qm, 1)
            dve.wait_ge(s_av, 1)
            dve.wait_ge(s_woz, 2)
            for t in range(TT):
                dve.tensor_tensor(vp[:, t, :, 0:DH], psum[:, 2, t * D:(t + 1) * D].rearrange("p (h d) -> p h d", d=DH),
                                  abv_b[:, :].rearrange("p (h d) -> p h d", d=DH), ALU.add).then_inc(s_avc, 1)

            def att_max(n):
                dve.wait_ge(s_as, n + 1)
                dve.tensor_reduce(nm[:, 2 * n:2 * n + 2], psum[:, n % 2, :].rearrange("p (j k) -> p j k", j=2),
                                  AX.X, ALU.max, negate=True).then_inc(s_anm, 1)

            att_max(0)
            for n in range(STEPS):
                if n + 1 < STEPS:
                    att_max(n + 1)
                dve.wait_ge(s_ae, 2 * n + 2)
                dve.reciprocal(rr[:, 2 * n:2 * n + 2], rs[:, 2 * n:2 * n + 2]).then_inc(s_ar, 1)
                dve.wait_ge(s_ar, n + 1)
                for j in range(2):
                    dve.tensor_scalar(pa[:, n % 2, j], pa[:, n % 2, j], rr[:, 2 * n + j:2 * n + j + 1], None, ALU.mult)\
                       .then_inc(s_an, 1)
                if n >= 1 and (n - 1) % 2 == 1:
                    att_copy(dve.tensor_copy, n - 1, dve, s_at, s_atV)
                for u in product_at(n, -1):
                    rot_combine(u)
            att_copy(dve.tensor_copy, STEPS - 1, dve, s_at, s_atV)
            for t in range(TT):
                ch.step(dve.tensor_tensor(x_sb[:, t], x_sb[:, t], abo_b[:, :], ALU.add))
            for t in range(TT):
                dve.wait_ge(s_ao, t + 1)
                ch.step(dve.tensor_tensor(x_sb[:, t], x_sb[:, t], psum[:, 7 - t, 0:D], ALU.add))

            norm(3, xp, x_sb, lambda: rot_combine(RPROD - 2))
            dve.wait_ge(s_ln, 8)
            norm_affine(4, xg, xp, n2, lng_b[:, :], lambda t: lnb_b[:, :], lambda: [
                ch.step(dve.tensor_tensor(x_sb[:, t], x_sb[:, t], xp[:, t], ALU.add)) for t in range(TT)])
            rot_combine(RPROD - 1)
            dve.wait_ge(s_lg, 1)
            for t in range(TT):
                ch.step(dve.tensor_tensor(lg[:, t], psum[:, 2, t * E:(t + 1) * E], gb_b[:, :], ALU.add))
            dve.tensor_reduce(lm[:, :], lg[:, :, :], AX.X, ALU.max, negate=True).then_inc(s_lm, 1)
            dve.wait_ge(s_ab, 1)
            for t in range(TT):
                dve.tensor_tensor(abin[:, t], psum[:, 1, t * D:(t + 1) * D], abb_b[:, :], ALU.add).then_inc(s_abi, 1)
            for t in range(TT):
                row = lg[:, t]
                other = bass.AP(row.tensor, row.offset, [list(row.ap[0]), [0, E], list(row.ap[1])])
                ch.step(dve.tensor_tensor(cgt[:, t], other, spread(row, E), ALU.is_gt))
                ch.step(dve.tensor_tensor(ceq[:, t], other, spread(row, E), ALU.is_equal))
                ch.step(dve.tensor_tensor(ceq[:, t], ceq[:, t], tri[:, :, :], ALU.mult))
                ch.step(dve.tensor_tensor(cgt[:, t], cgt[:, t], ceq[:, t], ALU.add))
            ch.step(dve.tensor_reduce(rank[:, :, :], cgt[:, :, :, :], AX.X, ALU.add))
            ch.step(dve.tensor_scalar(rank[:, :, :], rank[:, :, :], 2.0, None, ALU.is_lt))
            dve.wait_ge(s_ex, 2)
            ch.step(dve.tensor_tensor(wd[:, :, :], ex[:, :, :], rank[:, :, :], ALU.mult))
            ch.step(dve.tensor_reduce(wsum[:, :], wd[:, :, :], AX.X, ALU.add))
            ch.step(dve.reciprocal(wsum[:, :], wsum[:, :]))
            for t in range(TT):
                dve.tensor_scalar(wd[:, t], wd[:, t], wsum[:, t:t + 1], None, ALU.mult).then_inc(s_wd, 1)
            dve.wait_ge(s_abel, 1)
            dve.wait_ge(s_gcw, 16)
            for t in range(TT):
                ch.step(dve.tensor_tensor(x_sb[:, t], x_sb[:, t], abel[:, t], ALU.add))
                ch.step(dve.tensor_tensor_reduce(prod[:, :], abel[:, t], gcw_b[:, 0], 1.0, 0.0, ALU.mult, ALU.add,
                                                 gs[:, 0, t:t + 1]))
            ch.step(dve.tensor_scalar(gs[:, 0], gs[:, 0], gcb_b[:, 0:1], None, ALU.add))
            dve.wait_ge(s_b2, 1)
            dve.tensor_copy(moe[:, :, :].rearrange("p t d -> p (t d)"), psum[:, 0]).then_inc(s_acc, 1)
            dve.wait_ge(s_wd, 2)
            with dve.Fori(0, E // SLOTS) as r:
                for s in range(SLOTS):
                    dve.wait_ge(s_eo[s], 1 + r + 1)
                    for t in range(TT):
                        dve.wait_ge(s_acc, TT + (r * SLOTS + s) * TT + t + (1 if t == 0 else 0))
                        dve.scalar_tensor_tensor(moe[:, t], psum[:, 2 + s % 2, t * D:(t + 1) * D],
                                                 wd[:, t, bass.ds(r * SLOTS + s, 1)], moe[:, t],
                                                 ALU.mult, ALU.add).then_inc(s_acc, 1)
            for t in range(TT):
                dve.wait_ge(s_rot, t + 1)
                dve.wait_ge(s_acc, TT + 1 + E * TT)
                ch.step(dve.tensor_tensor(moe2[:, t], psum[:, 6 + t, 0:D], moe[:, t], ALU.add))
                ch.step(dve.tensor_tensor_reduce(prod[:, :], moe2[:, t], gcw_b[:, 1], 1.0, 0.0, ALU.mult, ALU.add,
                                                 gs[:, 3, t:t + 1]))
                dve.tensor_tensor(gs[:, 1, t:t + 1], gs[:, 0, t:t + 1], gs[:, 3, t:t + 1], ALU.add).then_inc(s_gz, 1)
                ch.step(dve.tensor_tensor(moe2[:, t], moe2[:, t], abel[:, t], ALU.subtract))
            for t in range(TT):
                dve.wait_ge(s_ge, t + 1)
                ch.step(dve.tensor_scalar(gs[:, 4, t:t + 1], gs[:, 2, t:t + 1], 0.5, 0.5, ALU.mult, ALU.add))
                dve.scalar_tensor_tensor(moe2[:, t], moe2[:, t], gs[:, 4, t:t + 1], x_sb[:, t], ALU.mult, ALU.add)\
                   .then_inc(s_out, 1)

        @block.tensor
        def _(pe):
            def transpose4(dst, src):
                for k in range(2):
                    for t in range(2):
                        last = pe.transpose(dst[:, k * 256 + t * P:k * 256 + (t + 1) * P],
                                            src[:, t, k * P:(k + 1) * P], identf[:, :])
                return last

            free_at_first(pe, *s_pv, *s_pv, s_zp, *s_eo)
            def stay_warm(n, bank):
                for _ in range(n):
                    pe.matmul(psum[:, bank, 0:P], onesb[:, :], onesb[:, :], start=True, stop=True)

            pe.wait_ge(s_c, 4)
            pe.wait_ge(s_w, 16 * 3)
            for bank, i in ((1, 1), (2, 2), (3, 0)):
                transpose4(psum[:, bank], wn[:, i]).then_inc(s_wt, 1)

            def turn(s, c):
                pe.wait_ge(s_ctx[s], 16 * (c + 1))
                if s > 0 or not first(c):
                    pe.wait_ge(s_ta[1 - s], c + s)
                    pe.wait_ge(s_tv[1 - s], c + s)
                for k in range(DT):
                    for t in range(CHUNK // P):
                        last = pe.transpose(psum[:, k, t * P:(t + 1) * P],
                                            cs[:, s, t, k * P:(k + 1) * P], identf[:, :])
                last.then_inc(s_tr[s], 1)

            def project_keys(s, c, o):
                if s > 0 or not first(c):
                    pe.wait_ge(s_r1[o], 2 * c + s)
                for k in range(DT):
                    last = pe.matmul(psum[:, 2 + o], wT[:, 0, k, o * P:(o + 1) * P], cT[:, s, k],
                                     start=(k == 0), stop=(k == DT - 1))
                last.then_inc(s_kmm[o], 1)

            def project_values(s, c, half):
                if half == 0 and (s > 0 or not first(c)):
                    pe.wait_ge(s_v, 2 * c + s)
                for t in (2 * half, 2 * half + 1):
                    for k in range(DT):
                        last = pe.matmul(psum[:, 4 + t // 2, (t % 2) * D:(t % 2 + 1) * D],
                                         cT[:, s, k, t * P:(t + 1) * P], wT[:, 1, k, :],
                                         start=(k == 0), stop=(k == DT - 1))
                if half == 1:
                    last.then_inc(s_vmm[s], 1)

            def project(s, c, maxima):
                pe.wait_ge(s_ta[s], c + 1)
                pe.wait_ge(s_tv[s], c + 1)
                steps = [(project_values, 0), (project_values, 1), (project_keys, 0), (project_keys, 1)]
                for i, (step, which) in enumerate(steps if s == 0 else steps[2:] + steps[:2]):
                    step(s, c, which)
                    maxima(4 * s + i)

            def first_maxima(c, pair):
                for v in (2 * pair, 2 * pair + 1):
                    j, t, half = v // 4, v // 2 % 2, v % 2
                    if c is LAST_SUPER:
                        j, t, half = v // 2 % 4, v % 2, v // 8
                        b, _, before = max_bank(v)
                        before += 8 * (NSUPER - 1) * (b > 0)
                    else:
                        b, before = 1 + v % 2, 8 * c + v // 2
                    pe.wait_ge(s_mx[b], 1 + before)
                    pe.matmul(psum[:, MB[b]], qst[0:ROWS, j, t * P:(t + 1) * P],
                              kst[0:ROWS, j, bass.ts(2 * c + half, 512)], start=True, stop=True)\
                      .then_inc(s_mmm[b], 1)

            def no_maxima(pair):
                pass

            pe.wait_ge(s_wtc, 3)
            turn(0, 0)
            pe.wait_ge(s_ln, 2)
            transpose4(psum[:, 7], dec).then_inc(s_xt, 1)
            pe.wait_ge(s_xtc, 1)
            for o in range(DT):
                for k in range(DT):
                    last = pe.matmul(psum[:, 4 + o, 0:NT], wqT[:, k, o * P:(o + 1) * P], xT[:, k],
                                     start=(k == 0), stop=(k == DT - 1))
                last.then_inc(s_q, 1)
            turn(1, 0)
            pe.wait_ge(s_q1, 2)
            pe.wait_ge(s_qr, 2)
            project(0, 0, no_maxima)
            turn(0, 1)
            project(1, 0, no_maxima)
            pe.wait_ge(s_qst, 16 * H)

            with pe.Fori(1, NSUPER - 1) as c:
                def before(pair):
                    if pair == 0:
                        pe.wait_ge(s_rg, 1 + 16 * GROUP * c)
                    first_maxima(c - 1, pair)
                turn(1, c)
                project(0, c, before)
                turn(0, c + 1)
                project(1, c, before)

            def before_last(pair):
                if pair == 0:
                    pe.wait_ge(s_rg, 1 + 16 * GROUP * (NSUPER - 1))
                first_maxima(NSUPER - 2, pair)
            turn(1, NSUPER - 1)
            project(0, NSUPER - 1, before_last)
            project(1, NSUPER - 1, before_last)

            def maxima(body, h, vs):
                for v in vs:
                    b, uses, before = max_bank(v)
                    pe.wait_ge(s_mx[b], MX0[b] + body * uses + before)
                    pe.matmul(psum[:, MB[b]], qst[0:ROWS, bass.ds(h, 1), (v // 8) * P:(v // 8 + 1) * P][:, 0],
                              kst[0:ROWS, bass.ds(h, 1), (v % 8) * 512:(v % 8 + 1) * 512][:, 0],
                              start=True, stop=True).then_inc(s_mmm[b], 1)

            def m_rows(g):
                pe.wait_ge(s_mp, 4 * (g + 1))
                for j in range(GROUP):
                    for t in range(TT):
                        col = j * NT + t * P
                        last = pe.matmul(psum[ROWS:ROWS + MROWS, 5 + col // 512, col % 512:col % 512 + P],
                                         mp[:, j * TT + t, :], identb[:, :], start=True, stop=True)
                last.then_inc(s_mr, 1)

            def scores(g, kt, s, k):
                pe.wait_ge(s_p[s], 1 + k)
                for j in range(GROUP):
                    last = pe.matmul(ps_s[s][:, j // 2, (j % 2) * NT:(j % 2 + 1) * NT],
                                     kst[0:ROWS + MROWS, bass.ds(g * GROUP + j, 1), bass.ts(kt, P)][:, 0],
                                     qst[0:ROWS + MROWS, bass.ds(g * GROUP + j, 1), :][:, 0],
                                     start=True, stop=True)
                last.then_inc(s_s[s], 1)

            def weigh(s, slot, k, last_of_group):
                pe.wait_ge(s_p[s], 1 + k + 1)
                pe.wait_ge(s_vr[s], k + 1)
                for j in range(GROUP):
                    last = pe.matmul(psum[VW * j:VW * (j + 1), 4, 0:NT], vr[:, s, j, :],
                                     pr[:, slot, j * NT:(j + 1) * NT], start=False, stop=last_of_group,
                                     skip_group_check=True, tile_position=(0, VW * j))
                last.then_inc(s_pv[s], 1)

            def open_sums(g):
                pe.wait_ge(s_zt, 1 + g)
                for j in range(GROUP):
                    pe.matmul(psum[VW * j:VW * (j + 1), 4, 0:NT], zero[:, 0:VW], zero[:, :],
                              start=True, stop=False, skip_group_check=True, tile_position=(0, VW * j))

            def rot_trans(u):
                m, i = u // NROT, rot_of(u)
                pe.wait_ge(s_rv if u >= NROT else s_rA, 1 if u < NROT else u if right_of(u) != i else u - NROT + 1)
                if u >= 1:
                    pe.wait_ge(s_rtc, u)
                src = (rA, rA2, rL)[m][:, i] if m < 3 else rY[:, i]
                for k in range(DT):
                    for t in range(DT):
                        last = pe.transpose(psum[:, 5, k * D + t * P:k * D + (t + 1) * P],
                                            src[:, t, k * P:(k + 1) * P], identf[:, :])
                last.then_inc(s_rt, 1)

            def rot_mul(u):
                m, i = u // NROT, rot_of(u)
                right = (rA, rU, rU)[m][:, i] if m < 3 else rY[:, right_of(u)]
                pe.wait_ge(s_rtc, u + 1)
                if u >= 2:
                    pe.wait_ge(s_rv, u - 1)
                for o in range(DT):
                    for k in range(DT):
                        last = pe.matmul(psum[:, rot_bank(u), o * D:(o + 1) * D], rT[:, i, k, o * P:(o + 1) * P],
                                         right[:, k], start=(k == 0), stop=(k == DT - 1))
                last.then_inc(s_rm, 1)

            def body(g, it, last, following):
                ahead = 1 if following else 2
                for u in range(UN):
                    e = (g * NIT + it) * UN + u
                    k = (g * NIT + it) * (UN // 2) + u // 2
                    if not (last and u >= UN - ahead):
                        scores(g, it * UN + u + ahead, (u + ahead) % 2, (g * NIT + it) * (UN // 2) + (u + ahead) // 2)
                    if following:
                        if u == 0:
                            pe.wait_ge(s_z, 1 + ZSTEPS * g)
                        maxima(NIT * g + it, (g + 1) * GROUP + it, range(2 * u + (u > 0), min(2 * u + 3, 16)))
                    weigh(u % 2, u % PRS, k, last and u == UN - 1)
                    if last and not following and u < BESIDE:
                        rot_trans(u)
                        if u > 0:
                            rot_mul(u - 1)

            def close_sums(g):
                pe.wait_ge(s_zt, 1 + g + 1)
                if g is LAST_GROUP:
                    pe.wait_ge(s_rv, BESIDE - 2)
                for t in range(TT):
                    last = pe.transpose(psum[:, 7, t * P:(t + 1) * P], zt[:, t * P:(t + 1) * P], identf[:, :])
                last.then_inc(s_zp, 1)

            def group(g, following):
                open_sums(g)
                stay_warm(12, 0)
                pe.wait_ge(s_mq, g + 1)
                pe.wait_ge(s_mw, g + 1)
                scores(g, 0, 0, g * NIT * (UN // 2))
                if not following:
                    scores(g, 1, 1, g * NIT * (UN // 2))
                with pe.Fori(0, NIT - 1) as it:
                    body(g, it, False, following)
                body(g, NIT - 1, True, following)
                if following:
                    pe.wait_ge(s_mxh, 1 + NIT * (g + 1))
                    stay_warm(12, 0)
                close_sums(g)
                if following:
                    stay_warm(12, 0)
                    m_rows(g + 1)

            pe.wait_ge(s_v, NCTX // CHUNK)
            pe.wait_ge(s_ob, 1)
            pe.wait_ge(s_rh, 16 * GROUP)
            for pair in range(4):
                first_maxima(LAST_SUPER, pair)
                stay_warm(6, 0)
            pe.wait_ge(s_rg, 1 + 16 * GROUP * NSUPER)
            for pair in range(4, 8):
                first_maxima(LAST_SUPER, pair)
                stay_warm(6, 0)
            pe.wait_ge(s_ones, 32)
            keys_stacked(pe, NSUPER)
            pe.wait_ge(s_c, 7)
            stay_warm(20, 0)
            m_rows(0)
            with pe.Fori(0, NG - 1) as g:
                group(g, True)
            group(LAST_GROUP, False)

            for u in range(BESIDE, EARLY):
                rot_trans(u)
                if u == BESIDE:
                    pe.wait_ge(s_z, 1 + ZSTEPS * NG)
                rot_mul(u - 1)

            def product(bank, cols, left, right, ks, width=P):
                for k in ks:
                    last = pe.matmul(psum[0:width, bank, cols], left(k), right(k),
                                     start=(k == ks[0]), stop=(k == ks[-1]))
                return last

            ks = list(range(DT))
            half = [slice(0, NT), slice(NT, 2 * NT)]
            tile = [slice(t * P, (t + 1) * P) for t in range(4)]
            pe.wait_ge(s_ln, 6)
            transpose4(psum[:, 0], n2).then_inc(s_t2, 1)
            rot_mul(EARLY - 1)
            pe.wait_ge(s_t2c, 1)
            product(2, slice(0, NT), lambda k: aWl_s[:, k, :], lambda k: xT2[:, k], ks, LAT).then_inc(s_al, 1)
            for o in range(DT):
                last = product(1, half[o], lambda k: aWq_s[:, k, tile[o]], lambda k: xT2[:, k], ks)
            last.then_inc(s_aq, 1)
            pe.wait_ge(s_alc, 1)
            for o in range(DT):
                last = product(3, half[o], lambda k: aWk_s[:, tile[o]], lambda k: latT[:, :], [0])
            last.then_inc(s_ak, 1)
            for t in range(TT):
                last = product(2, half[t], lambda k: latT[:, tile[t]], lambda k: aWv_s[:, :], [0])
            last.then_inc(s_av, 1)
            rot_trans(EARLY)
            rot_trans(EARLY + 1)
            pe.wait_ge(s_akc, 2)

            def att_scores(n):
                h, t = 2 * (n // 2), n % 2
                pe.wait_ge(s_qm, h + 2)
                if n == 1:
                    pe.wait_ge(s_qf, 2)
                if n >= 2:
                    pe.wait_ge(s_ae, 2 * (n - 1))
                for j in range(2):
                    last = product(n % 2, half[j], lambda k: qm[:, h + j, tile[t]],
                                   lambda k: kT[:, (h + j) // (P // DH)], [0])
                last.then_inc(s_as, 1)

            def att_turn(n):
                pe.wait_ge(s_an, 2 * n + 2)
                if n == 0:
                    pe.wait_ge(s_avc, 2)
                if n >= 2:
                    pe.wait_ge(s_atV if n % 2 else s_atA, 2 * (n // 2))
                for j in range(2):
                    for k in range(TT):
                        last = pe.transpose(psum[:, 2 + n % 2, tile[2 * j + k]], pa[:, n % 2, j, tile[k]], identf[:, :])
                last.then_inc(s_at, 1)

            def att_weigh(g):
                steps = (g + 1) * GROUP
                pe.wait_ge(s_atA, steps)
                pe.wait_ge(s_atV, steps)
                if g > 0:
                    pe.wait_ge(s_azc, g)
                for k in range(TT):
                    for j in range(GROUP):
                        last = pe.matmul(psum[VW * j:VW * (j + 1), 4, 0:NT], vp[:, k, GROUP * g + j, :],
                                         pT[:, k, GROUP * g + j, :], start=(k == 0), stop=(k == TT - 1),
                                         tile_position=(0, VW * j))
                last.then_inc(s_az, 1)

            def att_out(g):
                pe.wait_ge(s_azc, g + 1)
                for t in range(TT):
                    last = pe.matmul(psum[:, 7 - t, 0:D], zT[:, g, tile[t]], woP[:, g], start=(g == 0),
                                     stop=(g == NG - 1))
                    if g == NG - 1:
                        last.then_inc(s_ao, 1)

            att_scores(0)
            att_scores(1)
            for n in range(STEPS):
                if n == 0:
                    rot_mul(EARLY)
                att_turn(n)
                if n + 2 < STEPS:
                    att_scores(n + 2)
                if n > 0:
                    for u in product_at(n, 0):
                        rot_mul(u)
                for u in product_at(n, 2):
                    rot_trans(u)
                if n % GROUP == 1 and n > 1:
                    att_weigh(n // GROUP - 1)
            pe.wait_ge(s_rv, RPROD - 2)
            for g in range(NG - 1):
                att_out(g)
            att_weigh(NG - 1)
            att_out(NG - 1)
            for u in (RPROD - 2, RPROD - 1):
                rot_trans(u)
                stay_warm(12, 1)
                rot_mul(u)
                stay_warm(20, 1)

            def hidden(r, s):
                pe.wait_ge(s_ew1[s], 16 * (r + 1))
                if s < 2:
                    pe.wait_ge(s_hc[s + 2], 1 + HT * r)
                else:
                    pe.wait_ge(s_hc[s - 2], HT * (r + 1))
                for t in range(HT):
                    last = product(4 + 2 * (s % 2) + t // 2, half[t % 2], lambda k: ew1r[:, s, k, tile[t]],
                                   lambda k: xgT[:, k], ks)
                last.then_inc(s_h[s], 1)

            def expert_out(r, s):
                pe.wait_ge(s_ew2[s], 16 * (r + 1))
                pe.wait_ge(s_hc[s], (s >= 2) + HT * (r + 1))
                pe.wait_ge(s_acc, 1 + (r * SLOTS + s) * TT)
                for t in range(TT):
                    last = product(2 + s % 2, half[t], lambda k: hT[:, s % 2, k, tile[t]],
                                   lambda k: ew2r[:, s, k], list(range(HT)))
                last.then_inc(s_eo[s], 1)

            pe.transpose(psum[:, 4, 0:E * HT], eb1_n[:, :], identf[0:E * HT, 0:E * HT]).then_inc(s_e1t, 1)
            pe.wait_ge(s_ln, 10)
            transpose4(psum[:, 0], xg).then_inc(s_t3, 1)
            stay_warm(10, 1)
            pe.wait_ge(s_t3c, 1)
            for t in range(TT):
                last = product(2, slice(t * E, (t + 1) * E), lambda k: xgT[:, k, tile[t]], lambda k: gw_s[:, k], ks)
            last.then_inc(s_lg, 1)
            for t in range(TT):
                last = product(1, half[t], lambda k: xgT[:, k, tile[t]], lambda k: abw_s[:, k], ks)
            last.then_inc(s_ab, 1)
            pe.wait_ge(s_e1c, 1)
            hidden(0, 0)
            pe.wait_ge(s_wd, 2)
            pe.wait_ge(s_rv, RPROD)
            for t in range(TT):
                last = pe.transpose(psum[0:E, 3, tile[t]], wd[:, t], identf[:, :])
            last.then_inc(s_wt8, 1)
            pe.wait_ge(s_wt8c, 1)
            for t in range(TT):
                last = product(0, half[t], lambda k: wdT[:, tile[t]], lambda k: eb2_s[:, :], [0])
            last.then_inc(s_b2, 1)
            pe.wait_ge(s_lm, 1)

            def experts(r, last):
                for s in range(SLOTS):
                    if not (last and s == SLOTS - 1):
                        hidden(r + (s + 1) // SLOTS, (s + 1) % SLOTS)
                    expert_out(r, s)

            def rotated(t):
                pe.wait_ge(s_mtc, t + 1)
                product(6 + t, half[0], lambda k: moeT[:, k, tile[t]], lambda k: rY[:, 0, k], ks).then_inc(s_rot, 1)

            with pe.Fori(0, E // SLOTS - 1) as r:
                experts(r, False)
            experts(E // SLOTS - 1, True)
            for t in range(TT):
                pe.wait_ge(s_acc, TT + 1 + (E - 1) * TT + t + 1)
                for k in range(DT):
                    last = pe.transpose(psum[:, 4 + t, k * P:(k + 1) * P],
                                        moe[:, t, k * P:(k + 1) * P], identf[:, :])
                last.then_inc(s_mt, 1)
                if t > 0:
                    rotated(t - 1)
            rotated(TT - 1)


ZSTEPS = 1 + 2 * TT
STEPS = 2 * H // 2
RPROD = NROT * (3 + SQUARINGS) + NROT - 1
BESIDE = 6
EARLY = 14
COMBINED_FIRST, COMBINED_NEXT = 8, 10
LAST_GROUP = NG - 1
NPRM = 21


def rot_of(u):
    return u % NROT if u < NROT * (3 + SQUARINGS) else 0


def rot_bank(u):
    return 6 + u % 2 if u < RPROD - 2 else 3


def right_of(u):
    return u % NROT if u < NROT * (3 + SQUARINGS) else u - NROT * (3 + SQUARINGS) + 1


def product_at(n, lead):
    u = EARLY + lead + n
    return [u] if u < RPROD - 2 else []


MAX_BANK = [v % 3 for v in range(15)] + [1]
MAX_USES = [MAX_BANK.count(b) for b in range(3)]


LAST_SUPER = NSUPER - 1
FIRST_USES = [8 * (NSUPER - 1) * (b > 0) + MAX_USES[b] for b in range(3)]
MX0 = [1 + n for n in FIRST_USES]


def first(c):
    return isinstance(c, int) and c == 0


def max_bank(v):
    b = MAX_BANK[v]
    return b, MAX_USES[b], MAX_BANK[:v].count(b)


_INS = ['x', 'ctx_1024', 'L0_xattn_Wq', 'L0_xattn_bq', 'L0_xattn_Wk', 'L0_xattn_bk', 'L0_xattn_Wv', 'L0_xattn_bv',
        'L0_xattn_gamma', 'L0_xattn_beta', 'L0_attn_Wq', 'L0_attn_bq', 'L0_attn_Wl', 'L0_attn_bl', 'L0_attn_Wk',
        'L0_attn_bk', 'L0_attn_Wv', 'L0_attn_bv', 'L0_attn_Wo', 'L0_attn_bo', 'L0_ffn_ln_gamma', 'L0_ffn_ln_beta',
        'L0_ffn_abel_w', 'L0_ffn_abel_b', 'L0_ffn_moe_gate_w', 'L0_ffn_moe_gate_b', 'L0_ffn_ew1', 'L0_ffn_eb1',
        'L0_ffn_ew2', 'L0_ffn_eb2', 'L0_ffn_gens', 'L0_ffn_gc_w', 'L0_ffn_gc_b']
_OUTS = [((1, NT, D), 'float32')]


def kernel(**inputs):
    import numpy as _np
    import concourse.bacc as _bacc
    from concourse import mybir as _mybir
    from concourse.bass_utils import run_bass_kernel_spmd as _run

    nc = _bacc.Bacc("TRN2", target_bir_lowering=False, num_devices=1, dynamic_dma_scratch_size=1024)
    arrays, args = {}, []
    for name in _INS:
        a = _np.ascontiguousarray(inputs[name])
        arrays[f"in_{name}_dram"] = a
        args.append(nc.dram_tensor(f"in_{name}_dram", a.shape, _mybir.dt.from_np(a.dtype), kind="ExternalInput").ap())
    for i, (shape, dtype) in enumerate(_OUTS):
        dt = _mybir.dt.from_np(_np.dtype(dtype))
        args.append(nc.dram_tensor(f"out_{i}_dram", shape, dt, kind="ExternalOutput").ap())
    build(nc, *args)
    r = _run(nc, [arrays], core_ids=[0])
    return r.results[0]["out_0_dram"]
```
